# Optimizing a Trainium2 kernel written in Bass

```python
import numpy as np
import jax
import jax.numpy as jnp

def _softmax(x, axis=-1):
    return jax.nn.softmax(x, axis=axis)

def _gelu(x):
    return jax.nn.gelu(x, approximate=True)

def _silu(x):
    return jax.nn.silu(x)

def _sigmoid(x):
    return jax.nn.sigmoid(x)

def _layernorm(x, axis=-1, eps=1e-05):
    m = jnp.mean(x, axis=axis, keepdims=True)
    v = jnp.var(x, axis=axis, keepdims=True)
    return (x - m) / jnp.sqrt(v + eps)

def _scatter_add(tgt, idx, src, axis=0):
    return tgt.at[idx].add(src)

def _segment_sum(src, seg, n):
    return jax.ops.segment_sum(src, seg, n)
kernel_name = 'mk_seq_postln_d1_jaxref_r4_db6922'

def setup_inputs(seed: int=0):
    np.random.seed(seed)
    _w = jnp.asarray

    def _L0_attn_setup():
        import jax, jax.numpy as jnp
        import numpy as np
        D_MODEL, N_HEADS = (256, 16)
        D_H = D_MODEL // N_HEADS
        D_HR = D_H // 2
        D_LATENT = 64
        THETA = 10000.0

        def rope(x, theta=THETA):
            S, d = (x.shape[-2], x.shape[-1])
            inv = theta ** (-jnp.arange(0, d, 2, dtype=jnp.float32) / d)
            ang = jnp.arange(S, dtype=jnp.float32)[:, None] * inv
            cos, sin = (jnp.cos(ang), jnp.sin(ang))
            x1, x2 = (x[..., 0::2], x[..., 1::2])
            r1 = x1 * cos - x2 * sin
            r2 = x1 * sin + x2 * cos
            return jnp.stack([r1, r2], axis=-1).reshape(x.shape)
        key = jax.random.key(seed)
        ks = jax.random.split(key, 9)
        s = lambda fan_in: 1.0 / np.sqrt(fan_in)
        return {'x': jax.random.normal(ks[0], (4, 512, D_MODEL), jnp.float32), 'W_DQ': jax.random.normal(ks[1], (D_MODEL, D_LATENT), jnp.float32) * s(D_MODEL), 'W_UQ': jax.random.normal(ks[2], (D_LATENT, N_HEADS * D_H), jnp.float32) * s(D_LATENT), 'W_QR': jax.random.normal(ks[3], (D_LATENT, N_HEADS * D_HR), jnp.float32) * s(D_LATENT), 'W_DKV': jax.random.normal(ks[4], (D_MODEL, D_LATENT), jnp.float32) * s(D_MODEL), 'W_UK': jax.random.normal(ks[5], (D_LATENT, N_HEADS * D_H), jnp.float32) * s(D_LATENT), 'W_UV': jax.random.normal(ks[6], (D_LATENT, N_HEADS * D_H), jnp.float32) * s(D_LATENT), 'W_KR': jax.random.normal(ks[7], (D_MODEL, D_HR), jnp.float32) * s(D_MODEL), 'W_O': jax.random.normal(ks[8], (N_HEADS * D_H, D_MODEL), jnp.float32) * s(N_HEADS * D_H)}
    _L0_attn_in = _L0_attn_setup()

    def _L0_ffn_setup():
        import jax, jax.numpy as jnp
        import numpy as np
        NUM_EXPERTS = 8
        TOP_K = 2
        key = jax.random.key(seed)
        ks = jax.random.split(key, 6)
        B, S, D, H, E = (4, 256, 256, 512, NUM_EXPERTS)
        x = jax.random.normal(ks[0], (B, S, D), dtype=jnp.float32)
        Wg = jax.random.normal(ks[1], (D, E), dtype=jnp.float32) * 0.02
        W1 = jax.random.normal(ks[2], (E, D, H), dtype=jnp.float32) * 0.02
        b1 = jax.random.normal(ks[3], (E, H), dtype=jnp.float32) * 0.02
        W2 = jax.random.normal(ks[4], (E, H, D), dtype=jnp.float32) * 0.02
        b2 = jax.random.normal(ks[5], (E, D), dtype=jnp.float32) * 0.02
        return {'x': x, 'Wg': Wg, 'W1': W1, 'b1': b1, 'W2': W2, 'b2': b2}
    _L0_ffn_in = _L0_ffn_setup()
    _d = {'L0_attn_x': _L0_attn_in['x'], 'L0_attn_W_DQ': _L0_attn_in['W_DQ'], 'L0_attn_W_UQ': _L0_attn_in['W_UQ'], 'L0_attn_W_QR': _L0_attn_in['W_QR'], 'L0_attn_W_DKV': _L0_attn_in['W_DKV'], 'L0_attn_W_UK': _L0_attn_in['W_UK'], 'L0_attn_W_UV': _L0_attn_in['W_UV'], 'L0_attn_W_KR': _L0_attn_in['W_KR'], 'L0_attn_W_O': _L0_attn_in['W_O'], 'L0_ffn_Wg': _L0_ffn_in['Wg'], 'L0_ffn_W1': _L0_ffn_in['W1'], 'L0_ffn_b1': _L0_ffn_in['b1'], 'L0_ffn_W2': _L0_ffn_in['W2'], 'L0_ffn_b2': _L0_ffn_in['b2']}
    _x0 = _d['L0_attn_x']
    _d['L0_attn_x'] = jax.random.normal(jax.random.fold_in(jax.random.key(seed), 1), (4, 1024, 256), dtype=_x0.dtype)
    del _x0
    return _d

def reference(L0_attn_x, L0_attn_W_DQ, L0_attn_W_UQ, L0_attn_W_QR, L0_attn_W_DKV, L0_attn_W_UK, L0_attn_W_UV, L0_attn_W_KR, L0_attn_W_O, L0_ffn_Wg, L0_ffn_W1, L0_ffn_b1, L0_ffn_W2, L0_ffn_b2):

    def _L0_attn_ref(x, W_DQ, W_UQ, W_QR, W_DKV, W_UK, W_UV, W_KR, W_O):
        import jax, jax.numpy as jnp
        import numpy as np
        D_MODEL, N_HEADS = (256, 16)
        D_H = D_MODEL // N_HEADS
        D_HR = D_H // 2
        D_LATENT = 64
        THETA = 10000.0

        def rope(x, theta=THETA):
            S, d = (x.shape[-2], x.shape[-1])
            inv = theta ** (-jnp.arange(0, d, 2, dtype=jnp.float32) / d)
            ang = jnp.arange(S, dtype=jnp.float32)[:, None] * inv
            cos, sin = (jnp.cos(ang), jnp.sin(ang))
            x1, x2 = (x[..., 0::2], x[..., 1::2])
            r1 = x1 * cos - x2 * sin
            r2 = x1 * sin + x2 * cos
            return jnp.stack([r1, r2], axis=-1).reshape(x.shape)
        B, S, _ = x.shape
        d_qk = D_H + D_HR
        c_q = x @ W_DQ
        Qc = (c_q @ W_UQ).reshape(B, S, N_HEADS, D_H).transpose(0, 2, 1, 3)
        Qr = (c_q @ W_QR).reshape(B, S, N_HEADS, D_HR).transpose(0, 2, 1, 3)
        Qr = rope(Qr)
        c_kv = x @ W_DKV
        Kc = (c_kv @ W_UK).reshape(B, S, N_HEADS, D_H).transpose(0, 2, 1, 3)
        Kr = rope((x @ W_KR)[:, None, :, :])
        Kr = jnp.broadcast_to(Kr, (B, N_HEADS, S, D_HR))
        V = (c_kv @ W_UV).reshape(B, S, N_HEADS, D_H).transpose(0, 2, 1, 3)
        Q = jnp.concatenate([Qc, Qr], axis=-1)
        K = jnp.concatenate([Kc, Kr], axis=-1)
        scores = jnp.einsum('bhqd,bhkd->bhqk', Q, K)
        scores = jnp.clip(scores, -80.0, 80.0)
        causal = jnp.tril(jnp.ones((S, S), dtype=bool))
        scores = jnp.where(causal, scores, -jnp.inf)
        weights = jax.nn.softmax(scores / jnp.sqrt(jnp.float32(d_qk)), axis=-1)
        attn = jnp.einsum('bhqk,bhkd->bhqd', weights, V)
        attn = attn.transpose(0, 2, 1, 3).reshape(B, S, N_HEADS * D_H)
        return attn @ W_O

    def _L0_ffn_ref(x, Wg, W1, b1, W2, b2):
        import jax, jax.numpy as jnp
        import numpy as np
        NUM_EXPERTS = 8
        TOP_K = 2
        B, S, D = x.shape
        E, _, H = W1.shape
        OUT = W2.shape[2]
        xm = x.reshape(-1, D)
        logits = xm @ Wg
        probs = jax.nn.softmax(logits, axis=-1)
        topk_p, topk_i = jax.lax.top_k(probs, TOP_K)
        flat_e = topk_i.reshape(-1)
        flat_p = topk_p.reshape(-1)
        order = jnp.argsort(flat_e)
        tok_idx = order // TOP_K
        e_sorted = flat_e[order]
        p_sorted = flat_p[order]
        xs = xm[tok_idx]
        y = jnp.zeros((xs.shape[0], OUT), dtype=xs.dtype)
        for e in range(E):
            h = jax.nn.relu(xs @ W1[e] + b1[e])
            ye = h @ W2[e] + b2[e]
            m = (e_sorted == e)[:, None].astype(xs.dtype)
            y = y + m * ye
        y = y * p_sorted[:, None]
        out = jnp.zeros((B * S, OUT), dtype=y.dtype).at[tok_idx].add(y)
        return out.reshape(B, S, OUT)
    x = L0_attn_x
    x = _layernorm(x + _L0_attn_ref(x, L0_attn_W_DQ, L0_attn_W_UQ, L0_attn_W_QR, L0_attn_W_DKV, L0_attn_W_UK, L0_attn_W_UV, L0_attn_W_KR, L0_attn_W_O), axis=-1)
    x = _layernorm(x + _L0_ffn_ref(x, L0_ffn_Wg, L0_ffn_W1, L0_ffn_b1, L0_ffn_W2, L0_ffn_b2), axis=-1)
    return x

_drawn_inputs = setup_inputs


def setup_inputs(seed=0):
    import zlib

    import numpy as np

    out = dict(_drawn_inputs(seed))
    spreads = {}
    factors = {'L0_ffn_b1': 37.544, 'L0_ffn_b2': 8.0}
    for name, (base, spread) in spreads.items():
        noise = np.random.default_rng([zlib.crc32(name.encode()), seed]).standard_normal(out[name].shape)
        drawn = base * np.exp(spread * noise) if base else spread * noise
        out[name] = jnp.asarray(drawn.astype(out[name].dtype))
    for name, factor in factors.items():
        out[name] = (out[name] * factor).astype(out[name].dtype)
    return out
```

```python
from contextlib import ExitStack

import concourse.bass as bass
import numpy as np
from concourse import mybir

ALU = mybir.AluOpType
ACT = mybir.ActivationFunctionType
AX = mybir.AxisListType
F32 = mybir.dt.float32
F32R = mybir.dt.float32r
I32 = mybir.dt.int32
U32 = mybir.dt.uint32

P = 128
B, S, D = 4, 1024, 256
HEADS, DH, DR, LAT = 16, 16, 8, 64
QUAD = 32
GROUPS = HEADS // 4
TILES = S // P
CHUNK = 512
CHUNKS = S // CHUNK
DT = D // P
CONSTS = 14
DVE_MAIN_STEPS, DVE_LATE_STEPS = 8, 46
ROUTE_AT, SCATTER_AT = 24 + 18, 2 * 24 + 14
WEIGHT_LOADS = 2 * 8 + 2
STACK_DMAS = 8
E, TOPK, HID = 8, 2, 512
FT = HID // P
EPS = 1e-5
SCALE = float(DH + DR) ** -0.5
CLIP = 80.0
EXP_LO = float(np.exp(-CLIP * SCALE))
EXP_HI = float(np.exp(CLIP * SCALE))
TOKENS = B * S
REGION = TOKENS + P
SPARE = E * REGION
MOE_TILES = (TOKENS * TOPK + E * (P - 1)) // P + 1
assert MOE_TILES % 2 == 0

UNITS = [(g, c, kt, hp) for g in range(GROUPS) for c in range(CHUNKS)
         for kt in range(4 * c + 4) for hp in range(2)]
NU = len(UNITS)
PER_G = NU // GROUPS
C0 = 8
LAG = 4
S_SLOTS, P_SLOTS = 3, 6


def offset_in_chunk(c, kt):
    return max(0, kt - 4 * c) * P


def is_diag(u):
    _, c, kt, _ = UNITS[u]
    return kt >= 4 * c


MASKS_BEFORE = [sum(is_diag(v) for v in range(u)) for u in range(NU + 1)]
N_MASK = MASKS_BEFORE[NU]

MISC = {}
for _g in range(GROUPS):
    for _i, _n in ((1, 0), (3, 1), (6, 2), (8, 3)):
        MISC[_g * PER_G + _i] = ("proj", _n)
    MISC[_g * PER_G + 4] = ("ot", (2 * _g + 7) % 8)
    MISC[_g * PER_G + 14] = ("ot", 2 * _g)
for _n, _i in enumerate((9, 11, 16, 20)):
    MISC[_i] = ("at", _n)
for _n, _i in enumerate((10, 13, 18, 22)):
    MISC[_i] = ("wo", _n)
for _n, (_i, _j) in enumerate(((9, 10), (11, 12), (13, 15), (16, 17))):
    MISC[PER_G + _i] = ("x1t", _n)
    MISC[PER_G + _j] = ("lg", _n)
for _n in range(4):
    MISC[PER_G + 18 + _n] = ("x_t", _n)
MISC[2 * PER_G + 10] = ("rk", 0)
for _n in range(2):
    MISC[2 * PER_G + 16 + _n] = ("c_t", _n)
for _n in range(4):
    MISC[2 * PER_G + 19 + _n] = ("kr", _n)
for _n in range(4):
    MISC[3 * PER_G + 9 + _n] = ("v", _n)
ACT_TAKES = ("x_t", "c_t", "v", "at", "x1t")
LATE = ("at", "wo", "x1t", "lg", "rk")
NEXT = ("x_t", "c_t", "kr", "v")
JOBS = {"proj": 16, "ot": 8, "at": 4, "wo": 4, "x1t": 4, "lg": 4, "rk": 1, "x_t": 4, "c_t": 2,
        "kr": 4, "v": 4}


class Tally:

    def __init__(self):
        self.n, self.reg, self.start, self.per, self.at = 0, None, 0, 0, 0

    def value(self):
        return self.n if self.reg is None else (self.reg - self.start) * self.per + self.n

    def next(self):
        self.n += 1
        return self.value()

    def enter(self, reg, start, per):
        self.reg, self.start, self.per, self.at = reg, start, per, self.n

    def leave(self, iterations):
        assert self.n - self.at == self.per, f"{self.n - self.at} steps in the loop"
        self.n, self.reg = self.at + iterations * self.per, None


def layer(nc, x, w_dq, w_uq, w_qr, w_dkv, w_uk, w_uv, w_kr, w_o, wg, w1, b1, w2, b2,
          c_ident, c_sel, c_rope, c_tri, c_iota, out, dbg=None):
    ctx = ExitStack()
    with ctx:
        def sem(name):
            return ctx.enter_context(nc.semaphore(name))

        psum_scope = ExitStack()

        def psum(name, shape, where=None):
            return (where or psum_scope).enter_context(nc.psum_tensor(name, shape, F32))

        x1_d = dbg[0] if dbg else nc.dram_tensor("x1_scratch", (TOKENS, D), F32).ap()
        xs_d = dbg[1] if dbg else nc.dram_tensor("expert_in_scratch", (SPARE + P, D), F32).ap()
        ys_d = nc.dram_tensor("expert_out_scratch", (MOE_TILES * P, D), F32).ap()

        keep = ctx

        def sb(name, shape, dt=F32, where=None):
            return (where or keep).enter_context(nc.sbuf_tensor(name, shape, dt))

        ident = sb("ident", [P, P])
        iota = sb("iota", [P, MOE_TILES + 1])
        lane = iota[:, MOE_TILES:MOE_TILES + 1]
        load = sb("load", [P, TILES + 1, E])
        pos_all = sb("pos_all", [P, B, TOPK, TILES])
        exp_all = sb("exp_all", [P, B, TOPK, TILES])
        gate_all = sb("gate_all", [P, B, TOPK, TILES])
        row_all = sb("row_all", [P, B, TOPK * TILES], U32)

        s_const = sem("constants_loaded")
        s_xin = [sem(f"x_loaded{i}") for i in range(2)]
        s_stack = [sem(f"stack_loaded{i}") for i in range(2)]
        s_z = sem("z_loaded")
        s_x1st = sem("x1_stored")
        s_scat = sem("x1_scattered")
        s_zero = sem("weights_zeroed")
        s_pool0 = sem("constants_set")
        s_setup = sem("weights_padded")
        s_qk = sem("scores_ready")
        s_exp = sem("exp_ready")
        s_clip = sem("clip_ready")
        s_mask = sem("mask_ready")
        s_pv = sem("pv_done")
        s_acc = sem("acc_evacuated")
        ready = {k: sem(f"{k}_in_psum") for k in JOBS}
        taken = {k: sem(f"{k}_taken") for k in JOBS}
        s_hi, s_lo = sem("high_parts_ready"), sem("low_parts_ready")
        s_rstd = sem("rstd_ready")
        s_vcopy = sem("v_in_place")
        s_x1 = sem("x1_ready")
        s_stat = sem("ln_stats_ready")
        s_hot = sem("onehot_ready")
        s_dexp = sem("router_exp_in")
        s_eexp = sem("router_exp_out")
        s_posr = sem("pos_ready")
        c_main, c_late, c_pool = sem("dve_chain"), sem("dve_chain_late"), sem("pool_chain")

        attn_scope = ExitStack()
        A = attn_scope
        wdown = sb("wdown", [P, DT, P], where=A)
        wup = sb("wup", [P, GROUPS, 4, QUAD], where=A)
        wkr = sb("wkr", [P, DT, P], where=A)
        wuv = sb("wuv", [P, D], where=A)
        wo = sb("wo", [P, DT, D], where=A)
        wgate = sb("wgate", [P, DT, E], where=A)
        sel = sb("sel", [P, P], where=A)
        tri = sb("tri", [P, 2, P], where=A)
        rope = sb("rope", [P, S], where=A)
        x_in = sb("x_in", [P, 2, 2, D], where=A)
        x_t = sb("x_t", [P, DT, S], where=A)
        c_t = sb("c_t", [P, S], where=A)
        kr_part = sb("kr_part", [P, CHUNK], where=A)
        kr = sb("kr", [P, S], where=A)
        full = sb("full", [P, 2, CHUNK], where=A)
        home = sb("home", [P, 4, S], F32R, where=A)
        stacks = sb("stacks", [P, 2, 4, 2, S], F32R, where=A)
        v_new = sb("v_new", [P, TILES, D], where=A)
        v_aug = sb("v_aug", [P, TILES, HEADS, DH + 1], where=A)
        p_sb = sb("p_sb", [P, P_SLOTS, 2, CHUNK], where=A)
        o_t = sb("o_t", [P, 2, CHUNK], where=A)
        recip = sb("recip", [P, 4, 4], where=A)
        attn = sb("attn", [P, TILES, D], where=A)
        attn_t = sb("attn_t", [P, 2, DT, 2 * P], where=A)
        z = sb("z", [P, TILES, D], where=A)
        x1_t = sb("x1_t", [P, 2, DT, 2 * P], where=A)
        stats = sb("stats", [P, TILES, 6], where=A)
        mv = sb("mv", [P, TILES, 2], where=A)
        rstd = sb("rstd", [P, TILES, 1], where=A)
        expo = sb("expo", [P, TILES, 1], where=A)
        lg = sb("lg", [P, TILES, E], where=A)
        top = sb("top", [P, TILES, E], where=A)
        topi = sb("topi", [P, TILES, E], U32, where=A)
        topf = sb("topf", [P, TILES, E], where=A)
        dlt = sb("dlt", [P, TILES, E], where=A)
        ex = sb("ex", [P, TILES, E], where=A)
        den = sb("den", [P, TILES, 1], where=A)
        hot = sb("hot", [P, TOPK, TILES, E], where=A)
        hots = sb("hots", [P, TILES, E], where=A)
        rk = sb("rk", [P, 2, TILES, E], where=A)
        where_ = sb("where_", [P, TILES, E], where=A)
        tmp = sb("tmp", [P, TOPK, TILES, E], where=A)
        pos = sb("pos", [P, TOPK * TILES], U32, where=A)
        region0 = sb("region0", [P, E], where=A)

        scores = psum("scores", [P, S_SLOTS, 2, CHUNK])
        acc = psum("acc", [P, CHUNK])
        misc = psum("misc", [P, CHUNK])

        x_tiles = x.rearrange("b (n t p) d -> (b n) p t d", t=2, p=P)
        x_batch = x.rearrange("b (t p) d -> b p t d", p=P)
        x1_batch = x1_d.rearrange("(b t p) d -> b p t d", b=B, p=P)

        with nc.Block() as block:
            @block.sync
            def _(sp):
                n = 0

                def const(dst, src):
                    nonlocal n
                    sp.dma_start(dst, src).then_inc(s_const, 16)
                    n += 1

                for m in range(2):
                    sp.dma_start(x_in[:, m], x_tiles[m]).then_inc(s_xin[m], 16)
                const(ident[:], c_ident)
                const(wdown[:, :, 0:LAT], w_dq.rearrange("(t p) n -> p t n", p=P))
                const(wdown[:, :, LAT:P], w_dkv.rearrange("(t p) n -> p t n", p=P))
                const(sel[:], c_sel)
                const(rope[:], c_rope)
                sp.wait_ge(s_zero, 2)
                const(wup[0:LAT, :, :, 0:DH].rearrange("p g j d -> p (g j) d"),
                      w_uq.rearrange("k (h d) -> k h d", d=DH))
                const(wup[0:LAT, :, :, DH:DH + DR].rearrange("p g j d -> p (g j) d"),
                      w_qr.rearrange("k (h d) -> k h d", d=DR))
                const(wup[LAT:P, :, :, 0:DH].rearrange("p g j d -> p (g j) d"),
                      w_uk.rearrange("k (h d) -> k h d", d=DH))
                const(wkr[:, :, DH:DH + DR], w_kr.rearrange("(t p) n -> p t n", p=P))
                const(wuv[LAT:P, :], w_uv)
                const(wo[:], w_o.rearrange("(t p) n -> p t n", p=P))
                const(wgate[:], wg.rearrange("(t p) n -> p t n", p=P))
                const(tri[:], c_tri.rearrange("a p n -> p a n"))
                const(iota[:], c_iota)
                assert n == CONSTS

                def x_in_load(b, m):
                    sp.wait_ge(ready["x_t"], b * 4 + m - 1)
                    sp.nop(nofuse=True)
                    sp.dma_start(x_in[:, m % 2], x_tiles[b * 4 + m]).then_inc(s_xin[m % 2], 16)

                def stack(b, g):
                    sp.wait_ge(s_lo, (b * GROUPS + g + 1) * 4)
                    sp.nop(nofuse=True)
                    if not (isinstance(b, int) and b * GROUPS + g < 2):
                        sp.wait_ge(s_qk, (b * GROUPS + g - 1) * PER_G)
                    for j in range(4):
                        for r in range(4):
                            q_part, k_part = r // 2, 2 + r % 2
                            sp.dma_start(stacks[QUAD * r:QUAD * (r + 1), g % 2, j].bitcast(F32),
                                         home[QUAD * j:QUAD * (j + 1), q_part:k_part + 1:k_part - q_part, :].bitcast(F32)
                                         ).then_inc(s_stack[j // 2], 16)

                def body(b, late, nxt):
                    if late:
                        if not (isinstance(b, int) and b < 2):
                            sp.wait_ge(s_x1st, 16 * (b - 1))
                            sp.nop(nofuse=True)
                            sp.wait_ge(s_scat, 256 * (b - 1))
                        sp.nop(nofuse=True)
                        sp.dma_start(z[:], x_batch[b - 1]).then_inc(s_z, 16)
                    stack(b, 1)
                    if nxt:
                        x_in_load(b + 1, 0)
                        x_in_load(b + 1, 1)
                    if late:
                        sp.wait_ge(s_x1, 8 * b)
                        sp.nop(nofuse=True)
                        sp.dma_start(x1_batch[b - 1], z[:]).then_inc(s_x1st, 16)
                    stack(b, 2)
                    if nxt:
                        x_in_load(b + 1, 2)
                        x_in_load(b + 1, 3)
                    stack(b, 3)
                    if nxt:
                        stack(b + 1, 0)

                x_in_load(0, 2)
                x_in_load(0, 3)
                stack(0, 0)
                body(0, False, True)
                with sp.Fori(1, B - 1) as b:
                    body(b, True, True)
                body(B - 1, True, False)
                sp.wait_ge(s_x1st, 16 * (B - 1))
                sp.wait_ge(s_scat, 256 * (B - 1))
                sp.dma_start(z[:], x_batch[B - 1]).then_inc(s_z, 16)
                sp.wait_ge(s_x1, 8 * B)
                sp.dma_start(x1_batch[B - 1], z[:]).then_inc(s_x1st, 16)
                sp.wait_ge(s_x1st, 16 * B)
                sp.wait_ge(s_scat, 256 * B)

            @block.tensor
            def _(pe):
                last = [None, None]

                def bank(kind, count):
                    if last[0] is not None:
                        pe.wait_ge(last[0], last[1])
                    last[0], last[1] = taken[kind], count

                def job(kind, n, b):
                    count = b * JOBS[kind] + n + 1
                    bank(kind, count)
                    if kind == "x_t":
                        pe.wait_ge(s_xin[n % 2], (b * 2 + n // 2 + 1) * 16)
                        for dt in range(DT):
                            for t in range(2):
                                mm = nc.tensor.transpose(misc[:, (dt * 2 + t) * P:(dt * 2 + t + 1) * P],
                                                         x_in[:, n % 2, t, dt * P:(dt + 1) * P], ident[:])
                    elif kind == "c_t":
                        pe.wait_ge(taken["x_t"], b * 4 + 2 * n + 2)
                        for dt in range(DT):
                            mm = nc.tensor.matmul(misc[:], wdown[:, dt, :], x_t[:, dt, n * CHUNK:(n + 1) * CHUNK],
                                                  start=dt == 0, stop=dt == DT - 1)
                    elif kind == "kr" and n % 2 == 0:
                        pe.wait_ge(taken["x_t"], b * 4 + n + 2)
                        c = n // 2
                        for dt in range(DT):
                            mm = nc.tensor.matmul(misc[:], wkr[:, dt, :], x_t[:, dt, c * CHUNK:(c + 1) * CHUNK],
                                                  start=dt == 0, stop=dt == DT - 1)
                    elif kind == "kr":
                        mm = nc.tensor.matmul(misc[:], sel[:], kr_part[:], start=True, stop=True)
                    elif kind == "v":
                        pe.wait_ge(taken["c_t"], b * 2 + n // 2 + 1)
                        for t in range(2):
                            kt = 2 * n + t
                            mm = nc.tensor.matmul(misc[:, t * D:(t + 1) * D], c_t[LAT:P, kt * P:(kt + 1) * P],
                                                  wuv[LAT:P, :], start=True, stop=True)
                    elif kind == "proj":
                        g, c, is_k = n // 4, (n % 4) // 2, n % 2
                        pe.wait_ge(taken["c_t"], b * 2 + c + 1)
                        rows = slice(LAT, P) if is_k else slice(0, LAT)
                        mm = nc.tensor.matmul(misc[:], wup[rows, g].rearrange("p j d -> p (j d)"),
                                              c_t[rows, c * CHUNK:(c + 1) * CHUNK], start=True, stop=True)
                    elif kind == "ot":
                        pe.wait_ge(s_acc, b * 8 + n + 1)
                        for i in range(4):
                            mm = nc.tensor.transpose(misc[:, i * P:(i + 1) * P],
                                                     o_t[:, n % 2, i * P:(i + 1) * P], ident[:])
                    elif kind == "at":
                        pe.wait_ge(taken["ot"], b * 8 + (7 if n < 2 else 8))
                        for dt in range(DT):
                            for t in range(2):
                                mm = nc.tensor.transpose(misc[:, (dt * 2 + t) * P:(dt * 2 + t + 1) * P],
                                                         attn[:, 2 * n + t, dt * P:(dt + 1) * P], ident[:])
                    elif kind == "wo":
                        pe.wait_ge(taken["at"], b * 4 + n + 1)
                        for t in range(2):
                            for dt in range(DT):
                                mm = nc.tensor.matmul(misc[:, t * D:(t + 1) * D],
                                                      attn_t[:, n % 2, dt, t * P:(t + 1) * P], wo[:, dt, :],
                                                      start=dt == 0, stop=dt == DT - 1)
                    elif kind == "x1t":
                        pe.wait_ge(s_x1, b * 8 + 2 * n + 2)
                        for dt in range(DT):
                            for t in range(2):
                                mm = nc.tensor.transpose(misc[:, (dt * 2 + t) * P:(dt * 2 + t + 1) * P],
                                                         z[:, 2 * n + t, dt * P:(dt + 1) * P], ident[:])
                    elif kind == "lg":
                        pe.wait_ge(taken["x1t"], b * 4 + n + 1)
                        for t in range(2):
                            for dt in range(DT):
                                mm = nc.tensor.matmul(misc[:, t * E:(t + 1) * E],
                                                      x1_t[:, n % 2, dt, t * P:(t + 1) * P], wgate[:, dt, :],
                                                      start=dt == 0, stop=dt == DT - 1)
                    elif kind == "rk":
                        pe.wait_ge(s_hot, b + 1)
                        for a in range(2):
                            mm = nc.tensor.matmul(misc[:, a * TILES * E:(a + 1) * TILES * E], tri[:, a, :],
                                                  hots[:].rearrange("p t e -> p (t e)"), start=True, stop=True)
                    mm.then_inc(ready[kind], 1)

                def qk(b, u):
                    g, c, kt, hp = UNITS[u]
                    o = offset_in_chunk(c, kt)
                    if u % PER_G < 2:
                        pe.wait_ge(s_stack[hp], (b * GROUPS + g + 1) * STACK_DMAS * 16)
                    if not (isinstance(b, int) and b == 0 and u < S_SLOTS):
                        pe.wait_ge(s_exp, b * NU + u - S_SLOTS + 1)
                    for a in range(2):
                        j = 2 * hp + a
                        mm = nc.tensor.matmul(scores[:, u % S_SLOTS, a, o:CHUNK],
                                              stacks[:, g % 2, j, 1, kt * P:(kt + 1) * P],
                                              stacks[:, g % 2, j, 0, c * CHUNK + o:(c + 1) * CHUNK],
                                              start=True, stop=True)
                    mm.then_inc(s_qk, 1)

                def pv(b, u):
                    g, c, kt, hp = UNITS[u]
                    o = offset_in_chunk(c, kt)
                    if u == 0:
                        pe.wait_ge(s_vcopy, b + 1)
                    if kt == 0 and not (isinstance(b, int) and b == 0 and u == 0):
                        pe.wait_ge(s_acc, b * 8 + 2 * g + c)
                    if is_diag(u):
                        pe.wait_ge(s_mask, b * N_MASK + MASKS_BEFORE[u] + 2)
                    else:
                        pe.wait_ge(s_clip, b * NU + u + 2)
                    for j in range(4):
                        mm = nc.tensor.matmul(acc[QUAD * j:QUAD * j + DH + 1, o:CHUNK],
                                              v_aug[:, kt, 4 * g + j, :],
                                              p_sb[:, (u + j // 2) % P_SLOTS, j % 2, o:CHUNK],
                                              start=kt == 0, stop=kt == 4 * c + 3)
                    mm.then_inc(s_pv, 1)

                def body(b, late, nxt):
                    for u in range(NU):
                        qk(b, u)
                        if u in MISC:
                            kind, n = MISC[u]
                            if kind == "proj":
                                if u < 3 * PER_G:
                                    job("proj", (u // PER_G + 1) * 4 + n, b)
                                elif nxt:
                                    job("proj", n, b + 1)
                            elif kind == "ot" and n == 7:
                                if late:
                                    job("ot", 7, b - 1)
                            elif kind in LATE:
                                if late:
                                    job(kind, n, b - 1)
                            elif kind in NEXT:
                                if nxt:
                                    job(kind, n, b + 1)
                            else:
                                job("ot", n, b)
                        if u % 2 == 0 and u >= LAG:
                            pv(b, u - LAG)
                        elif u % 2 == 0 and late:
                            pv(b - 1, NU - LAG + u)

                pe.wait_ge(s_const, 16 * CONSTS)
                pe.wait_ge(s_setup, 5)
                for kind in ("x_t", "c_t", "kr"):
                    for n in range(JOBS[kind]):
                        job(kind, n, 0)
                for n in range(4):
                    job("proj", n, 0)
                for n in range(4):
                    job("v", n, 0)
                body(0, False, True)
                with pe.Fori(1, B - 1) as b:
                    last[0], last[1] = taken["ot"], b * 8 - 1
                    body(b, True, True)
                last[0], last[1] = taken["ot"], (B - 1) * 8 - 1
                body(B - 1, True, False)
                for u in range(NU - LAG, NU, 2):
                    pv(B - 1, u)
                job("ot", 7, B - 1)
                for n in range(4):
                    job("at", n, B - 1)
                    job("wo", n, B - 1)
                for n in range(4):
                    job("x1t", n, B - 1)
                    job("lg", n, B - 1)
                job("rk", 0, B - 1)

            @block.scalar
            def _(act):
                def exp(b, u):
                    _, c, kt, _ = UNITS[u]
                    o = offset_in_chunk(c, kt)
                    act.wait_ge(s_qk, b * NU + u + 1)
                    if not (isinstance(b, int) and b == 0 and u < P_SLOTS):
                        act.wait_ge(s_pv, b * (NU // 2) + (u - P_SLOTS) // 2 + 1)
                    nc.scalar.activation(p_sb[:, u % P_SLOTS, :, o:CHUNK], scores[:, u % S_SLOTS, :, o:CHUNK],
                                         ACT.Exp, scale=SCALE).then_inc(s_exp, 1)

                def evac(kind, n, b):
                    act.wait_ge(ready[kind], b * JOBS[kind] + n + 1)
                    m2 = misc[:].rearrange("p (a n) -> p a n", a=2)
                    if kind == "x_t":
                        if not (isinstance(b, int) and b == 0):
                            act.wait_ge(ready["kr"], b * 4)
                        to = x_t[:, :, n * 2 * P:(n + 1) * 2 * P]
                    elif kind == "c_t":
                        if not (isinstance(b, int) and b == 0):
                            act.wait_ge(ready["proj"], b * 16)
                            act.wait_ge(ready["v"], b * 4)
                        to, m2 = c_t[:, n * CHUNK:(n + 1) * CHUNK], misc[:]
                    elif kind == "v":
                        if not (isinstance(b, int) and b == 0):
                            act.wait_ge(s_vcopy, b)
                        to = v_new[:, 2 * n:2 * n + 2, :]
                    elif kind == "at":
                        if n >= 2:
                            act.wait_ge(ready["wo"], b * 4 + n - 1)
                        else:
                            act.wait_ge(ready["ot"], b * 8 + 7)
                        to = attn_t[:, n % 2, :, :]
                    elif kind == "x1t":
                        if n >= 2:
                            act.wait_ge(ready["lg"], b * 4 + n - 1)
                        to = x1_t[:, n % 2, :, :]
                    nc.scalar.copy(to, m2).then_inc(taken[kind], 1)

                def router_exp(b):
                    act.wait_ge(s_dexp, b + 1)
                    nc.scalar.activation(ex[:].rearrange("p t e -> p (t e)"),
                                         dlt[:].rearrange("p t e -> p (t e)"), ACT.Exp).then_inc(s_eexp, 1)

                def body(b, late, nxt):
                    for u in range(NU):
                        if u in MISC and MISC[u][0] in ACT_TAKES:
                            kind, n = MISC[u]
                            if kind in LATE and late:
                                evac(kind, n, b - 1)
                            if kind in NEXT and nxt:
                                evac(kind, n, b + 1)
                        if u == ROUTE_AT + 4 and late:
                            router_exp(b - 1)
                        exp(b, u)

                for kind in ("x_t", "c_t", "v"):
                    for n in range(JOBS[kind]):
                        evac(kind, n, 0)
                body(0, False, True)
                with act.Fori(1, B - 1) as b:
                    body(b, True, True)
                body(B - 1, True, False)
                for kind in ("at", "x1t"):
                    for n in range(4):
                        evac(kind, n, B - 1)
                router_exp(B - 1)

            @block.vector
            def _(dve):
                main, late_t = Tally(), Tally()

                def evac(kind, n, b):
                    dve.wait_ge(ready[kind], b * JOBS[kind] + n + 1)
                    m2 = misc[:].rearrange("p (a n) -> p a n", a=2)
                    if kind == "kr" and n % 2 == 0:
                        c = n // 2
                        nc.vector.tensor_tensor(kr_part[:], misc[:], rope[:, c * CHUNK:(c + 1) * CHUNK],
                                                ALU.mult).then_inc(taken[kind], 1)
                    elif kind == "kr":
                        c = n // 2
                        nc.vector.tensor_copy(kr[:, c * CHUNK:(c + 1) * CHUNK], misc[:]).then_inc(taken[kind], 1)
                    elif kind == "proj":
                        g, c, is_k = n // 4, (n % 4) // 2, n % 2
                        if not (isinstance(b, int) and b == 0 and n < 2):
                            dve.wait_ge(s_lo, b * 16 + n - 1)
                        cs = slice(c * CHUNK, (c + 1) * CHUNK)
                        if is_k:
                            dve.wait_ge(taken["kr"], b * 4 + 2 * c + 2)
                            nc.vector.tensor_tensor(full[:, 1, :], misc[:], kr[:, cs], ALU.add).then_inc(taken[kind], 1)
                        else:
                            nc.vector.tensor_tensor(full[:, 0, :], misc[:], rope[:, cs], ALU.mult).then_inc(taken[kind], 1)
                        if n % 4 == 0 and not (isinstance(b, int) and b * 4 + g == 0):
                            for i in range(2):
                                dve.wait_ge(s_stack[i], (b * GROUPS + g) * STACK_DMAS * 16)
                        dve.wait_ge(taken[kind], b * 16 + n + 1)
                        nc.vector.tensor_copy(home[:, 2 * is_k, cs], full[:, is_k, :]).then_inc(s_hi, 1)
                    elif kind == "ot":
                        g, c = n // 2, n % 2
                        m4 = misc[:].rearrange("p (i j r) -> p i j r", i=4, j=4)
                        if not (isinstance(b, int) and b == 0):
                            dve.wait_ge(ready["at"], (b - 1) * 4 + 2 * c + 2)
                        nc.vector.reciprocal(recip[:], m4[:, :, :, DH]).then_inc(c_main, 1)
                        dve.wait_ge(c_main, main.next())
                        nc.vector.tensor_tensor(
                            attn[:, 4 * c:4 * c + 4, g * 4 * DH:(g + 1) * 4 * DH].rearrange("p i (j d) -> p i j d", j=4),
                            m4[:, :, :, 0:DH], recip[:].unsqueeze(3).to_broadcast([P, 4, 4, DH]), ALU.mult
                        ).then_inc(taken[kind], 1)
                    elif kind == "wo":
                        dve.wait_ge(s_z, (b + 1) * 16)
                        zz = z[:, 2 * n:2 * n + 2, :]
                        nc.vector.tensor_tensor(zz, m2, zz, ALU.add).then_inc(taken[kind], 1)
                        dve.wait_ge(taken[kind], b * 4 + n + 1)
                        for t in range(2 * n, 2 * n + 2):
                            nc.vector.bn_stats(stats[:, t, :], z[:, t, :]).then_inc(c_late, 1)
                            v = late_t.next()
                        dve.wait_ge(c_late, v)
                        dve.nop(nofuse=True)
                        for t in range(2 * n, 2 * n + 2):
                            nc.vector.bn_aggr(mv[:, t, :], stats[:, t, :]).then_inc(s_stat, 1)
                    elif kind == "lg":
                        nc.vector.tensor_copy(lg[:, 2 * n:2 * n + 2, :],
                                              misc[:, 0:2 * E].rearrange("p (t e) -> p t e", t=2)
                                              ).then_inc(taken[kind], 1)
                    elif kind == "rk":
                        nc.vector.tensor_copy(rk[:], misc[:, 0:2 * TILES * E].rearrange(
                            "p (a t e) -> p a t e", a=2, t=TILES)).then_inc(taken[kind], 1)

                def step(ins):
                    ins.then_inc(c_late, 1)
                    dve.wait_ge(c_late, late_t.next())

                def top_two(b):
                    dve.wait_ge(taken["lg"], (b + 1) * 4)
                    if not (isinstance(b, int) and b == 0):
                        dve.wait_ge(s_eexp, b)
                        dve.wait_ge(ready["rk"], b)
                    dve.nop(nofuse=True)
                    for t in range(TILES):
                        nc.vector.max(top[:, t, :], lg[:, t, :]).then_inc(c_late, 1)
                        v = late_t.next()
                    dve.wait_ge(c_late, v)
                    dve.nop(nofuse=True)
                    for t in range(TILES):
                        nc.vector.max_index(topi[:, t, :], top[:, t, :], lg[:, t, :]).then_inc(c_late, 1)
                        v = late_t.next()
                    nc.vector.tensor_tensor(dlt[:], top[:], top[:, :, 0:1].to_broadcast([P, TILES, E]),
                                            ALU.subtract).then_inc(s_dexp, 1)
                    dve.wait_ge(c_late, v)
                    step(nc.vector.tensor_copy(topf[:, :, 0:TOPK], topi[:, :, 0:TOPK]))
                    dve.nop(nofuse=True)
                    nc.vector.tensor_copy(exp_all[:, b].rearrange("p k t -> p t k"),
                                          topf[:, :, 0:TOPK]).then_inc(c_late, 1)
                    late_t.next()
                    for k in range(TOPK):
                        nc.vector.tensor_tensor(hot[:, k], iota[:, 0:E].unsqueeze(1).to_broadcast([P, TILES, E]),
                                                topf[:, :, k:k + 1].to_broadcast([P, TILES, E]),
                                                ALU.is_equal).then_inc(c_late, 1)
                        v = late_t.next()
                    dve.wait_ge(c_late, v)
                    nc.vector.tensor_tensor(hots[:], hot[:, 0], hot[:, 1], ALU.add).then_inc(s_hot, 1)

                def gates_of(b):
                    dve.wait_ge(s_eexp, b + 1)
                    step(nc.vector.tensor_reduce(den[:].rearrange("p t o -> p (t o)"), ex[:], AX.X, ALU.add))
                    step(nc.vector.reciprocal(den[:], den[:]))
                    step(nc.vector.tensor_tensor(gate_all[:, b].rearrange("p k t -> p t k"), ex[:, :, 0:TOPK],
                                                 den[:].to_broadcast([P, TILES, TOPK]), ALU.mult))

                def positions(b):
                    dve.wait_ge(taken["rk"], b + 1)
                    for t in range(TILES):
                        step(nc.vector.tensor_tensor(load[:, t + 1, :], load[:, t, :], rk[:, 1, t, :], ALU.add))
                    step(nc.vector.tensor_tensor(where_[:], rk[:, 0], load[:, 0:TILES, :], ALU.add))
                    step(nc.vector.tensor_tensor(where_[:], where_[:],
                                                 region0[:].unsqueeze(1).to_broadcast([P, TILES, E]), ALU.add))
                    for k in range(TOPK):
                        step(nc.vector.tensor_tensor(tmp[:, k], where_[:], hot[:, k], ALU.mult))
                        step(nc.vector.tensor_reduce(pos_all[:, b, k, :], tmp[:, k], AX.X, ALU.add))
                    if not (isinstance(b, int) and b == 0):
                        dve.wait_ge(s_scat, b * 256)
                    dve.nop(nofuse=True)
                    nc.vector.tensor_copy(pos[:], pos_all[:, b].rearrange("p k t -> p (k t)")).then_inc(s_posr, 1)
                    step(nc.vector.tensor_copy(load[:, 0, :], load[:, TILES, :]))

                def norm(b, t):
                    if t == 0:
                        dve.wait_ge(s_rstd, b + 1)
                    nc.vector.tensor_scalar(z[:, t, :], z[:, t, :], mv[:, t, 0:1], rstd[:, t, :],
                                            ALU.subtract, ALU.mult).then_inc(s_x1, 1)

                def clip(b, u):
                    _, c, kt, _ = UNITS[u]
                    o = offset_in_chunk(c, kt)
                    dve.wait_ge(s_exp, b * NU + u + 1)
                    pp = p_sb[:, u % P_SLOTS, :, o:CHUNK]
                    nc.vector.tensor_scalar(pp, pp, EXP_LO, EXP_HI, ALU.max, ALU.min).then_inc(s_clip, 1)

                def acc_out(b, n):
                    units = PER_G * (n // 2) + (C0 if n % 2 == 0 else PER_G)
                    dve.wait_ge(s_pv, (b * NU + units) // 2 if isinstance(b, int) else b * (NU // 2) + units // 2)
                    if not (isinstance(b, int) and b == 0 and n < 2):
                        dve.wait_ge(ready["ot"], b * 8 + n - 1)
                    nc.vector.tensor_copy(o_t[:, n % 2, :], acc[:]).then_inc(s_acc, 1)

                def v_place(b):
                    if not (isinstance(b, int) and b == 0):
                        dve.wait_ge(s_pv, b * (NU // 2))
                    dve.wait_ge(taken["v"], (b + 1) * 4)
                    nc.vector.tensor_copy(v_aug[:, :, :, 0:DH],
                                          v_new[:].rearrange("p t (h d) -> p t h d", h=HEADS)).then_inc(s_vcopy, 1)

                def body(b, late, nxt):
                    for u in range(NU):
                        if u in MISC:
                            kind, n = MISC[u]
                            if kind == "proj":
                                if u < 3 * PER_G:
                                    evac("proj", (u // PER_G + 1) * 4 + n, b)
                                elif nxt:
                                    evac("proj", n, b + 1)
                            elif kind == "ot" and n == 7:
                                if late:
                                    evac("ot", 7, b - 1)
                            elif kind in ACT_TAKES:
                                pass
                            elif kind in LATE:
                                if late:
                                    evac(kind, n, b - 1)
                            elif kind in NEXT:
                                if nxt:
                                    evac(kind, n, b + 1)
                            else:
                                evac("ot", n, b)
                        if late and PER_G <= u < PER_G + TILES:
                            norm(b - 1, u - PER_G)
                        if late and u == ROUTE_AT:
                            top_two(b - 1)
                        if late and u == ROUTE_AT + 8:
                            gates_of(b - 1)
                        if late and u == 2 * PER_G + 11:
                            positions(b - 1)
                        clip(b, u)
                        if u % PER_G == C0 - 2 + LAG:
                            acc_out(b, 2 * (u // PER_G))
                        if u % PER_G == LAG - 2:
                            if u >= PER_G:
                                acc_out(b, 2 * (u // PER_G) - 1)
                            elif late:
                                acc_out(b - 1, 7)
                        if u == LAG - 2:
                            v_place(b)

                dve.wait_ge(s_pool0, 3)
                dve.wait_ge(s_const, 16 * CONSTS)
                for to, of in ((0, 1), (1, 0)):
                    nc.vector.tensor_copy(wup[0:LAT, :, :, DH + DR + to:QUAD:2],
                                          wup[0:LAT, :, :, DH + of:DH + DR:2]).then_inc(s_setup, 1)
                    nc.vector.tensor_copy(wkr[:, :, DH + DR + to:QUAD:2],
                                          wkr[:, :, DH + of:DH + DR:2]).then_inc(s_setup, 1)
                nc.vector.tensor_scalar(region0[:], iota[:, 0:E], float(REGION), None, ALU.mult).then_inc(c_main, 1)
                dve.wait_ge(c_main, main.next())
                nc.vector.memset(acc[:], 0.0).then_inc(s_setup, 1)
                for n in range(4):
                    evac("kr", n, 0)
                for n in range(4):
                    evac("proj", n, 0)
                body(0, False, True)
                with dve.Fori(1, B - 1) as b:
                    main.enter(b, 1, DVE_MAIN_STEPS)
                    late_t.enter(b, 1, DVE_LATE_STEPS)
                    body(b, True, True)
                main.leave(B - 2)
                late_t.leave(B - 2)
                body(B - 1, True, False)
                acc_out(B - 1, 7)
                evac("ot", 7, B - 1)
                for n in range(4):
                    evac("wo", n, B - 1)
                for t in range(TILES):
                    norm(B - 1, t)
                for n in range(4):
                    evac("lg", n, B - 1)
                top_two(B - 1)
                gates_of(B - 1)
                evac("rk", 0, B - 1)
                positions(B - 1)

            @block.gpsimd
            def _(pool):
                chain = Tally()

                def low_part(b, n):
                    c, is_k = (n % 4) // 2, n % 2
                    cs = slice(c * CHUNK, (c + 1) * CHUNK)
                    pool.wait_ge(s_hi, b * 16 + n + 1)
                    nc.gpsimd.tensor_tensor(home[:, 2 * is_k + 1, cs], full[:, is_k, :],
                                            home[:, 2 * is_k, cs].bitcast(F32), ALU.subtract).then_inc(s_lo, 1)

                def mask(b, u):
                    _, c, kt, _ = UNITS[u]
                    o = offset_in_chunk(c, kt)
                    pool.wait_ge(s_clip, b * NU + u + 1)
                    pool.nop(nofuse=True)
                    pp = p_sb[:, u % P_SLOTS, :, o:o + P]
                    nc.gpsimd.affine_select(out=pp, in_=pp, compare_op=ALU.is_ge, fill=0.0, base=0,
                                            pattern=[[0, 2], [1, P]], channel_multiplier=-1).then_inc(s_mask, 1)

                def rstd_of(b):
                    pool.wait_ge(s_stat, (b + 1) * 8)
                    pool.nop(nofuse=True)
                    nc.gpsimd.tensor_scalar(rstd[:], mv[:, :, 1:2], EPS, None, ALU.add).then_inc(c_pool, 1)
                    pool.wait_ge(c_pool, chain.next())
                    nc.gpsimd.tensor_tensor(rstd[:], rstd[:], expo[:], ALU.pow).then_inc(s_rstd, 1)

                def scatter(b, n):
                    k, t = n % 2, n // 2
                    if n == 0:
                        pool.wait_ge(s_posr, b + 1)
                        pool.wait_ge(s_x1, (b + 1) * 8)
                        pool.nop(nofuse=True)
                    nc.gpsimd.indirect_dma_start(
                        out=xs_d, out_offset=bass.IndirectOffsetOnAxis(ap=pos[:, k * TILES + t:k * TILES + t + 1], axis=0),
                        in_=z[:, t, :], in_offset=None).then_inc(s_scat, 16)

                def body(b, late, nxt):
                    for u in range(NU):
                        if u in MISC and MISC[u][0] == "proj":
                            n = MISC[u][1]
                            if u < 3 * PER_G:
                                low_part(b, (u // PER_G + 1) * 4 + n)
                            elif nxt:
                                low_part(b + 1, n)
                        if late and u == PER_G:
                            rstd_of(b - 1)
                        if late and SCATTER_AT <= u < SCATTER_AT + 2 * TILES:
                            scatter(b - 1, u - SCATTER_AT)
                        if is_diag(u):
                            mask(b, u)

                nc.gpsimd.memset(wup[:], 0.0).then_inc(s_zero, 1)
                nc.gpsimd.memset(wkr[:], 0.0).then_inc(s_zero, 1)
                nc.gpsimd.memset(v_aug[:], 1.0).then_inc(s_pool0, 1)
                nc.gpsimd.memset(expo[:], -0.5).then_inc(s_pool0, 1)
                nc.gpsimd.memset(load[:], 0.0).then_inc(s_pool0, 1)
                for n in range(4):
                    low_part(0, n)
                body(0, False, True)
                with pool.Fori(1, B - 1) as b:
                    chain.enter(b, 1, 1)
                    body(b, True, True)
                chain.leave(B - 2)
                body(B - 1, True, False)
                rstd_of(B - 1)
                for n in range(2 * TILES):
                    scatter(B - 1, n)

        psum_scope.close()
        attn_scope.close()

        tables_ready, tails_zero = sem("tile_tables_ready"), sem("region_tails_zeroed")
        s_w = sem("expert_weights_loaded")
        s_xs = [sem(f"rows_loaded{i}") for i in range(2)]
        s_xsT_ps, s_xsT = sem("rows_t_in_psum"), sem("rows_t_ready")
        s_h_ps, s_h = sem("hidden_in_psum"), sem("hidden_ready")
        s_hT_ps, s_hT = sem("hidden_t_in_psum"), sem("hidden_t_ready")
        s_y_ps, s_y = sem("expert_out_in_psum"), sem("expert_out_ready")
        s_yst = [sem(f"expert_out_stored{i}") for i in range(2)]
        s_zero_rows = sem("zero_rows_ready")
        s_spare = sem("spare_rows_zeroed")
        c_tab = sem("table_chain")
        moe_scope = ExitStack()
        M = moe_scope
        w1_sb = sb("w1_sb", [P, E, DT, HID], where=M)
        w2_sb = sb("w2_sb", [P, E, FT, D], where=M)
        b1_sb = sb("b1_sb", [P, E, HID], where=M)
        b2_sb = sb("b2_sb", [P, E, D], where=M)
        zero_rows = sb("zero_rows", [P, D], where=M)
        counts = sb("counts", [P, E], where=M)
        thr = sb("thr", [P, TOKENS // P], where=M)
        over = sb("over", [P, E, TOKENS // P], where=M)
        n_tiles = sb("n_tiles", [P, E], where=M)
        ends = sb("ends", [P, E], where=M)
        row_shift = sb("row_shift", [P, E], where=M)
        cmp = sb("cmp", [P, MOE_TILES, E], where=M)
        tile_e = sb("tile_e", [P, MOE_TILES], where=M)
        tile_u = sb("tile_u", [P, MOE_TILES], where=M)
        tile_r = sb("tile_r", [P, MOE_TILES], where=M)
        t128 = sb("t128", [P, MOE_TILES], where=M)
        table = sb("table", [P, 2, MOE_TILES], I32, where=M)
        pick = sb("pick", [P, B * TOPK * TILES, E], where=M)
        shift = sb("shift", [P, B * TOPK * TILES], where=M)
        tailf = sb("tailf", [P, E], where=M)
        tail = sb("tail", [P, E], U32, where=M)
        xs = sb("xs", [P, 2, D], where=M)
        xs_t = sb("xs_t", [P, 2, DT, P], where=M)
        h = sb("h", [P, 2, HID], where=M)
        h_t = sb("h_t", [P, 2, FT, P], where=M)
        y = sb("y", [P, 2, D], where=M)
        ps_x = [psum(f"ps_x{i}", [P, CHUNK], M) for i in range(2)]
        ps_h = [psum(f"ps_h{i}", [P, CHUNK], M) for i in range(2)]
        ps_t = [psum(f"ps_t{i}", [P, CHUNK], M) for i in range(2)]
        ps_y = [psum(f"ps_y{i}", [P, CHUNK], M) for i in range(2)]
        LOOP_END = MOE_TILES - 2
        ys_tiles = ys_d.rearrange("(n p) d -> n p d", p=P)
        EXPERT, READ = range(2)

        with nc.Block() as block:
            @block.sync
            def _(sp):
                for e in range(E):
                    sp.dma_start(w1_sb[:, e], w1[e].rearrange("(t p) n -> p t n", p=P)).then_inc(s_w, 16)
                    sp.dma_start(w2_sb[:, e], w2[e].rearrange("(t p) n -> p t n", p=P)).then_inc(s_w, 16)
                sp.dma_start(b1_sb[:], b1.partition_broadcast(P)).then_inc(s_w, 16)
                sp.dma_start(b2_sb[:], b2.partition_broadcast(P)).then_inc(s_w, 16)
                sp.wait_ge(s_zero_rows, 1)
                sp.dma_start(xs_d[SPARE:SPARE + P, :], zero_rows[:]).then_inc(s_spare, 16)
                sp.wait_ge(s_spare, 16)
                sp.wait_ge(tables_ready, 1)
                sp.wait_ge(tails_zero, 16 * E)

                def load_rows(n, slot, first=False):
                    row = sp.value_load(table[0:1, READ, bass.ds(n, 1)], min_val=0, max_val=SPARE)
                    if not first:
                        sp.wait_ge(s_xsT_ps, n - 1)
                    sp.nop(nofuse=True)
                    sp.dma_start(xs[:, slot, :], xs_d[bass.ds(row, P), :]).then_inc(s_xs[slot], 16)

                load_rows(0, 0, True)
                load_rows(1, 1, True)
                with sp.Fori(1, MOE_TILES // 2) as pair:
                    load_rows(2 * pair, 0)
                    load_rows(2 * pair + 1, 1)

            @block.tensor
            def _(pe):
                def rows_t(n, slot, first=False):
                    pe.wait_ge(s_xs[slot], 16 * (n // 2 + 1) if isinstance(n, int) else (n - slot) * 8 + 16)
                    if not first:
                        pe.wait_ge(s_xsT, n - 1)
                    for dt in range(DT):
                        mm = nc.tensor.transpose(ps_x[slot][:, dt * P:(dt + 1) * P],
                                                 xs[:, slot, dt * P:(dt + 1) * P], ident[:])
                    mm.then_inc(s_xsT_ps, 1)

                def up(n, slot, first=False):
                    e = pe.value_load(table[0:1, EXPERT, bass.ds(n, 1)], min_val=0, max_val=E - 1)
                    pe.wait_ge(s_xsT, n + 1)
                    if not first:
                        pe.wait_ge(s_h, n - 1)
                    for dt in range(DT):
                        mm = nc.tensor.matmul(ps_h[slot][:, :], xs_t[:, slot, dt, :], w1_sb[:, e, dt, :],
                                              start=dt == 0, stop=dt == DT - 1)
                    mm.then_inc(s_h_ps, 1)

                def hidden_t(n, slot, first=False):
                    pe.wait_ge(s_h, n + 1)
                    if not first:
                        pe.wait_ge(s_hT, n - 1)
                    for f in range(FT):
                        mm = nc.tensor.transpose(ps_t[slot][:, f * P:(f + 1) * P],
                                                 h[:, slot, f * P:(f + 1) * P], ident[:])
                    mm.then_inc(s_hT_ps, 1)

                def down(n, slot, first=False):
                    e = pe.value_load(table[0:1, EXPERT, bass.ds(n, 1)], min_val=0, max_val=E - 1)
                    pe.wait_ge(s_hT, n + 1)
                    if not first:
                        pe.wait_ge(s_y, n - 1)
                    for f in range(FT):
                        mm = nc.tensor.matmul(ps_y[slot][:, 0:D], h_t[:, slot, f, :], w2_sb[:, e, f, :],
                                              start=f == 0, stop=f == FT - 1)
                    mm.then_inc(s_y_ps, 1)

                pe.wait_ge(tables_ready, 1)
                rows_t(0, 0, True)
                pe.wait_ge(s_w, 16 * WEIGHT_LOADS)

                def turn(n, slot):
                    static = isinstance(n, int)
                    if not static or n < MOE_TILES:
                        up(n, slot, static and n < 2)
                    if not static or 1 <= n <= MOE_TILES:
                        hidden_t(n - 1, 1 - slot, static and n < 3)
                    if not static or n + 1 < MOE_TILES:
                        rows_t(n + 1, 1 - slot, static and n < 1)
                    if not static or n >= 2:
                        down(n - 2, slot, static and n < 4)

                for n in range(4):
                    turn(n, n % 2)
                with pe.Fori(2, LOOP_END // 2) as pair:
                    for k in range(2):
                        turn(2 * pair + k, k)
                for n in range(LOOP_END, MOE_TILES + 2):
                    turn(n, n % 2)

            @block.scalar
            def _(act):
                def rows_out(n, slot, first=False):
                    act.wait_ge(s_xsT_ps, n + 1)
                    if not first:
                        act.wait_ge(s_h_ps, n - 1)
                    nc.scalar.copy(xs_t[:, slot].rearrange("p t n -> p (t n)"), ps_x[slot][:, 0:D]).then_inc(s_xsT, 1)

                def relu_out(n, slot, first=False):
                    act.wait_ge(s_hT_ps, n + 1)
                    if not first:
                        act.wait_ge(s_y_ps, n - 1)
                    nc.scalar.activation(h_t[:, slot].rearrange("p t n -> p (t n)"), ps_t[slot][:, :],
                                         ACT.Relu).then_inc(s_hT, 1)

                rows_out(0, 0, True)
                rows_out(1, 1, True)
                relu_out(0, 0, True)
                rows_out(2, 0)
                relu_out(1, 1, True)
                rows_out(3, 1)
                with act.Fori(1, LOOP_END // 2) as pair:
                    for k in range(2):
                        n = 2 * pair
                        relu_out(n + k, k)
                        rows_out(n + k + 2, k)
                for n in range(MOE_TILES - 2, MOE_TILES):
                    relu_out(n, n % 2)

            @block.vector
            def _(dve):
                steps = Tally()

                def step(ins):
                    ins.then_inc(c_tab, 1)
                    dve.wait_ge(c_tab, steps.next())

                nc.vector.memset(zero_rows[:], 0.0).then_inc(s_zero_rows, 1)
                NT = MOE_TILES
                step(nc.vector.tensor_copy(counts[:], load[:, 0, :]))
                step(nc.vector.tensor_scalar(row_shift[:], iota[:, 0:E], float(REGION), None, ALU.mult))
                step(nc.vector.tensor_tensor(tailf[:], counts[:], row_shift[:], ALU.add))
                step(nc.vector.tensor_scalar(tailf[:], tailf[:], lane, None, ALU.add))
                nc.vector.tensor_copy(tail[:], tailf[:]).then_inc(s_zero_rows, 1)
                step(nc.vector.tensor_scalar(thr[:], iota[:, 0:TOKENS // P], float(P), None, ALU.mult))
                sh = [P, E, TOKENS // P]
                step(nc.vector.tensor_tensor(over[:], counts[:].unsqueeze(2).to_broadcast(sh),
                                             thr[:].unsqueeze(1).to_broadcast(sh), ALU.is_gt))
                step(nc.vector.tensor_reduce(n_tiles[:], over[:], AX.X, ALU.add))
                step(nc.vector.tensor_copy(ends[:], n_tiles[:]))
                for e in range(1, E):
                    step(nc.vector.tensor_tensor(ends[:, e:e + 1], ends[:, e:e + 1], ends[:, e - 1:e], ALU.add))
                sh = [P, NT, E]
                ends_b = ends[:].unsqueeze(1).to_broadcast(sh)
                step(nc.vector.tensor_tensor(cmp[:], iota[:, 0:NT].unsqueeze(2).to_broadcast(sh), ends_b, ALU.is_ge))
                step(nc.vector.tensor_reduce(tile_e[:], cmp[:], AX.X, ALU.add))
                step(nc.vector.tensor_tensor(ends[:], ends[:], n_tiles[:], ALU.subtract))
                step(nc.vector.tensor_scalar(ends[:], ends[:], float(P), None, ALU.mult))
                step(nc.vector.tensor_tensor(row_shift[:], row_shift[:], ends[:], ALU.subtract))
                step(nc.vector.tensor_tensor(cmp[:], iota[:, 0:E].unsqueeze(1).to_broadcast(sh),
                                             tile_e[:].unsqueeze(2).to_broadcast(sh), ALU.is_equal))
                step(nc.vector.tensor_tensor(cmp[:], cmp[:], row_shift[:].unsqueeze(1).to_broadcast(sh), ALU.mult))
                step(nc.vector.tensor_reduce(tile_r[:], cmp[:], AX.X, ALU.add))
                step(nc.vector.tensor_scalar(t128[:], iota[:, 0:NT], float(P), None, ALU.mult))
                step(nc.vector.tensor_tensor(tile_r[:], tile_r[:], t128[:], ALU.add))
                step(nc.vector.tensor_scalar(tile_u[:], tile_e[:], float(E), None, ALU.is_ge))
                step(nc.vector.tensor_scalar(table[:, EXPERT, :], tile_e[:], float(E - 1), None, ALU.min))
                step(nc.vector.scalar_tensor_tensor(tile_r[:], tile_u[:], float(SPARE), tile_r[:], ALU.mult, ALU.add))
                step(nc.vector.tensor_tensor(t128[:], t128[:], tile_u[:], ALU.mult))
                nc.vector.tensor_tensor(table[:, READ, :], tile_r[:], t128[:], ALU.subtract).then_inc(tables_ready, 1)
                sh = [P, B * TOPK * TILES, E]
                step(nc.vector.tensor_tensor(pick[:], iota[:, 0:E].unsqueeze(1).to_broadcast(sh),
                                             exp_all[:].rearrange("p b k t -> p (b k t)").unsqueeze(2).to_broadcast(sh),
                                             ALU.is_equal))
                step(nc.vector.tensor_tensor(pick[:], pick[:], row_shift[:].unsqueeze(1).to_broadcast(sh), ALU.mult))
                step(nc.vector.tensor_reduce(shift[:], pick[:], AX.X, ALU.add))
                step(nc.vector.tensor_tensor(row_all[:].rearrange("p b n -> p (b n)"),
                                             pos_all[:].rearrange("p b k t -> p (b k t)"), shift[:], ALU.subtract))

                def hidden(n, slot, first=False):
                    e = dve.value_load(table[0:1, EXPERT, bass.ds(n, 1)], min_val=0, max_val=E - 1)
                    dve.wait_ge(s_h_ps, n + 1)
                    if not first:
                        dve.wait_ge(s_hT_ps, n - 1)
                    nc.vector.tensor_tensor(h[:, slot, :], ps_h[slot][:, :], b1_sb[:, e, :], ALU.add).then_inc(s_h, 1)

                def expert_out(n, slot, first=False):
                    e = dve.value_load(table[0:1, EXPERT, bass.ds(n, 1)], min_val=0, max_val=E - 1)
                    dve.wait_ge(s_y_ps, n + 1)
                    if not first:
                        dve.wait_ge(s_yst[slot], (n - slot) * 8)
                    nc.vector.tensor_tensor(y[:, slot, :], ps_y[slot][:, 0:D], b2_sb[:, e, :], ALU.add).then_inc(s_y, 1)

                dve.wait_ge(tables_ready, 1)
                dve.wait_ge(s_w, 16 * WEIGHT_LOADS)
                hidden(0, 0, True)
                hidden(1, 1, True)
                hidden(2, 0)
                expert_out(0, 0, True)
                hidden(3, 1)
                expert_out(1, 1, True)
                with dve.Fori(2, MOE_TILES // 2) as pair:
                    for k in range(2):
                        n = 2 * pair
                        hidden(n + k, k)
                        expert_out(n + k - 2, k)
                for n in range(MOE_TILES - 2, MOE_TILES):
                    expert_out(n, n % 2)

            @block.gpsimd
            def _(pool):
                pool.wait_ge(s_zero_rows, 2)
                for e in range(E):
                    nc.gpsimd.indirect_dma_start(
                        out=xs_d, out_offset=bass.IndirectOffsetOnAxis(ap=tail[:, e:e + 1], axis=0),
                        in_=zero_rows[:], in_offset=None).then_inc(tails_zero, 16)

                def store_rows(n, slot):
                    pool.wait_ge(s_y, n + 1)
                    pool.dma_start(ys_tiles[n], y[:, slot, :]).then_inc(s_yst[slot], 16)

                with pool.Fori(0, MOE_TILES // 2) as pair:
                    store_rows(2 * pair, 0)
                    store_rows(2 * pair + 1, 1)
                for slot in range(2):
                    pool.wait_ge(s_yst[slot], 8 * MOE_TILES)

        moe_scope.close()

        s_x1l = sem("residual_loaded")
        s_cur = sem("batch_tables_ready")
        s_curd = sem("batch_gates_ready")
        s_gath = [sem(f"rows_gathered{i}") for i in range(2)]
        s_zz = sem("sums_ready")
        s_st = sem("final_stats_ready")
        s_rs = sem("final_rstd_ready")
        s_o = sem("out_ready")
        s_ost = sem("out_stored")
        c_fin, c_fp = sem("final_chain"), sem("final_pool_chain")
        F = ExitStack()
        pos_cur = sb("pos_cur", [P, TOPK * TILES], U32, where=F)
        gate_cur = sb("gate_cur", [P, TOPK, TILES], where=F)
        res = sb("res", [P, TILES, D], where=F)
        rows = sb("rows", [P, TILES, TOPK, D], where=F)
        sums = sb("sums", [P, TILES, D], where=F)
        fst = sb("fst", [P, TILES, 6], where=F)
        fmv = sb("fmv", [P, TILES, 2], where=F)
        frs = sb("frs", [P, TILES, 1], where=F)
        fexpo = sb("fexpo", [P, TILES, 1], where=F)
        HALF = TILES // 2
        out_batch = out.rearrange("b (t p) d -> b p t d", p=P)
        FIN_STEPS = TILES * 2

        with nc.Block() as block:
            @block.sync
            def _(sp):
                def store(b, hf):
                    ts = slice(hf * HALF, (hf + 1) * HALF)
                    sp.wait_ge(s_o, b * TILES + (hf + 1) * HALF)
                    sp.dma_start(out_batch[b, :, ts, :], sums[:, ts, :]).then_inc(s_ost, 16)

                with sp.Fori(0, B) as b:
                    sp.wait_ge(s_zz, b * TILES)
                    sp.dma_start(res[:], x1_batch[b]).then_inc(s_x1l, 16)
                    store(b, 0)
                    store(b, 1)
                sp.wait_ge(s_ost, B * 2 * 16)

            @block.gpsimd
            def _(pool):
                nc.gpsimd.memset(fexpo[:], -0.5).then_inc(c_fp, 1)
                pool.wait_ge(c_fp, 1)
                chain = Tally()
                chain.next()
                with pool.Fori(0, B) as b:
                    chain.enter(b, 0, 2)
                    for i in range(2):
                        pool.wait_ge(s_gath[i], b * TILES * 16)
                    nc.gpsimd.tensor_copy(pos_cur[:], row_all[:, b, :]).then_inc(s_cur, 1)
                    pool.wait_ge(s_cur, b + 1)
                    pool.wait_ge(s_zz, b * TILES)
                    pool.nop(nofuse=True)
                    for t in range(TILES):
                        for k in range(TOPK):
                            nc.gpsimd.indirect_dma_start(
                                out=rows[:, t, k, :], out_offset=None, in_=ys_d,
                                in_offset=bass.IndirectOffsetOnAxis(ap=pos_cur[:, k * TILES + t:k * TILES + t + 1], axis=0)
                            ).then_inc(s_gath[t // HALF], 16)
                    for hf in range(2):
                        ts = slice(hf * HALF, (hf + 1) * HALF)
                        pool.wait_ge(s_st, b * TILES + (hf + 1) * HALF)
                        pool.nop(nofuse=True)
                        nc.gpsimd.tensor_scalar(frs[:, ts], fmv[:, ts, 1:2], EPS, None, ALU.add).then_inc(c_fp, 1)
                        pool.wait_ge(c_fp, chain.next())
                        pool.nop(nofuse=True)
                        nc.gpsimd.tensor_tensor(frs[:, ts], frs[:, ts], fexpo[:, ts], ALU.pow).then_inc(s_rs, 1)
                chain.leave(B)

            @block.vector
            def _(dve):
                steps = Tally()
                with dve.Fori(0, B) as b:
                    steps.enter(b, 0, FIN_STEPS)
                    nc.vector.tensor_copy(gate_cur[:].rearrange("p k t -> p (k t)"),
                                          gate_all[:, b].rearrange("p k t -> p (k t)")).then_inc(s_curd, 1)
                    dve.wait_ge(s_curd, b + 1)
                    dve.wait_ge(s_x1l, (b + 1) * 16)
                    dve.wait_ge(s_ost, b * 32)
                    for t in range(TILES):
                        if t % HALF == 0:
                            dve.wait_ge(s_gath[t // HALF], (b + 1) * TILES * 16)
                        nc.vector.scalar_tensor_tensor(sums[:, t, :], rows[:, t, 0, :], gate_cur[:, 0, t:t + 1],
                                                       res[:, t, :], ALU.mult, ALU.add).then_inc(c_fin, 1)
                        dve.wait_ge(c_fin, steps.next())
                        nc.vector.scalar_tensor_tensor(sums[:, t, :], rows[:, t, 1, :], gate_cur[:, 1, t:t + 1],
                                                       sums[:, t, :], ALU.mult, ALU.add).then_inc(s_zz, 1)
                        dve.wait_ge(s_zz, b * TILES + t + 1)
                        nc.vector.bn_stats(fst[:, t, :], sums[:, t, :]).then_inc(c_fin, 1)
                        dve.wait_ge(c_fin, steps.next())
                        dve.nop(nofuse=True)
                        nc.vector.bn_aggr(fmv[:, t, :], fst[:, t, :]).then_inc(s_st, 1)
                    for t in range(TILES):
                        if t % HALF == 0:
                            dve.wait_ge(s_rs, b * 2 + t // HALF + 1)
                        nc.vector.tensor_scalar(sums[:, t, :], sums[:, t, :], fmv[:, t, 0:1], frs[:, t, :],
                                                ALU.subtract, ALU.mult).then_inc(s_o, 1)
                steps.leave(B)

        F.close()


def constants():
    ident = np.eye(P, dtype=np.float32)
    sel = np.zeros((P, P), np.float32)
    for d in range(DR):
        for j in range(4):
            for half in range(2):
                to = QUAD * j + DH + DR * half + d
                sel[DH + d, to] = sel[DH + DR + d, to] = 1.0
    inv = np.float32(10000.0) ** (-np.arange(0, DR, 2, dtype=np.float32) / np.float32(DR))
    ang = np.arange(S, dtype=np.float32)[:, None] * inv.astype(np.float32)
    cos, sin = np.cos(ang).T, np.sin(ang).T
    rope = np.ones((P, S), np.float32)
    for j in range(4):
        for d in range(DR):
            rope[QUAD * j + DH + d] = cos[d // 2]
            rope[QUAD * j + DH + DR + d] = sin[d // 2] if d % 2 else -sin[d // 2]
    tri = np.stack([np.triu(np.ones((P, P), np.float32), 1), np.ones((P, P), np.float32)])
    iota = np.zeros((P, MOE_TILES + 1), np.float32)
    iota[:, 0:MOE_TILES] = np.arange(MOE_TILES)
    iota[:, MOE_TILES] = np.arange(P)
    return {"ident": ident, "sel": sel, "rope": rope, "tri": tri, "iota": iota}


_INS = ["L0_attn_x", "L0_attn_W_DQ", "L0_attn_W_UQ", "L0_attn_W_QR", "L0_attn_W_DKV", "L0_attn_W_UK",
        "L0_attn_W_UV", "L0_attn_W_KR", "L0_attn_W_O", "L0_ffn_Wg", "L0_ffn_W1", "L0_ffn_b1",
        "L0_ffn_W2", "L0_ffn_b2"]


def kernel(**inputs):
    import concourse.bacc as _bacc
    from concourse.bass_utils import run_bass_kernel_spmd as _run

    nc = _bacc.Bacc("TRN2", target_bir_lowering=False, num_devices=1)
    arrays, args = {}, []
    given = {name: np.ascontiguousarray(inputs[name]) for name in _INS} | constants()
    for name, a in given.items():
        arrays[f"in_{name}_dram"] = a
        args.append(nc.dram_tensor(f"in_{name}_dram", a.shape, mybir.dt.from_np(a.dtype), kind="ExternalInput").ap())
    out = nc.dram_tensor("out_0_dram", (B, S, D), F32, kind="ExternalOutput").ap()
    layer(nc, *args, out)
    r = _run(nc, [arrays], core_ids=[0])
    return r.results[0]["out_0_dram"]
```

```python
from contextlib import ExitStack

import concourse.bass as bass
import numpy as np
from concourse import mybir

ALU = mybir.AluOpType
ACT = mybir.ActivationFunctionType
AX = mybir.AxisListType
F32 = mybir.dt.float32
F32R = mybir.dt.float32r
I32 = mybir.dt.int32
U32 = mybir.dt.uint32

P = 128
B, S, D = 4, 1024, 256
HEADS, DH, DR, LAT = 16, 16, 8, 64
QUAD = 32
GROUPS = HEADS // 4
TILES = S // P
CHUNK = 512
CHUNKS = S // CHUNK
DT = D // P
CONSTS = 14
DVE_MAIN_STEPS, DVE_LATE_STEPS = 8, 48
WEIGHT_LOADS = 2 * 8 + 2
STACK_DMAS = 8
E, TOPK, HID = 8, 2, 512
FT = HID // P
EPS = 1e-5
SCALE = float(DH + DR) ** -0.5
CLIP = 80.0
EXP_LO = float(np.exp(-CLIP * SCALE))
EXP_HI = float(np.exp(CLIP * SCALE))
TOKENS = B * S
REGION = TOKENS + P
SPARE = E * REGION
MOE_TILES = (TOKENS * TOPK + E * (P - 1)) // P + 1
assert MOE_TILES % 2 == 0
ROW = D + 2
DUMMY = 2 * P

UNITS = [(g, c, kt, hp) for g in range(GROUPS) for c in range(CHUNKS)
         for kt in range(4 * c + 4) for hp in range(2)]
NU = len(UNITS)
PER_G = NU // GROUPS
C0 = 8
LAG = 6
S_SLOTS, P_SLOTS = 3, LAG + 2
POOL_BEHIND = 1


def offset_in_chunk(c, kt):
    return max(0, kt - 4 * c) * P


def is_diag(u):
    _, c, kt, _ = UNITS[u]
    return kt >= 4 * c


def behind(b, u, k, before):
    if u >= k:
        return b, u - k
    return (b - 1, NU + u - k) if before else None


MASKS_BEFORE = [sum(is_diag(v) for v in range(u)) for u in range(NU + 1)]
N_MASK = MASKS_BEFORE[NU]

MISC = {}


def place(kind, group, positions, first=0):
    for n, i in enumerate(positions):
        assert group * PER_G + i not in MISC
        MISC[group * PER_G + i] = (kind, n + first)


PLAN = dict(proj=[1, 3, 8, 9], ot=[6, 16], at=[10, 12, 17, 20], wo=[11, 14, 19, 22], x1t=[10, 12, 14, 17], lg=[11, 13, 15, 18], x_t=[19, 20, 21, 22], rk=[11], c_t=[14, 18], kr=[19, 20, 21, 22], v=[10, 11, 12, 13])
RSTD_AT, NORM_AT, ROUTE_AT, EXP_AT, GATES_AT, POS_AT, SCATTER_AT = 24, 24, 43, 47, 51, 59, 62
for _g in range(GROUPS):
    place("proj", _g, PLAN["proj"])
    place("ot", _g, PLAN["ot"][0:1], (2 * _g + 7) % 8)
    place("ot", _g, PLAN["ot"][1:2], 2 * _g)
for _k, _g in (("at", 0), ("wo", 0), ("x1t", 1), ("lg", 1), ("x_t", 1), ("rk", 2), ("c_t", 2), ("kr", 2), ("v", 3)):
    place(_k, _g, PLAN[_k])
ACT_TAKES = ("x_t", "c_t", "v", "at", "x1t")
LATE = ("at", "wo", "x1t", "lg", "rk")
NEXT = ("x_t", "c_t", "kr", "v")
JOBS = {"proj": 16, "ot": 8, "at": 4, "wo": 4, "x1t": 4, "lg": 4, "rk": 1, "x_t": 4, "c_t": 2,
        "kr": 4, "v": 4}


class Tally:

    def __init__(self):
        self.n, self.reg, self.start, self.per, self.at = 0, None, 0, 0, 0

    def value(self):
        return self.n if self.reg is None else (self.reg - self.start) * self.per + self.n

    def next(self):
        self.n += 1
        return self.value()

    def enter(self, reg, start, per):
        self.reg, self.start, self.per, self.at = reg, start, per, self.n

    def leave(self, iterations):
        assert self.n - self.at == self.per, f"{self.n - self.at} steps in the loop"
        self.n, self.reg = self.at + iterations * self.per, None


def layer(nc, x, w_dq, w_uq, w_qr, w_dkv, w_uk, w_uv, w_kr, w_o, wg, w1, b1, w2, b2,
          c_ident, c_sel, c_rope, c_tri, c_iota, out, dbg=None):
    ctx = ExitStack()
    with ctx:
        def sem(name):
            return ctx.enter_context(nc.semaphore(name))

        psum_scope = ExitStack()

        def psum(name, shape, where=None):
            return (where or psum_scope).enter_context(nc.psum_tensor(name, shape, F32))

        x1_d = dbg[0] if dbg else nc.dram_tensor("x1_scratch", (TOKENS, D), F32).ap()
        xs_d = dbg[1] if dbg else nc.dram_tensor("expert_in_scratch", (SPARE + P, ROW), F32).ap()
        ys_d = nc.dram_tensor("expert_out_scratch", (DUMMY + TOPK * TOKENS, D), F32).ap()

        keep = ctx

        def sb(name, shape, dt=F32, where=None):
            return (where or keep).enter_context(nc.sbuf_tensor(name, shape, dt))

        ident = sb("ident", [P, P])
        iota = sb("iota", [P, MOE_TILES + 1])
        lane = iota[:, MOE_TILES:MOE_TILES + 1]
        load = sb("load", [P, TILES + 1, E])
        gate_all = sb("gate_all", [P, B, TOPK, TILES])
        table = sb("table", [P, 2, MOE_TILES], I32)
        tile_expert = sb("tile_expert", [P, MOE_TILES])
        tail_row = sb("tail_row", [P, E], I32)
        zero_rows = sb("zero_rows", [P, ROW])
        with ExitStack() as operands:
            stacks = sb("stacks", [P, 2, 4, 2, S], F32R, where=operands)
            home = sb("home", [P, 4, S], F32R, where=operands)
            x_t = sb("x_t", [P, DT, S], where=operands)
        w1_sb = sb("w1_sb", [P, E, DT, HID])
        w2_sb = sb("w2_sb", [P, E, FT, D])
        b1_sb = sb("b1_sb", [P, E, HID])
        b2_sb = sb("b2_sb", [P, E, D])

        s_const = sem("constants_loaded")
        s_xin = [sem(f"x_loaded{i}") for i in range(2)]
        s_stack = [sem(f"stack_loaded{i}") for i in range(2)]
        s_z = sem("z_loaded")
        s_x1st = sem("x1_stored")
        s_scat = sem("x1_scattered")
        s_zero = sem("weights_zeroed")
        s_pool0 = sem("constants_set")
        s_setup = sem("weights_padded")
        s_qk = sem("scores_ready")
        s_exp = sem("exp_ready")
        s_clip = sem("clip_ready")
        s_mask = sem("mask_ready")
        s_pv = sem("pv_done")
        s_acc = sem("acc_evacuated")
        ready = {k: sem(f"{k}_in_psum") for k in JOBS}
        taken = {k: sem(f"{k}_taken") for k in JOBS}
        s_hi, s_lo = sem("high_parts_ready"), sem("low_parts_ready")
        s_rstd = sem("rstd_ready")
        s_vcopy = sem("v_in_place")
        s_x1 = sem("x1_ready")
        s_stat = sem("ln_stats_ready")
        s_hot = sem("onehot_ready")
        s_dexp = sem("router_exp_in")
        s_eexp = sem("router_exp_out")
        s_posr = sem("pos_ready")
        s_zero_rows, s_spare = sem("zero_rows_ready"), sem("spare_rows_zeroed")
        s_w = sem("expert_weights_loaded")
        tails_ready, tables_ready = sem("tail_rows_ready"), sem("tile_tables_ready")
        tails_zero = sem("region_tails_zeroed")
        c_tab = sem("table_chain")
        c_main, c_late, c_pool = sem("dve_chain"), sem("dve_chain_late"), sem("pool_chain")

        attn_scope = ExitStack()
        A = attn_scope
        wdown = sb("wdown", [P, DT, P], where=A)
        wup = sb("wup", [P, GROUPS, 4, QUAD], where=A)
        wkr = sb("wkr", [P, DT, P], where=A)
        wuv = sb("wuv", [P, D], where=A)
        wo = sb("wo", [P, DT, D], where=A)
        wgate = sb("wgate", [P, DT, E], where=A)
        sel = sb("sel", [P, P], where=A)
        tri = sb("tri", [P, 2, P], where=A)
        rope = sb("rope", [P, S], where=A)
        x_in = sb("x_in", [P, 2, 2, D], where=A)
        c_t = sb("c_t", [P, S], where=A)
        kr_part = sb("kr_part", [P, CHUNK], where=A)
        kr = sb("kr", [P, S], where=A)
        full = sb("full", [P, 2, CHUNK], where=A)
        v_new = sb("v_new", [P, TILES, 4 * DH], where=A)
        v_aug = sb("v_aug", [P, TILES, HEADS, DH + 1], where=A)
        p_sb = sb("p_sb", [P, P_SLOTS, 2, CHUNK], where=A)
        o_t = sb("o_t", [P, 2, CHUNK], where=A)
        recip = sb("recip", [P, 4, 4], where=A)
        attn = sb("attn", [P, TILES, D], where=A)
        attn_t = sb("attn_t", [P, 2, DT, 2 * P], where=A)
        z = sb("z", [P, TILES, ROW], where=A)
        token = sb("token", [P, TILES, 1], where=A)
        scratch = attn[:].rearrange("p t d -> p (t d)")

        def piece(at, *shape):
            view = scratch[:, at:at + int(np.prod(shape))]
            return view if len(shape) == 1 else view.rearrange("p (a b) -> p a b", a=shape[0])

        NT = MOE_TILES
        EXPERT, READ = range(2)
        cmp = piece(0, NT, E)
        over = piece(NT * E, E, TOKENS // P)
        tile_u, tile_r, t128 = (piece(NT * E + E * TOKENS // P + i * NT, NT) for i in range(3))
        n_tiles, ends, row_shift = (piece(NT * E + E * TOKENS // P + 3 * NT + i * E, E) for i in range(3))
        thr = piece(NT * E + E * TOKENS // P + 3 * NT + 3 * E, TOKENS // P)
        x1_t = sb("x1_t", [P, 2, DT, 2 * P], where=A)
        stats = sb("stats", [P, TILES, 6], where=A)
        mv = sb("mv", [P, TILES, 2], where=A)
        rstd = sb("rstd", [P, TILES, 1], where=A)
        expo = sb("expo", [P, TILES, 1], where=A)
        lg = sb("lg", [P, TILES, E], where=A)
        top = sb("top", [P, TILES, E], where=A)
        topi = sb("topi", [P, TILES, E], U32, where=A)
        topf = sb("topf", [P, TILES, E], where=A)
        dlt = sb("dlt", [P, TILES, E], where=A)
        ex = sb("ex", [P, TILES, E], where=A)
        den = sb("den", [P, TILES, 1], where=A)
        hot = sb("hot", [P, TOPK, TILES, E], where=A)
        hots = sb("hots", [P, TILES, E], where=A)
        rk = sb("rk", [P, 2, TILES, E], where=A)
        where_ = sb("where_", [P, TILES, E], where=A)
        tmp = sb("tmp", [P, TOPK, TILES, E], where=A)
        posf = sb("posf", [P, TOPK, TILES], where=A)
        pos = sb("pos", [P, TOPK * TILES], U32, where=A)
        region0 = sb("region0", [P, E], where=A)

        scores = psum("scores", [P, S_SLOTS, 2, CHUNK])
        acc = psum("acc", [P, CHUNK])
        misc = psum("misc", [P, CHUNK])

        x_tiles = x.rearrange("b (n t p) d -> (b n) p t d", t=2, p=P)
        x_batch = x.rearrange("b (t p) d -> b p t d", p=P)
        x1_batch = x1_d.rearrange("(b t p) d -> b p t d", b=B, p=P)

        with nc.Block() as block:
            @block.sync
            def _(sp):
                n = 0

                def const(dst, src):
                    nonlocal n
                    sp.dma_start(dst, src).then_inc(s_const, 16)
                    n += 1

                for m in range(2):
                    sp.dma_start(x_in[:, m], x_tiles[m]).then_inc(s_xin[m], 16)
                const(ident[:], c_ident)
                const(wdown[:, :, 0:LAT], w_dq.rearrange("(t p) n -> p t n", p=P))
                const(wdown[:, :, LAT:P], w_dkv.rearrange("(t p) n -> p t n", p=P))
                const(sel[:], c_sel)
                const(rope[:], c_rope)
                sp.wait_ge(s_zero, 2)
                const(wup[0:LAT, :, :, 0:DH].rearrange("p g j d -> p (g j) d"),
                      w_uq.rearrange("k (h d) -> k h d", d=DH))
                const(wup[0:LAT, :, :, DH:DH + DR].rearrange("p g j d -> p (g j) d"),
                      w_qr.rearrange("k (h d) -> k h d", d=DR))
                const(wup[LAT:P, :, :, 0:DH].rearrange("p g j d -> p (g j) d"),
                      w_uk.rearrange("k (h d) -> k h d", d=DH))
                const(wkr[:, :, DH:DH + DR], w_kr.rearrange("(t p) n -> p t n", p=P))
                const(wuv[LAT:P, :], w_uv)
                const(wo[:], w_o.rearrange("(t p) n -> p t n", p=P))
                const(wgate[:], wg.rearrange("(t p) n -> p t n", p=P))
                const(tri[:], c_tri.rearrange("a p n -> p a n"))
                const(iota[:], c_iota)
                assert n == CONSTS

                def x_in_load(b, m):
                    sp.wait_ge(ready["x_t"], b * 4 + m - 1)
                    sp.nop(nofuse=True)
                    sp.dma_start(x_in[:, m % 2], x_tiles[b * 4 + m]).then_inc(s_xin[m % 2], 16)

                def stack(b, g):
                    sp.wait_ge(s_lo, (b * GROUPS + g + 1) * 4)
                    sp.nop(nofuse=True)
                    if not (isinstance(b, int) and b * GROUPS + g < 2):
                        sp.wait_ge(s_qk, (b * GROUPS + g - 1) * PER_G)
                    for j in range(4):
                        for r in range(4):
                            q_part, k_part = r // 2, 2 + r % 2
                            sp.dma_start(stacks[QUAD * r:QUAD * (r + 1), g % 2, j].bitcast(F32),
                                         home[QUAD * j:QUAD * (j + 1), q_part:k_part + 1:k_part - q_part, :].bitcast(F32)
                                         ).then_inc(s_stack[j // 2], 16)

                def body(b, late, nxt):
                    if late:
                        if not (isinstance(b, int) and b < 2):
                            sp.wait_ge(s_x1st, 16 * (b - 1))
                            sp.nop(nofuse=True)
                            sp.wait_ge(s_scat, 256 * (b - 1))
                        sp.nop(nofuse=True)
                        sp.dma_start(z[:, :, 0:D], x_batch[b - 1]).then_inc(s_z, 16)
                    stack(b, 1)
                    if nxt:
                        x_in_load(b + 1, 0)
                        x_in_load(b + 1, 1)
                    if late:
                        sp.wait_ge(s_x1, 8 * b)
                        sp.nop(nofuse=True)
                        sp.dma_start(x1_batch[b - 1], z[:, :, 0:D]).then_inc(s_x1st, 16)
                    stack(b, 2)
                    if nxt:
                        x_in_load(b + 1, 2)
                        x_in_load(b + 1, 3)
                    stack(b, 3)
                    if nxt:
                        stack(b + 1, 0)

                sp.wait_ge(s_zero_rows, 1)
                sp.dma_start(xs_d[SPARE:SPARE + P, :], zero_rows[:]).then_inc(s_spare, 16)
                x_in_load(0, 2)
                x_in_load(0, 3)
                stack(0, 0)
                body(0, False, True)
                with sp.Fori(1, B - 1) as b:
                    body(b, True, True)
                body(B - 1, True, False)
                sp.wait_ge(s_x1st, 16 * (B - 1))
                sp.wait_ge(s_scat, 256 * (B - 1))
                sp.dma_start(z[:, :, 0:D], x_batch[B - 1]).then_inc(s_z, 16)
                sp.wait_ge(s_qk, (B - 1) * NU + 3 * PER_G)
                for e in range(E):
                    sp.dma_start(w1_sb[:, e], w1[e].rearrange("(t p) n -> p t n", p=P)).then_inc(s_w, 16)
                sp.wait_ge(ready["kr"], 4 * B)
                sp.dma_start(b2_sb[:], b2.partition_broadcast(P)).then_inc(s_w, 16)
                for i in range(2):
                    sp.wait_ge(s_stack[i], B * GROUPS * STACK_DMAS * 16)
                sp.dma_start(b1_sb[:], b1.partition_broadcast(P)).then_inc(s_w, 16)
                sp.wait_ge(s_qk, B * NU)
                for e in range(E):
                    sp.dma_start(w2_sb[:, e], w2[e].rearrange("(t p) n -> p t n", p=P)).then_inc(s_w, 16)
                sp.wait_ge(s_x1, 8 * B)
                sp.dma_start(x1_batch[B - 1], z[:, :, 0:D]).then_inc(s_x1st, 16)
                sp.wait_ge(tails_ready, 1)
                for e in range(E):
                    row = sp.value_load(tail_row[0:1, e:e + 1], min_val=0, max_val=SPARE - P)
                    sp.dma_start(xs_d[bass.ds(row, P), :], zero_rows[:]).then_inc(tails_zero, 16)
                sp.wait_ge(tails_zero, 16 * E)
                sp.wait_ge(s_spare, 16)
                sp.wait_ge(s_w, 16 * WEIGHT_LOADS)
                sp.wait_ge(s_x1st, 16 * B)
                sp.wait_ge(s_scat, 256 * B)

            @block.tensor
            def _(pe):
                last = [None, None]

                def bank(kind, count):
                    if last[0] is not None:
                        pe.wait_ge(last[0], last[1])
                    last[0], last[1] = taken[kind], count

                def job(kind, n, b):
                    count = b * JOBS[kind] + n + 1
                    bank(kind, count)
                    if kind == "x_t":
                        pe.wait_ge(s_xin[n % 2], (b * 2 + n // 2 + 1) * 16)
                        for dt in range(DT):
                            for t in range(2):
                                mm = nc.tensor.transpose(misc[:, (dt * 2 + t) * P:(dt * 2 + t + 1) * P],
                                                         x_in[:, n % 2, t, dt * P:(dt + 1) * P], ident[:])
                    elif kind == "c_t":
                        pe.wait_ge(taken["x_t"], b * 4 + 2 * n + 2)
                        for dt in range(DT):
                            mm = nc.tensor.matmul(misc[:], wdown[:, dt, :], x_t[:, dt, n * CHUNK:(n + 1) * CHUNK],
                                                  start=dt == 0, stop=dt == DT - 1)
                    elif kind == "kr" and n % 2 == 0:
                        pe.wait_ge(taken["x_t"], b * 4 + n + 2)
                        c = n // 2
                        for dt in range(DT):
                            mm = nc.tensor.matmul(misc[:], wkr[:, dt, :], x_t[:, dt, c * CHUNK:(c + 1) * CHUNK],
                                                  start=dt == 0, stop=dt == DT - 1)
                    elif kind == "kr":
                        mm = nc.tensor.matmul(misc[:], sel[:], kr_part[:], start=True, stop=True)
                    elif kind == "v":
                        pe.wait_ge(taken["c_t"], b * 2 + n // 2 + 1)
                        for t in range(2):
                            kt = 2 * n + t
                            mm = nc.tensor.matmul(misc[:, t * D:(t + 1) * D], c_t[LAT:P, kt * P:(kt + 1) * P],
                                                  wuv[LAT:P, :], start=True, stop=True)
                    elif kind == "proj":
                        g, c, is_k = n // 4, (n % 4) // 2, n % 2
                        pe.wait_ge(taken["c_t"], b * 2 + c + 1)
                        rows = slice(LAT, P) if is_k else slice(0, LAT)
                        mm = nc.tensor.matmul(misc[:], wup[rows, g].rearrange("p j d -> p (j d)"),
                                              c_t[rows, c * CHUNK:(c + 1) * CHUNK], start=True, stop=True)
                    elif kind == "ot":
                        pe.wait_ge(s_acc, b * 8 + n + 1)
                        for i in range(4):
                            mm = nc.tensor.transpose(misc[:, i * P:(i + 1) * P],
                                                     o_t[:, n % 2, i * P:(i + 1) * P], ident[:])
                    elif kind == "at":
                        pe.wait_ge(taken["ot"], b * 8 + (7 if n < 2 else 8))
                        for dt in range(DT):
                            for t in range(2):
                                mm = nc.tensor.transpose(misc[:, (dt * 2 + t) * P:(dt * 2 + t + 1) * P],
                                                         attn[:, 2 * n + t, dt * P:(dt + 1) * P], ident[:])
                    elif kind == "wo":
                        pe.wait_ge(taken["at"], b * 4 + n + 1)
                        for t in range(2):
                            for dt in range(DT):
                                mm = nc.tensor.matmul(misc[:, t * D:(t + 1) * D],
                                                      attn_t[:, n % 2, dt, t * P:(t + 1) * P], wo[:, dt, :],
                                                      start=dt == 0, stop=dt == DT - 1)
                    elif kind == "x1t":
                        pe.wait_ge(s_x1, b * 8 + 2 * n + 2)
                        for dt in range(DT):
                            for t in range(2):
                                mm = nc.tensor.transpose(misc[:, (dt * 2 + t) * P:(dt * 2 + t + 1) * P],
                                                         z[:, 2 * n + t, dt * P:(dt + 1) * P], ident[:])
                    elif kind == "lg":
                        pe.wait_ge(taken["x1t"], b * 4 + n + 1)
                        for t in range(2):
                            for dt in range(DT):
                                mm = nc.tensor.matmul(misc[:, t * E:(t + 1) * E],
                                                      x1_t[:, n % 2, dt, t * P:(t + 1) * P], wgate[:, dt, :],
                                                      start=dt == 0, stop=dt == DT - 1)
                    elif kind == "rk":
                        pe.wait_ge(s_hot, b + 1)
                        for a in range(2):
                            mm = nc.tensor.matmul(misc[:, a * TILES * E:(a + 1) * TILES * E], tri[:, a, :],
                                                  hots[:].rearrange("p t e -> p (t e)"), start=True, stop=True)
                    mm.then_inc(ready[kind], 1)

                def qk(b, u):
                    g, c, kt, hp = UNITS[u]
                    o = offset_in_chunk(c, kt)
                    if u % PER_G < 2:
                        pe.wait_ge(s_stack[hp], (b * GROUPS + g + 1) * STACK_DMAS * 16)
                    if not (isinstance(b, int) and b == 0 and u < S_SLOTS):
                        pe.wait_ge(s_exp, b * NU + u - S_SLOTS + 1)
                    for a in range(2):
                        j = 2 * hp + a
                        mm = nc.tensor.matmul(scores[:, u % S_SLOTS, a, o:CHUNK],
                                              stacks[:, g % 2, j, 1, kt * P:(kt + 1) * P],
                                              stacks[:, g % 2, j, 0, c * CHUNK + o:(c + 1) * CHUNK],
                                              start=True, stop=True)
                    mm.then_inc(s_qk, 1)

                def pv(b, u):
                    g, c, kt, hp = UNITS[u]
                    o = offset_in_chunk(c, kt)
                    if u == 0:
                        pe.wait_ge(taken["v"], (b + 1) * 4)
                    if u == (GROUPS - 1) * PER_G:
                        pe.wait_ge(s_vcopy, b + 1)
                    if kt == 0 and not (isinstance(b, int) and b == 0 and u == 0):
                        pe.wait_ge(s_acc, b * 8 + 2 * g + c)
                    if is_diag(u):
                        pe.wait_ge(s_mask, b * N_MASK + MASKS_BEFORE[u] + 2)
                    else:
                        pe.wait_ge(s_clip, b * NU + u + 2)
                    for j in range(4):
                        mm = nc.tensor.matmul(acc[QUAD * j:QUAD * j + DH + 1, o:CHUNK],
                                              v_aug[:, kt, 4 * g + j, :],
                                              p_sb[:, (u + j // 2) % P_SLOTS, j % 2, o:CHUNK],
                                              start=kt == 0, stop=kt == 4 * c + 3)
                    mm.then_inc(s_pv, 1)

                def body(b, late, nxt):
                    for u in range(NU):
                        qk(b, u)
                        if u in MISC:
                            kind, n = MISC[u]
                            if kind == "proj":
                                if u < 3 * PER_G:
                                    job("proj", (u // PER_G + 1) * 4 + n, b)
                                elif nxt:
                                    job("proj", n, b + 1)
                            elif kind == "ot" and n == 7:
                                if late:
                                    job("ot", 7, b - 1)
                            elif kind in LATE:
                                if late:
                                    job(kind, n, b - 1)
                            elif kind in NEXT:
                                if nxt:
                                    job(kind, n, b + 1)
                            else:
                                job("ot", n, b)
                        if u % 2 == 0 and u >= LAG:
                            pv(b, u - LAG)
                        elif u % 2 == 0 and late:
                            pv(b - 1, NU - LAG + u)

                pe.wait_ge(s_const, 16 * CONSTS)
                pe.wait_ge(s_setup, 5)
                for kind in ("x_t", "c_t", "kr"):
                    for n in range(JOBS[kind]):
                        job(kind, n, 0)
                for n in range(4):
                    job("proj", n, 0)
                for n in range(4):
                    job("v", n, 0)
                body(0, False, True)
                with pe.Fori(1, B - 1) as b:
                    last[0], last[1] = taken["ot"], b * 8 - 1
                    body(b, True, True)
                last[0], last[1] = taken["ot"], (B - 1) * 8 - 1
                body(B - 1, True, False)
                for u in range(NU - LAG, NU, 2):
                    pv(B - 1, u)
                job("ot", 7, B - 1)
                for n in range(4):
                    job("at", n, B - 1)
                    job("wo", n, B - 1)
                for n in range(4):
                    job("x1t", n, B - 1)
                    job("lg", n, B - 1)
                job("rk", 0, B - 1)

            @block.scalar
            def _(act):
                def exp(b, u):
                    _, c, kt, _ = UNITS[u]
                    o = offset_in_chunk(c, kt)
                    act.wait_ge(s_qk, b * NU + u + 1)
                    if not (isinstance(b, int) and b == 0 and u < P_SLOTS):
                        act.wait_ge(s_pv, b * (NU // 2) + (u - P_SLOTS) // 2 + 1)
                    nc.scalar.activation(p_sb[:, u % P_SLOTS, :, o:CHUNK], scores[:, u % S_SLOTS, :, o:CHUNK],
                                         ACT.Exp, scale=SCALE).then_inc(s_exp, 1)

                def evac(kind, n, b):
                    act.wait_ge(ready[kind], b * JOBS[kind] + n + 1)
                    m2 = misc[:].rearrange("p (a n) -> p a n", a=2)
                    if kind == "x_t":
                        if not (isinstance(b, int) and b == 0):
                            act.wait_ge(ready["kr"], b * 4)
                        to = x_t[:, :, n * 2 * P:(n + 1) * 2 * P]
                    elif kind == "c_t":
                        if not (isinstance(b, int) and b == 0):
                            act.wait_ge(ready["proj"], b * 16)
                            act.wait_ge(ready["v"], b * 4)
                        to, m2 = c_t[:, n * CHUNK:(n + 1) * CHUNK], misc[:]
                    elif kind == "v":
                        if not (isinstance(b, int) and b == 0):
                            act.wait_ge(s_vcopy, b)
                            act.wait_ge(s_pv, (b - 1) * (NU // 2) + (GROUPS - 1) * PER_G // 2)
                        last_g = (GROUPS - 1) * 4
                        vh = m2.rearrange("p t (h d) -> p t h d", d=DH)
                        nc.scalar.copy(v_aug[:, 2 * n:2 * n + 2, 0:last_g, 0:DH], vh[:, :, 0:last_g, :])
                        to, m2 = v_new[:, 2 * n:2 * n + 2, :], m2[:, :, last_g * DH:]
                    elif kind == "at":
                        if n >= 2:
                            act.wait_ge(ready["wo"], b * 4 + n - 1)
                        else:
                            act.wait_ge(ready["ot"], b * 8 + 7)
                        to = attn_t[:, n % 2, :, :]
                    elif kind == "x1t":
                        if n >= 2:
                            act.wait_ge(ready["lg"], b * 4 + n - 1)
                        to = x1_t[:, n % 2, :, :]
                    nc.scalar.copy(to, m2).then_inc(taken[kind], 1)

                def acc_out(b, n):
                    units = PER_G * (n // 2) + (C0 if n % 2 == 0 else PER_G)
                    act.wait_ge(s_pv, (b * NU + units) // 2 if isinstance(b, int) else b * (NU // 2) + units // 2)
                    if not (isinstance(b, int) and b == 0 and n < 2):
                        act.wait_ge(ready["ot"], b * 8 + n - 1)
                    nc.scalar.copy(o_t[:, n % 2, :], acc[:]).then_inc(s_acc, 1)

                def router_exp(b):
                    act.wait_ge(s_dexp, b + 1)
                    nc.scalar.activation(ex[:].rearrange("p t e -> p (t e)"),
                                         dlt[:].rearrange("p t e -> p (t e)"), ACT.Exp).then_inc(s_eexp, 1)

                def body(b, late, nxt):
                    for u in range(NU):
                        if u in MISC and MISC[u][0] in ACT_TAKES:
                            kind, n = MISC[u]
                            if kind in LATE and late:
                                evac(kind, n, b - 1)
                            if kind in NEXT and nxt:
                                evac(kind, n, b + 1)
                        if u == EXP_AT and late:
                            router_exp(b - 1)
                        if u % PER_G == C0 - 2 + LAG:
                            acc_out(b, 2 * (u // PER_G))
                        if u % PER_G == LAG - 2:
                            if u >= PER_G:
                                acc_out(b, 2 * (u // PER_G) - 1)
                            elif late:
                                acc_out(b - 1, 7)
                        exp(b, u)

                for kind in ("x_t", "c_t", "v"):
                    for n in range(JOBS[kind]):
                        evac(kind, n, 0)
                body(0, False, True)
                with act.Fori(1, B - 1) as b:
                    body(b, True, True)
                body(B - 1, True, False)
                acc_out(B - 1, 7)
                for kind in ("at", "x1t"):
                    for n in range(4):
                        evac(kind, n, B - 1)
                router_exp(B - 1)

            @block.vector
            def _(dve):
                main, late_t = Tally(), Tally()

                def evac(kind, n, b):
                    dve.wait_ge(ready[kind], b * JOBS[kind] + n + 1)
                    m2 = misc[:].rearrange("p (a n) -> p a n", a=2)
                    if kind == "kr" and n % 2 == 0:
                        c = n // 2
                        nc.vector.tensor_tensor(kr_part[:], misc[:], rope[:, c * CHUNK:(c + 1) * CHUNK],
                                                ALU.mult).then_inc(taken[kind], 1)
                    elif kind == "kr":
                        c = n // 2
                        nc.vector.tensor_copy(kr[:, c * CHUNK:(c + 1) * CHUNK], misc[:]).then_inc(taken[kind], 1)
                    elif kind == "proj":
                        g, c, is_k = n // 4, (n % 4) // 2, n % 2
                        if not (isinstance(b, int) and b == 0 and n < 2):
                            dve.wait_ge(s_lo, b * 16 + n - 1)
                        cs = slice(c * CHUNK, (c + 1) * CHUNK)
                        if is_k:
                            dve.wait_ge(taken["kr"], b * 4 + 2 * c + 2)
                            nc.vector.tensor_tensor(full[:, 1, :], misc[:], kr[:, cs], ALU.add).then_inc(taken[kind], 1)
                        else:
                            nc.vector.tensor_tensor(full[:, 0, :], misc[:], rope[:, cs], ALU.mult).then_inc(taken[kind], 1)
                        if n % 4 == 0 and not (isinstance(b, int) and b * 4 + g == 0):
                            for i in range(2):
                                dve.wait_ge(s_stack[i], (b * GROUPS + g) * STACK_DMAS * 16)
                        dve.wait_ge(taken[kind], b * 16 + n + 1)
                        nc.vector.tensor_copy(home[:, 2 * is_k, cs], full[:, is_k, :]).then_inc(s_hi, 1)
                    elif kind == "ot":
                        g, c = n // 2, n % 2
                        m4 = misc[:].rearrange("p (i j r) -> p i j r", i=4, j=4)
                        if not (isinstance(b, int) and b == 0):
                            dve.wait_ge(ready["at"], (b - 1) * 4 + 2 * c + 2)
                        nc.vector.reciprocal(recip[:], m4[:, :, :, DH]).then_inc(c_main, 1)
                        dve.wait_ge(c_main, main.next())
                        nc.vector.tensor_tensor(
                            attn[:, 4 * c:4 * c + 4, g * 4 * DH:(g + 1) * 4 * DH].rearrange("p i (j d) -> p i j d", j=4),
                            m4[:, :, :, 0:DH], recip[:].unsqueeze(3).to_broadcast([P, 4, 4, DH]), ALU.mult
                        ).then_inc(taken[kind], 1)
                    elif kind == "wo":
                        dve.wait_ge(s_z, (b + 1) * 16)
                        zz = z[:, 2 * n:2 * n + 2, 0:D]
                        nc.vector.tensor_tensor(zz, m2, zz, ALU.add).then_inc(taken[kind], 1)
                        dve.wait_ge(taken[kind], b * 4 + n + 1)
                        for t in range(2 * n, 2 * n + 2):
                            nc.vector.bn_stats(stats[:, t, :], z[:, t, 0:D]).then_inc(c_late, 1)
                            v = late_t.next()
                        dve.wait_ge(c_late, v)
                        dve.nop(nofuse=True)
                        for t in range(2 * n, 2 * n + 2):
                            nc.vector.bn_aggr(mv[:, t, :], stats[:, t, :]).then_inc(s_stat, 1)
                    elif kind == "lg":
                        nc.vector.tensor_copy(lg[:, 2 * n:2 * n + 2, :],
                                              misc[:, 0:2 * E].rearrange("p (t e) -> p t e", t=2)
                                              ).then_inc(taken[kind], 1)
                    elif kind == "rk":
                        nc.vector.tensor_copy(rk[:], misc[:, 0:2 * TILES * E].rearrange(
                            "p (a t e) -> p a t e", a=2, t=TILES)).then_inc(taken[kind], 1)

                def step(ins):
                    ins.then_inc(c_late, 1)
                    dve.wait_ge(c_late, late_t.next())

                def top_two(b):
                    dve.wait_ge(taken["lg"], (b + 1) * 4)
                    if not (isinstance(b, int) and b == 0):
                        dve.wait_ge(s_eexp, b)
                        dve.wait_ge(ready["rk"], b)
                    dve.nop(nofuse=True)
                    for t in range(TILES):
                        nc.vector.max(top[:, t, :], lg[:, t, :]).then_inc(c_late, 1)
                        v = late_t.next()
                    dve.wait_ge(c_late, v)
                    dve.nop(nofuse=True)
                    for t in range(TILES):
                        nc.vector.max_index(topi[:, t, :], top[:, t, :], lg[:, t, :]).then_inc(c_late, 1)
                        v = late_t.next()
                    nc.vector.tensor_tensor(dlt[:], top[:], top[:, :, 0:1].to_broadcast([P, TILES, E]),
                                            ALU.subtract).then_inc(s_dexp, 1)
                    dve.wait_ge(c_late, v)
                    step(nc.vector.tensor_copy(topf[:, :, 0:TOPK], topi[:, :, 0:TOPK]))
                    for k in range(TOPK):
                        nc.vector.tensor_tensor(hot[:, k], iota[:, 0:E].unsqueeze(1).to_broadcast([P, TILES, E]),
                                                topf[:, :, k:k + 1].to_broadcast([P, TILES, E]),
                                                ALU.is_equal).then_inc(c_late, 1)
                        v = late_t.next()
                    dve.wait_ge(c_late, v)
                    nc.vector.tensor_tensor(hots[:], hot[:, 0], hot[:, 1], ALU.add).then_inc(s_hot, 1)

                def gates_of(b):
                    dve.wait_ge(s_eexp, b + 1)
                    step(nc.vector.tensor_reduce(den[:].rearrange("p t o -> p (t o)"), ex[:], AX.X, ALU.add))
                    step(nc.vector.reciprocal(den[:], den[:]))
                    step(nc.vector.tensor_tensor(gate_all[:, b].rearrange("p k t -> p t k"), ex[:, :, 0:TOPK],
                                                 den[:].to_broadcast([P, TILES, TOPK]), ALU.mult))

                def positions(b):
                    dve.wait_ge(taken["rk"], b + 1)
                    for t in range(TILES):
                        step(nc.vector.tensor_tensor(load[:, t + 1, :], load[:, t, :], rk[:, 1, t, :], ALU.add))
                    step(nc.vector.tensor_tensor(where_[:], rk[:, 0], load[:, 0:TILES, :], ALU.add))
                    step(nc.vector.tensor_tensor(where_[:], where_[:],
                                                 region0[:].unsqueeze(1).to_broadcast([P, TILES, E]), ALU.add))
                    for k in range(TOPK):
                        step(nc.vector.tensor_tensor(tmp[:, k], where_[:], hot[:, k], ALU.mult))
                        step(nc.vector.tensor_reduce(posf[:, k, :], tmp[:, k], AX.X, ALU.add))
                    step(nc.vector.tensor_scalar(token[:], token[:], float(S), None, ALU.add))
                    if not (isinstance(b, int) and b == 0):
                        dve.wait_ge(s_scat, b * 256)
                    dve.nop(nofuse=True)
                    step(nc.vector.tensor_copy(z[:, :, D:D + 1], token[:]))
                    step(nc.vector.tensor_copy(z[:, :, D + 1:D + 2], topf[:, :, 0:1]))
                    nc.vector.tensor_copy(pos[:], posf[:].rearrange("p k t -> p (k t)")).then_inc(s_posr, 1)
                    step(nc.vector.tensor_copy(load[:, 0, :], load[:, TILES, :]))

                def norm(b, t):
                    if t == 0:
                        dve.wait_ge(s_rstd, b + 1)
                    nc.vector.tensor_scalar(z[:, t, 0:D], z[:, t, 0:D], mv[:, t, 0:1], rstd[:, t, :],
                                            ALU.subtract, ALU.mult).then_inc(s_x1, 1)

                def clip(b, u):
                    _, c, kt, _ = UNITS[u]
                    o = offset_in_chunk(c, kt)
                    dve.wait_ge(s_exp, b * NU + u + 1)
                    pp = p_sb[:, u % P_SLOTS, :, o:CHUNK]
                    nc.vector.tensor_scalar(pp, pp, EXP_LO, EXP_HI, ALU.max, ALU.min).then_inc(s_clip, 1)

                def v_place(b):
                    if not (isinstance(b, int) and b == 0):
                        dve.wait_ge(s_pv, b * (NU // 2))
                    dve.wait_ge(taken["v"], (b + 1) * 4)
                    nc.vector.tensor_copy(v_aug[:, :, (GROUPS - 1) * 4:, 0:DH],
                                          v_new[:].rearrange("p t (h d) -> p t h d", d=DH)).then_inc(s_vcopy, 1)

                def body(b, late, nxt):
                    for u in range(NU):
                        if u in MISC:
                            kind, n = MISC[u]
                            if kind == "proj":
                                if u < 3 * PER_G:
                                    evac("proj", (u // PER_G + 1) * 4 + n, b)
                                elif nxt:
                                    evac("proj", n, b + 1)
                            elif kind == "ot" and n == 7:
                                if late:
                                    evac("ot", 7, b - 1)
                            elif kind in ACT_TAKES:
                                pass
                            elif kind in LATE:
                                if late:
                                    evac(kind, n, b - 1)
                            elif kind in NEXT:
                                if nxt:
                                    evac(kind, n, b + 1)
                            else:
                                evac("ot", n, b)
                        if late and NORM_AT <= u < NORM_AT + TILES:
                            norm(b - 1, u - NORM_AT)
                        if late and u == ROUTE_AT:
                            top_two(b - 1)
                        if late and u == GATES_AT:
                            gates_of(b - 1)
                        if late and u == POS_AT:
                            positions(b - 1)
                        clip(b, u)
                        if u == LAG - 2:
                            v_place(b)

                def tables():
                    counts = load[:, 0, :]
                    steps = Tally()

                    def step(ins):
                        ins.then_inc(c_tab, 1)
                        dve.wait_ge(c_tab, steps.next())

                    step(nc.vector.tensor_scalar(row_shift, iota[:, 0:E], float(REGION), None, ALU.mult))
                    nc.vector.tensor_tensor(tail_row[:], counts, row_shift, ALU.add).then_inc(tails_ready, 1)
                    step(nc.vector.tensor_scalar(thr, iota[:, 0:TOKENS // P], float(P), None, ALU.mult))
                    sh = [P, E, TOKENS // P]
                    step(nc.vector.tensor_tensor(over, counts.unsqueeze(2).to_broadcast(sh),
                                                 thr.unsqueeze(1).to_broadcast(sh), ALU.is_gt))
                    step(nc.vector.tensor_reduce(n_tiles, over, AX.X, ALU.add))
                    step(nc.vector.tensor_copy(ends, n_tiles))
                    for e in range(1, E):
                        step(nc.vector.tensor_tensor(ends[:, e:e + 1], ends[:, e:e + 1], ends[:, e - 1:e], ALU.add))
                    sh = [P, NT, E]
                    ends_b = ends.unsqueeze(1).to_broadcast(sh)
                    step(nc.vector.tensor_tensor(cmp, iota[:, 0:NT].unsqueeze(2).to_broadcast(sh), ends_b, ALU.is_ge))
                    step(nc.vector.tensor_reduce(tile_expert[:], cmp, AX.X, ALU.add))
                    step(nc.vector.tensor_tensor(ends, ends, n_tiles, ALU.subtract))
                    step(nc.vector.tensor_scalar(ends, ends, float(P), None, ALU.mult))
                    step(nc.vector.tensor_tensor(row_shift, row_shift, ends, ALU.subtract))
                    step(nc.vector.tensor_tensor(cmp, iota[:, 0:E].unsqueeze(1).to_broadcast(sh),
                                                 tile_expert[:].unsqueeze(2).to_broadcast(sh), ALU.is_equal))
                    step(nc.vector.tensor_tensor(cmp, cmp, row_shift.unsqueeze(1).to_broadcast(sh), ALU.mult))
                    step(nc.vector.tensor_reduce(tile_r, cmp, AX.X, ALU.add))
                    step(nc.vector.tensor_scalar(t128, iota[:, 0:NT], float(P), None, ALU.mult))
                    step(nc.vector.tensor_tensor(tile_r, tile_r, t128, ALU.add))
                    step(nc.vector.tensor_scalar(tile_u, tile_expert[:], float(E), None, ALU.is_ge))
                    step(nc.vector.tensor_scalar(tile_expert[:], tile_expert[:], float(E - 1), None, ALU.min))
                    step(nc.vector.tensor_copy(table[:, EXPERT, :], tile_expert[:]))
                    step(nc.vector.scalar_tensor_tensor(tile_r, tile_u, float(SPARE), tile_r, ALU.mult, ALU.add))
                    step(nc.vector.tensor_tensor(t128, t128, tile_u, ALU.mult))
                    nc.vector.tensor_tensor(table[:, READ, :], tile_r, t128, ALU.subtract).then_inc(tables_ready, 1)

                nc.vector.memset(zero_rows[:], 0.0).then_inc(s_zero_rows, 1)
                dve.wait_ge(s_pool0, 3)
                dve.wait_ge(s_const, 16 * CONSTS)
                for to, of in ((0, 1), (1, 0)):
                    nc.vector.tensor_copy(wup[0:LAT, :, :, DH + DR + to:QUAD:2],
                                          wup[0:LAT, :, :, DH + of:DH + DR:2]).then_inc(s_setup, 1)
                    nc.vector.tensor_copy(wkr[:, :, DH + DR + to:QUAD:2],
                                          wkr[:, :, DH + of:DH + DR:2]).then_inc(s_setup, 1)
                nc.vector.tensor_scalar(region0[:], iota[:, 0:E], float(REGION), None, ALU.mult).then_inc(c_main, 1)
                dve.wait_ge(c_main, main.next())
                nc.vector.tensor_scalar(token[:].rearrange("p t o -> p (t o)"), iota[:, 0:TILES], float(P),
                                        float(DUMMY + TOKENS - S), ALU.mult, ALU.add).then_inc(c_main, 1)
                dve.wait_ge(c_main, main.next())
                nc.vector.tensor_scalar(token[:].rearrange("p t o -> p (t o)"),
                                        token[:].rearrange("p t o -> p (t o)"), lane, None, ALU.add).then_inc(c_main, 1)
                dve.wait_ge(c_main, main.next())
                nc.vector.memset(acc[:], 0.0).then_inc(s_setup, 1)
                for n in range(4):
                    evac("kr", n, 0)
                for n in range(4):
                    evac("proj", n, 0)
                body(0, False, True)
                with dve.Fori(1, B - 1) as b:
                    main.enter(b, 1, DVE_MAIN_STEPS)
                    late_t.enter(b, 1, DVE_LATE_STEPS)
                    body(b, True, True)
                main.leave(B - 2)
                late_t.leave(B - 2)
                body(B - 1, True, False)
                evac("ot", 7, B - 1)
                for n in range(4):
                    evac("wo", n, B - 1)
                for t in range(TILES):
                    norm(B - 1, t)
                for n in range(4):
                    evac("lg", n, B - 1)
                top_two(B - 1)
                gates_of(B - 1)
                evac("rk", 0, B - 1)
                positions(B - 1)
                tables()

            @block.gpsimd
            def _(pool):
                chain = Tally()

                def low_part(b, n):
                    c, is_k = (n % 4) // 2, n % 2
                    cs = slice(c * CHUNK, (c + 1) * CHUNK)
                    pool.wait_ge(s_hi, b * 16 + n + 1)
                    nc.gpsimd.tensor_tensor(home[:, 2 * is_k + 1, cs], full[:, is_k, :],
                                            home[:, 2 * is_k, cs].bitcast(F32), ALU.subtract).then_inc(s_lo, 1)

                def mask(b, u):
                    _, c, kt, _ = UNITS[u]
                    o = offset_in_chunk(c, kt)
                    pool.wait_ge(s_clip, b * NU + u + 1)
                    pool.nop(nofuse=True)
                    pp = p_sb[:, u % P_SLOTS, :, o:o + P]
                    nc.gpsimd.affine_select(out=pp, in_=pp, compare_op=ALU.is_ge, fill=0.0, base=0,
                                            pattern=[[0, 2], [1, P]], channel_multiplier=-1).then_inc(s_mask, 1)

                def rstd_of(b):
                    pool.wait_ge(s_stat, (b + 1) * 8)
                    pool.nop(nofuse=True)
                    nc.gpsimd.tensor_scalar(rstd[:], mv[:, :, 1:2], EPS, None, ALU.add).then_inc(c_pool, 1)
                    pool.wait_ge(c_pool, chain.next())
                    nc.gpsimd.tensor_tensor(rstd[:], rstd[:], expo[:], ALU.pow).then_inc(s_rstd, 1)

                def scatter(b, n):
                    k, t = n % 2, n // 2
                    if n == 0:
                        pool.wait_ge(s_posr, b + 1)
                        pool.wait_ge(s_x1, (b + 1) * 8)
                        pool.nop(nofuse=True)
                    nc.gpsimd.indirect_dma_start(
                        out=xs_d, out_offset=bass.IndirectOffsetOnAxis(ap=pos[:, k * TILES + t:k * TILES + t + 1], axis=0),
                        in_=z[:, t, :], in_offset=None).then_inc(s_scat, 16)

                def body(b, late, nxt):
                    for u in range(NU):
                        if u in MISC and MISC[u][0] == "proj":
                            n = MISC[u][1]
                            if u < 3 * PER_G:
                                low_part(b, (u // PER_G + 1) * 4 + n)
                            elif nxt:
                                low_part(b + 1, n)
                        if late and u == RSTD_AT:
                            rstd_of(b - 1)
                        if late and SCATTER_AT <= u < SCATTER_AT + 2 * TILES:
                            scatter(b - 1, u - SCATTER_AT)
                        at = behind(b, u, POOL_BEHIND, late)
                        if at and is_diag(at[1]):
                            mask(*at)

                nc.gpsimd.memset(wup[:], 0.0).then_inc(s_zero, 1)
                nc.gpsimd.memset(wkr[:], 0.0).then_inc(s_zero, 1)
                nc.gpsimd.memset(v_aug[:], 1.0).then_inc(s_pool0, 1)
                nc.gpsimd.memset(expo[:], -0.5).then_inc(s_pool0, 1)
                nc.gpsimd.memset(load[:], 0.0).then_inc(s_pool0, 1)
                for n in range(4):
                    low_part(0, n)
                body(0, False, True)
                with pool.Fori(1, B - 1) as b:
                    chain.enter(b, 1, 1)
                    body(b, True, True)
                chain.leave(B - 2)
                body(B - 1, True, False)
                for u in range(NU - POOL_BEHIND, NU):
                    mask(B - 1, u)
                rstd_of(B - 1)
                for n in range(2 * TILES):
                    scatter(B - 1, n)

        psum_scope.close()
        attn_scope.close()

        s_xs = [sem(f"rows_loaded{i}") for i in range(2)]
        s_xsT_ps, s_xsT = sem("rows_t_in_psum"), sem("rows_t_ready")
        s_h_ps, s_h = sem("hidden_in_psum"), sem("hidden_ready")
        s_hT_ps, s_hT = sem("hidden_t_in_psum"), sem("hidden_t_ready")
        s_y_ps, s_y = sem("expert_out_in_psum"), sem("expert_out_ready")
        s_yst = [sem(f"expert_out_stored{i}") for i in range(2)]
        s_dest = sem("destinations_ready")
        c_dest = sem("destination_chain")
        s_res = [sem(f"residual_loaded{i}") for i in range(2)]
        rows = sb("rows", [P, 2, TOPK, TILES, D])
        res = sb("res", [P, 2, TILES, D])
        moe_scope = ExitStack()
        M = moe_scope
        xs = sb("xs", [P, 2, ROW], where=M)
        mine = sb("mine", [P, 2, 1], where=M)
        destf = sb("destf", [P, MOE_TILES], where=M)
        dest = sb("dest", [P, 2, 1], U32, where=M)
        dummy = sb("padding_rows", [P, 2, 1], where=M)
        xs_t = sb("xs_t", [P, 2, DT, P], where=M)
        h = sb("h", [P, 2, HID], where=M)
        h_t = sb("h_t", [P, 2, FT, P], where=M)
        y = sb("y", [P, 2, D], where=M)
        ps_x = [psum(f"ps_x{i}", [P, CHUNK], M) for i in range(2)]
        ps_h = [psum(f"ps_h{i}", [P, CHUNK], M) for i in range(2)]
        ps_t = [psum(f"ps_t{i}", [P, CHUNK], M) for i in range(2)]
        ps_y = [psum(f"ps_y{i}", [P, CHUNK], M) for i in range(2)]
        LOOP_END = MOE_TILES - 2

        with nc.Block() as block:
            @block.sync
            def _(sp):
                def load_rows(n, slot, first=False):
                    row = sp.value_load(table[0:1, READ, bass.ds(n, 1)], min_val=0, max_val=SPARE)
                    if not first:
                        sp.wait_ge(s_xsT_ps, n - 1)
                        sp.wait_ge(c_dest, 2 * n - 2)
                    sp.nop(nofuse=True)
                    sp.dma_start(xs[:, slot, :], xs_d[bass.ds(row, P), :]).then_inc(s_xs[slot], 16)

                load_rows(0, 0, True)
                load_rows(1, 1, True)
                for i in range(2):
                    sp.dma_start(res[:, i], x1_batch[i]).then_inc(s_res[i], 16)
                with sp.Fori(1, MOE_TILES // 2) as pair:
                    load_rows(2 * pair, 0)
                    load_rows(2 * pair + 1, 1)

            @block.tensor
            def _(pe):
                def rows_t(n, slot, first=False):
                    pe.wait_ge(s_xs[slot], 16 * (n // 2 + 1) if isinstance(n, int) else (n - slot) * 8 + 16)
                    if not first:
                        pe.wait_ge(s_xsT, n - 1)
                    for dt in range(DT):
                        mm = nc.tensor.transpose(ps_x[slot][:, dt * P:(dt + 1) * P],
                                                 xs[:, slot, dt * P:(dt + 1) * P], ident[:])
                    mm.then_inc(s_xsT_ps, 1)

                def up(n, slot, first=False):
                    e = pe.value_load(table[0:1, EXPERT, bass.ds(n, 1)], min_val=0, max_val=E - 1)
                    pe.wait_ge(s_xsT, n + 1)
                    if not first:
                        pe.wait_ge(s_h, n - 1)
                    for dt in range(DT):
                        mm = nc.tensor.matmul(ps_h[slot][:, :], xs_t[:, slot, dt, :], w1_sb[:, e, dt, :],
                                              start=dt == 0, stop=dt == DT - 1)
                    mm.then_inc(s_h_ps, 1)

                def hidden_t(n, slot, first=False):
                    pe.wait_ge(s_h, n + 1)
                    if not first:
                        pe.wait_ge(s_hT, n - 1)
                    for f in range(FT):
                        mm = nc.tensor.transpose(ps_t[slot][:, f * P:(f + 1) * P],
                                                 h[:, slot, f * P:(f + 1) * P], ident[:])
                    mm.then_inc(s_hT_ps, 1)

                def down(n, slot, first=False):
                    e = pe.value_load(table[0:1, EXPERT, bass.ds(n, 1)], min_val=0, max_val=E - 1)
                    pe.wait_ge(s_hT, n + 1)
                    if not first:
                        pe.wait_ge(s_y, n - 1)
                    for f in range(FT):
                        mm = nc.tensor.matmul(ps_y[slot][:, 0:D], h_t[:, slot, f, :], w2_sb[:, e, f, :],
                                              start=f == 0, stop=f == FT - 1)
                    mm.then_inc(s_y_ps, 1)

                rows_t(0, 0, True)

                def turn(n, slot):
                    static = isinstance(n, int)
                    if not static or n < MOE_TILES:
                        up(n, slot, static and n < 2)
                    if not static or 1 <= n <= MOE_TILES:
                        hidden_t(n - 1, 1 - slot, static and n < 3)
                    if not static or n + 1 < MOE_TILES:
                        rows_t(n + 1, 1 - slot, static and n < 1)
                    if not static or n >= 2:
                        down(n - 2, slot, static and n < 4)

                for n in range(4):
                    turn(n, n % 2)
                with pe.Fori(2, LOOP_END // 2) as pair:
                    for k in range(2):
                        turn(2 * pair + k, k)
                for n in range(LOOP_END, MOE_TILES + 2):
                    turn(n, n % 2)

            @block.scalar
            def _(act):
                def rows_out(n, slot, first=False):
                    act.wait_ge(s_xsT_ps, n + 1)
                    if not first:
                        act.wait_ge(s_h_ps, n - 1)
                    nc.scalar.copy(xs_t[:, slot].rearrange("p t n -> p (t n)"), ps_x[slot][:, 0:D]).then_inc(s_xsT, 1)

                def relu_out(n, slot, first=False):
                    act.wait_ge(s_hT_ps, n + 1)
                    if not first:
                        act.wait_ge(s_y_ps, n - 1)
                    nc.scalar.activation(h_t[:, slot].rearrange("p t n -> p (t n)"), ps_t[slot][:, :],
                                         ACT.Relu).then_inc(s_hT, 1)

                rows_out(0, 0, True)
                rows_out(1, 1, True)
                relu_out(0, 0, True)
                rows_out(2, 0)
                relu_out(1, 1, True)
                rows_out(3, 1)
                with act.Fori(1, LOOP_END // 2) as pair:
                    for k in range(2):
                        n = 2 * pair
                        relu_out(n + k, k)
                        rows_out(n + k + 2, k)
                for n in range(MOE_TILES - 2, MOE_TILES):
                    relu_out(n, n % 2)

            @block.vector
            def _(dve):
                def hidden(n, slot, first=False):
                    e = dve.value_load(table[0:1, EXPERT, bass.ds(n, 1)], min_val=0, max_val=E - 1)
                    dve.wait_ge(s_h_ps, n + 1)
                    if not first:
                        dve.wait_ge(s_hT_ps, n - 1)
                    static = isinstance(n, int)
                    dve.wait_ge(s_xs[slot], 16 * (n // 2 + 1) if static else (n - slot) * 8 + 16)
                    nc.vector.tensor_tensor(mine[:, slot], xs[:, slot, D + 1:D + 2],
                                            tile_expert[:, bass.ds(n, 1)], ALU.is_equal).then_inc(c_dest, 1)
                    dve.wait_ge(c_dest, 2 * n + 1)
                    nc.vector.scalar_tensor_tensor(destf[:, bass.ds(n, 1)], mine[:, slot], float(-TOKENS),
                                                   xs[:, slot, D:D + 1], ALU.mult, ALU.add).then_inc(c_dest, 1)
                    nc.vector.tensor_tensor(h[:, slot, :], ps_h[slot][:, :], b1_sb[:, e, :], ALU.add).then_inc(s_h, 1)

                def expert_out(n, slot, first=False):
                    e = dve.value_load(table[0:1, EXPERT, bass.ds(n, 1)], min_val=0, max_val=E - 1)
                    dve.wait_ge(s_y_ps, n + 1)
                    if not first:
                        dve.wait_ge(s_yst[slot], (n - slot) * 8)
                    dve.wait_ge(c_dest, 2 * n + 2)
                    nc.vector.tensor_tensor(dest[:, slot], destf[:, bass.ds(n, 1)], dummy[:, slot],
                                            ALU.max).then_inc(s_dest, 1)
                    nc.vector.tensor_tensor(y[:, slot, :], ps_y[slot][:, 0:D], b2_sb[:, e, :], ALU.add).then_inc(s_y, 1)

                for slot in range(2):
                    nc.vector.tensor_scalar(dummy[:, slot], lane, float(slot * P), None, ALU.add)
                hidden(0, 0, True)
                hidden(1, 1, True)
                hidden(2, 0)
                expert_out(0, 0, True)
                hidden(3, 1)
                expert_out(1, 1, True)
                with dve.Fori(2, MOE_TILES // 2) as pair:
                    for k in range(2):
                        n = 2 * pair
                        hidden(n + k, k)
                        expert_out(n + k - 2, k)
                for n in range(MOE_TILES - 2, MOE_TILES):
                    expert_out(n, n % 2)

            @block.gpsimd
            def _(pool):
                def store_rows(n, slot):
                    pool.wait_ge(s_y, n + 1)
                    pool.wait_ge(s_dest, n + 1)
                    pool.nop(nofuse=True)
                    nc.gpsimd.indirect_dma_start(
                        out=ys_d, out_offset=bass.IndirectOffsetOnAxis(ap=dest[:, slot], axis=0),
                        in_=y[:, slot, :], in_offset=None).then_inc(s_yst[slot], 16)

                with pool.Fori(0, MOE_TILES // 2) as pair:
                    store_rows(2 * pair, 0)
                    store_rows(2 * pair + 1, 1)
                for slot in range(2):
                    pool.wait_ge(s_yst[slot], 8 * MOE_TILES)

        moe_scope.close()

        s_rows = [[sem(f"rows_loaded{i}{hf}") for hf in range(2)] for i in range(2)]
        s_gate = sem("batch_gates_ready")
        s_sum = sem("sums_ready")
        s_st = sem("final_stats_ready")
        s_rs = sem("final_rstd_ready")
        s_o = sem("out_ready")
        s_ost = sem("out_stored")
        c_fin, c_fp = sem("final_chain"), sem("final_pool_chain")
        F = ExitStack()
        gate_cur = sb("gate_cur", [P, 2, TOPK, TILES], where=F)
        fst = sb("fst", [P, 2, TILES, 6], where=F)
        fmv = sb("fmv", [P, 2, TILES, 2], where=F)
        frs = sb("frs", [P, 2, TILES, 1], where=F)
        fexpo = sb("fexpo", [P, TILES, 1], where=F)
        HALF = TILES // 2
        out_batch = out.rearrange("b (t p) d -> b p t d", p=P)
        ys_batch = ys_d[DUMMY:DUMMY + TOPK * TOKENS, :].rearrange("(k b t p) d -> k b p t d", k=TOPK, b=B, p=P)

        def half(hf):
            return slice(hf * HALF, (hf + 1) * HALF)

        with nc.Block() as block:
            @block.sync
            def _(sp):
                def load(b):
                    i = b % 2
                    for hf in range(2):
                        if b >= 2:
                            sp.wait_ge(s_sum, (b - 2) * TILES + (hf + 1) * HALF)
                        for k in range(TOPK):
                            sp.dma_start(rows[:, i, k, half(hf), :], ys_batch[k, b, :, half(hf), :]
                                         ).then_inc(s_rows[i][hf], 16)
                    if b >= 2:
                        sp.wait_ge(s_ost, 32 * (b - 1))
                        sp.dma_start(res[:, i], x1_batch[b]).then_inc(s_res[i], 16)

                def store(b):
                    for hf in range(2):
                        sp.wait_ge(s_o, b * TILES + (hf + 1) * HALF)
                        sp.dma_start(out_batch[b, :, half(hf), :], res[:, b % 2, half(hf), :]).then_inc(s_ost, 16)

                load(0)
                load(1)
                for b in range(B):
                    store(b)
                    if b + 2 < B:
                        load(b + 2)
                sp.wait_ge(s_ost, B * 2 * 16)

            @block.gpsimd
            def _(pool):
                nc.gpsimd.memset(fexpo[:], -0.5).then_inc(c_fp, 1)
                pool.wait_ge(c_fp, 1)
                chain = Tally()
                chain.next()
                with pool.Fori(0, B // 2) as pair:
                    chain.enter(pair, 0, 4)
                    for i in range(2):
                        for hf in range(2):
                            ts = half(hf)
                            pool.wait_ge(s_st, (2 * pair + i) * TILES + (hf + 1) * HALF)
                            pool.nop(nofuse=True)
                            nc.gpsimd.tensor_scalar(frs[:, i, ts], fmv[:, i, ts, 1:2], EPS, None, ALU.add
                                                    ).then_inc(c_fp, 1)
                            pool.wait_ge(c_fp, chain.next())
                            pool.nop(nofuse=True)
                            nc.gpsimd.tensor_tensor(frs[:, i, ts], frs[:, i, ts], fexpo[:, ts], ALU.pow
                                                    ).then_inc(s_rs, 1)
                chain.leave(B // 2)

            @block.vector
            def _(dve):
                steps = Tally()

                def sum_half(b, i, hf):
                    dve.wait_ge(s_rows[i][hf], (b - i) * 16 + 32)
                    for t in range(hf * HALF, (hf + 1) * HALF):
                        for k in range(TOPK):
                            nc.vector.scalar_tensor_tensor(
                                res[:, i, t, :], rows[:, i, k, t, :], gate_cur[:, i, k, t:t + 1], res[:, i, t, :],
                                ALU.mult, ALU.add).then_inc(s_sum if k else c_fin, 1)
                            if k == 0:
                                dve.wait_ge(c_fin, steps.next())
                        dve.wait_ge(s_sum, b * TILES + t + 1)
                        nc.vector.bn_stats(fst[:, i, t, :], res[:, i, t, :]).then_inc(c_fin, 1)
                        dve.wait_ge(c_fin, steps.next())
                        dve.nop(nofuse=True)
                        nc.vector.bn_aggr(fmv[:, i, t, :], fst[:, i, t, :]).then_inc(s_st, 1)

                def norm_half(b, i, hf):
                    dve.wait_ge(s_rs, b * 2 + hf + 1)
                    for t in range(hf * HALF, (hf + 1) * HALF):
                        nc.vector.tensor_scalar(res[:, i, t, :], res[:, i, t, :], fmv[:, i, t, 0:1],
                                                frs[:, i, t, :], ALU.subtract, ALU.mult).then_inc(s_o, 1)

                with dve.Fori(0, B // 2) as pair:
                    steps.enter(pair, 0, 4 * TILES)
                    for i in range(2):
                        b = 2 * pair + i
                        nc.vector.tensor_copy(gate_cur[:, i].rearrange("p k t -> p (k t)"),
                                              gate_all[:, b].rearrange("p k t -> p (k t)")).then_inc(s_gate, 1)
                        dve.wait_ge(s_gate, b + 1)
                        dve.wait_ge(s_res[i], pair * 16 + 16)
                        sum_half(b, i, 0)
                        sum_half(b, i, 1)
                        norm_half(b, i, 0)
                        norm_half(b, i, 1)
                steps.leave(B // 2)

        F.close()


def constants():
    ident = np.eye(P, dtype=np.float32)
    sel = np.zeros((P, P), np.float32)
    for d in range(DR):
        for j in range(4):
            for half in range(2):
                to = QUAD * j + DH + DR * half + d
                sel[DH + d, to] = sel[DH + DR + d, to] = 1.0
    inv = np.float32(10000.0) ** (-np.arange(0, DR, 2, dtype=np.float32) / np.float32(DR))
    ang = np.arange(S, dtype=np.float32)[:, None] * inv.astype(np.float32)
    cos, sin = np.cos(ang).T, np.sin(ang).T
    rope = np.ones((P, S), np.float32)
    for j in range(4):
        for d in range(DR):
            rope[QUAD * j + DH + d] = cos[d // 2]
            rope[QUAD * j + DH + DR + d] = sin[d // 2] if d % 2 else -sin[d // 2]
    tri = np.stack([np.triu(np.ones((P, P), np.float32), 1), np.ones((P, P), np.float32)])
    iota = np.zeros((P, MOE_TILES + 1), np.float32)
    iota[:, 0:MOE_TILES] = np.arange(MOE_TILES)
    iota[:, MOE_TILES] = np.arange(P)
    return {"ident": ident, "sel": sel, "rope": rope, "tri": tri, "iota": iota}


_INS = ["L0_attn_x", "L0_attn_W_DQ", "L0_attn_W_UQ", "L0_attn_W_QR", "L0_attn_W_DKV", "L0_attn_W_UK",
        "L0_attn_W_UV", "L0_attn_W_KR", "L0_attn_W_O", "L0_ffn_Wg", "L0_ffn_W1", "L0_ffn_b1",
        "L0_ffn_W2", "L0_ffn_b2"]


def kernel(**inputs):
    import concourse.bacc as _bacc
    from concourse.bass_utils import run_bass_kernel_spmd as _run

    nc = _bacc.Bacc("TRN2", target_bir_lowering=False, num_devices=1)
    arrays, args = {}, []
    given = {name: np.ascontiguousarray(inputs[name]) for name in _INS} | constants()
    for name, a in given.items():
        arrays[f"in_{name}_dram"] = a
        args.append(nc.dram_tensor(f"in_{name}_dram", a.shape, mybir.dt.from_np(a.dtype), kind="ExternalInput").ap())
    out = nc.dram_tensor("out_0_dram", (B, S, D), F32, kind="ExternalOutput").ap()
    layer(nc, *args, out)
    r = _run(nc, [arrays], core_ids=[0])
    return r.results[0]["out_0_dram"]
```

```python
from contextlib import ExitStack

import concourse.bass as bass
import numpy as np
from concourse import mybir

ALU = mybir.AluOpType
ACT = mybir.ActivationFunctionType
AX = mybir.AxisListType
F32 = mybir.dt.float32
F32R = mybir.dt.float32r
I32 = mybir.dt.int32
U32 = mybir.dt.uint32

P = 128
B, S, D = 4, 1024, 256
HEADS, DH, DR, LAT = 16, 16, 8, 64
QUAD = 32
GROUPS = HEADS // 4
TILES = S // P
CHUNK = 512
CHUNKS = S // CHUNK
DT = D // P
QUARTER = S // 4
FIRST_CONSTS = 3
PROLOGUE_CONSTS = 12
LATER_CONSTS = 4
DVE_MAIN_STEPS, DVE_LATE_STEPS = 8, 48
WEIGHT_LOADS = 2 * 8 + 2
STACK_DMAS = 8
E, TOPK, HID = 8, 2, 512
FT = HID // P
EPS = 1e-5
SCALE = float(DH + DR) ** -0.5
CLIP = 80.0
EXP_LO = float(np.exp(-CLIP * SCALE))
EXP_HI = float(np.exp(CLIP * SCALE))
TOKENS = B * S
REGION = TOKENS + P
SPARE = E * REGION
MOE_TILES = (TOKENS * TOPK + E * (P - 1)) // P + 1
assert MOE_TILES % 2 == 0
ROW = D + 2
DUMMY = 2 * P

UNITS = [(g, c, kt, hp) for g in range(GROUPS) for c in range(CHUNKS)
         for kt in range(4 * c + 4) for hp in range(2)]
NU = len(UNITS)
PER_G = NU // GROUPS
C0 = 8
LAG = 6
S_SLOTS, P_SLOTS = 2, LAG + 2


def offset_in_chunk(c, kt):
    return max(0, kt - 4 * c) * P


def is_diag(u):
    _, c, kt, _ = UNITS[u]
    return kt >= 4 * c


MASKS_BEFORE = [sum(is_diag(v) for v in range(u)) for u in range(NU + 1)]
N_MASK = MASKS_BEFORE[NU]

PLAN = dict(proj=[1, 3, 5, 6], ot=[9, 15], at=[10, 13, 18, 20],
            wo=[11, 14, 19, 21], x1t=[10, 11, 14, 16],
            lg=[12, 13, 17, 18], x_t=[19, 20, 21, 23], rk=[10],
            c_t=[14, 18], kr=[19, 20, 23], v=[10, 11, 12, 13])
RSTD_AT, NORM_AT, ROUTE_AT, EXP_AT, GATES_AT, POS_AT = 24, 28, 45, 47, 46, 59
SCATTER_AT = [63, 64, 65, 66, 67, 68, 69, 70, 81, 82, 83, 84, 85, 86, 87, 88]
EDGE_PROJ = [1, 2, 4, 6]


def misc_jobs(proj):
    jobs = {}

    def place(kind, group, positions, first=0):
        for n, i in enumerate(positions):
            assert group * PER_G + i not in jobs
            jobs[group * PER_G + i] = (kind, n + first)

    for g in range(GROUPS):
        place("proj", g, proj)
        place("ot", g, PLAN["ot"][0:1], (2 * g + 7) % 8)
        place("ot", g, PLAN["ot"][1:2], 2 * g)
    for kind, g in (("at", 0), ("wo", 0), ("x1t", 1), ("lg", 1), ("x_t", 1), ("rk", 2), ("c_t", 2), ("kr", 2),
                    ("v", 3)):
        place(kind, g, PLAN[kind])
    return jobs


def misc_turns(jobs):
    assert len(jobs) % 2 == 0
    return {u: i % 2 for i, u in enumerate(sorted(jobs))}


LOOP_JOBS, EDGE_JOBS = misc_jobs(PLAN["proj"]), misc_jobs(EDGE_PROJ)
ACT_TAKES = ("x_t", "v", "at", "x1t")
ACT_READS = ACT_TAKES + ("c_t",)
LATE = ("at", "wo", "x1t", "lg", "rk")
NEXT = ("x_t", "c_t", "kr", "v")
JOBS = {"proj": 16, "ot": 8, "at": 4, "wo": 4, "x1t": 4, "lg": 4, "rk": 1, "x_t": 4, "c_t": 2,
        "kr": 3, "v": 4}

PROLOGUE = ([("x_t", 0), ("x_t", 1), ("c_t", 0), ("x_t", 2), ("x_t", 3), ("c_t", 1), ("kr", 0), ("proj", 0),
             ("kr", 1), ("proj", 1), ("kr", 2), ("proj", 2), ("proj", 3)]
            + [("v", n) for n in range(4)])
EPILOGUE = [("at", 0), ("at", 1), ("wo", 0), ("wo", 1), ("ot", 7), ("at", 2), ("at", 3), ("wo", 2), ("wo", 3),
            ("x1t", 0), ("x1t", 1), ("lg", 0), ("lg", 1), ("rk", 0),
            ("x1t", 2), ("x1t", 3), ("lg", 2), ("lg", 3), ("rk", 1)]


def tiles_of(h):
    return range(TILES) if h is None else range(h * TILES // 2, (h + 1) * TILES // 2)


def span(h):
    tiles = tiles_of(h)
    return slice(tiles[0], tiles[-1] + 1)


def part(b, h, per_batch=1):
    if h is None:
        return (b + 1) * per_batch
    return b * per_batch + (h + 1) * max(per_batch // 2, 1)


class Tally:

    def __init__(self):
        self.n, self.reg, self.start, self.per, self.at = 0, None, 0, 0, 0

    def value(self):
        return self.n if self.reg is None else (self.reg - self.start) * self.per + self.n

    def next(self):
        self.n += 1
        return self.value()

    def enter(self, reg, start, per):
        self.reg, self.start, self.per, self.at = reg, start, per, self.n

    def leave(self, iterations):
        assert self.n - self.at == self.per, f"{self.n - self.at} steps in the loop"
        self.n, self.reg = self.at + iterations * self.per, None


def layer(nc, x, w_dq, w_uq, w_qr, w_dkv, w_uk, w_uv, w_kr, w_o, wg, w1, b1, w2, b2,
          c_ident, c_sel, c_rope, c_rope_q, c_tri, c_iota, out, dbg=None):
    ctx = ExitStack()
    with ctx:
        def sem(name):
            return ctx.enter_context(nc.semaphore(name))

        psum_scope = ExitStack()

        def psum(name, shape, where=None):
            return (where or psum_scope).enter_context(nc.psum_tensor(name, shape, F32))

        x1_d = dbg[0] if dbg else nc.dram_tensor("x1_scratch", (TOKENS, D), F32).ap()
        xs_d = dbg[1] if dbg else nc.dram_tensor("expert_in_scratch", (SPARE + P, ROW), F32).ap()
        ys_d = nc.dram_tensor("expert_out_scratch", (DUMMY + TOPK * TOKENS, D), F32).ap()

        keep = ctx

        def sb(name, shape, dt=F32, where=None):
            return (where or keep).enter_context(nc.sbuf_tensor(name, shape, dt))

        ident = sb("ident", [P, P])
        iota = sb("iota", [P, MOE_TILES + 1])
        lane = iota[:, MOE_TILES:MOE_TILES + 1]
        load = sb("load", [P, TILES + 1, E])
        gate_all = sb("gate_all", [P, B, TOPK, TILES])
        table = sb("table", [P, 2, MOE_TILES], I32)
        tile_expert = sb("tile_expert", [P, MOE_TILES])
        tail_row = sb("tail_row", [P, E], I32)
        with ExitStack() as operands:
            stacks = sb("stacks", [P, 2, 4, 2, S], F32R, where=operands)
            home = sb("home", [P, 4, S], F32R, where=operands)
            x_t = sb("x_t", [P, DT, S], where=operands)
        w1_sb = sb("w1_sb", [P, E, DT, HID])
        w2_sb = sb("w2_sb", [P, E, FT, D])
        b1_sb = sb("b1_sb", [P, E, HID])
        b2_sb = sb("b2_sb", [P, E, D])

        s_first = sem("first_constants_loaded")
        s_const = sem("prologue_constants_loaded")
        s_later = sem("later_constants_loaded")
        s_xin = [sem(f"x_loaded{i}") for i in range(2)]
        s_stack = [sem(f"stack_loaded{i}") for i in range(2)]
        s_z = sem("z_loaded")
        s_x1st = sem("x1_stored")
        s_scat = sem("x1_scattered")
        s_zero = sem("weights_zeroed")
        s_pool0 = sem("constants_set")
        s_setup = sem("weights_padded")
        s_chi, s_clo = sem("latent_high_ready"), sem("query_latent_low_ready")
        s_cst = [sem(f"latents_stacked{c}") for c in range(2)]
        s_qk = sem("scores_ready")
        s_exp = sem("exp_ready")
        s_clip = sem("clip_ready")
        s_mask = sem("mask_ready")
        s_pv = sem("pv_done")
        s_acc = sem("acc_evacuated")
        ready = {k: sem(f"{k}_in_psum") for k in JOBS}
        taken = {k: sem(f"{k}_taken") for k in JOBS}
        s_hi, s_lo = sem("high_parts_ready"), sem("low_parts_ready")
        s_rstd = sem("rstd_ready")
        s_vcopy = sem("v_in_place")
        s_x1 = sem("x1_ready")
        s_stat = sem("ln_stats_ready")
        s_hot = sem("onehot_ready")
        s_dexp = sem("router_exp_in")
        s_eexp = sem("router_exp_out")
        s_posr = sem("pos_ready")
        s_zero_rows, s_spare = sem("zero_rows_ready"), sem("spare_rows_zeroed")
        s_w = sem("expert_weights_loaded")
        tails_ready, tables_ready = sem("tail_rows_ready"), sem("tile_tables_ready")
        tails_zero = sem("region_tails_zeroed")
        c_tab = sem("table_chain")
        c_main, c_late, c_pool = sem("dve_chain"), sem("dve_chain_late"), sem("pool_chain")

        attn_scope = ExitStack()
        A = attn_scope
        wdown = sb("wdown", [P, DT, P], where=A)
        wup = sb("wup", [P, 2, 2, GROUPS, 4, QUAD], F32R, where=A)
        wkr = sb("wkr", [P, DT, QUAD], where=A)
        wuv = sb("wuv", [P, 2, D], F32R, where=A)
        wo = sb("wo", [P, DT, D], where=A)
        wgate = sb("wgate", [P, DT, E], where=A)
        sel = sb("sel", [P, 4, P], where=A)
        tri = sb("tri", [P, 2, P], where=A)
        rope = sb("rope", [P, S], where=A)
        rope_q = sb("rope_q", [P, QUARTER], where=A)
        x_in = sb("x_in", [P, 2, 2, D], where=A)
        cq_t = sb("cq_t", [P, S], F32R, where=A)
        ckv_t = sb("ckv_t", [P, S], F32R, where=A)
        c_low = sb("c_low", [P, 2, CHUNK], F32R, where=A)
        kr_part = sb("kr_part", [P, QUARTER], where=A)
        kr = sb("kr", [P, S], where=A)
        full = sb("full", [P, 2, CHUNK], where=A)
        v_new = sb("v_new", [P, TILES, 4 * DH], where=A)
        v_aug = sb("v_aug", [P, TILES, HEADS, DH + 1], where=A)
        p_sb = sb("p_sb", [P, P_SLOTS, 2, CHUNK], where=A)
        up_whole = p_sb[:, 0].rearrange("p a (g j q) -> p a g j q", g=GROUPS, j=4)
        uv_whole = p_sb[:, 1, 0, 0:D]
        o_t = sb("o_t", [P, 2, CHUNK], where=A)
        recip = sb("recip", [P, 4, 4], where=A)
        attn = sb("attn", [P, TILES, D], where=A)
        attn_t = sb("attn_t", [P, 2, DT, 2 * P], where=A)
        z = sb("z", [P, TILES, ROW], where=A)
        token = sb("token", [P, TILES, 1], where=A)
        scratch = attn[:].rearrange("p t d -> p (t d)")

        def piece(at, *shape):
            view = scratch[:, at:at + int(np.prod(shape))]
            return view if len(shape) == 1 else view.rearrange("p (a b) -> p a b", a=shape[0])

        NT = MOE_TILES
        EXPERT, READ = range(2)
        cmp = piece(0, NT, E)
        over = piece(NT * E, E, TOKENS // P)
        tile_u, tile_r, t128 = (piece(NT * E + E * TOKENS // P + i * NT, NT) for i in range(3))
        n_tiles, ends, row_shift = (piece(NT * E + E * TOKENS // P + 3 * NT + i * E, E) for i in range(3))
        zero_rows = piece(NT * E + E * TOKENS // P + 3 * NT + 3 * E + TOKENS // P, ROW)
        thr = piece(NT * E + E * TOKENS // P + 3 * NT + 3 * E, TOKENS // P)
        stats = sb("stats", [P, TILES, 6], where=A)
        mv = sb("mv", [P, TILES, 2], where=A)
        rstd = sb("rstd", [P, TILES, 1], where=A)
        expo = sb("expo", [P, TILES, 1], where=A)
        lg = sb("lg", [P, TILES, E], where=A)
        top = sb("top", [P, TILES, E], where=A)
        topi = sb("topi", [P, TILES, E], U32, where=A)
        topf = sb("topf", [P, TILES, E], where=A)
        dlt = sb("dlt", [P, TILES, E], where=A)
        ex = sb("ex", [P, TILES, E], where=A)
        den = sb("den", [P, TILES, 1], where=A)
        hot = sb("hot", [P, TOPK, TILES, E], where=A)
        hots = sb("hots", [P, TILES, E], where=A)
        rk = sb("rk", [P, 2, TILES, E], where=A)
        where_ = sb("where_", [P, TILES, E], where=A)
        tmp = sb("tmp", [P, TOPK, TILES, E], where=A)
        posf = sb("posf", [P, TOPK, TILES], where=A)
        pos = sb("pos", [P, TOPK, TILES], U32, where=A)
        region0 = sb("region0", [P, E], where=A)

        scores = psum("scores", [P, S_SLOTS, 2, CHUNK])
        acc = psum("acc", [P, 2, CHUNK])
        misc_banks = psum("misc", [P, 2, CHUNK])

        def bank_for(kind, n, sequence):
            if isinstance(sequence, int):
                return misc_banks[:, sequence, :]
            i = sequence.index((kind, n)) % (2 * S_SLOTS)
            return scores[:, i // 2, i % 2, :]

        x_tiles = x.rearrange("b (n t p) d -> (b n) p t d", t=2, p=P)
        x_batch = x.rearrange("b (t p) d -> b p t d", p=P)
        x1_batch = x1_d.rearrange("(b t p) d -> b p t d", b=B, p=P)

        with nc.Block() as block:
            @block.sync
            def _(sp):
                n = 0

                def const(dst, src):
                    nonlocal n
                    n += 1
                    signal = (s_first if n <= FIRST_CONSTS else
                              s_const if n <= FIRST_CONSTS + PROLOGUE_CONSTS else s_later)
                    sp.dma_start(dst, src).then_inc(signal, 16)

                for m in range(2):
                    sp.dma_start(x_in[:, m], x_tiles[m]).then_inc(s_xin[m], 16)
                const(ident[:], c_ident)
                const(wdown[:, :, 0:LAT], w_dq.rearrange("(t p) n -> p t n", p=P))
                const(wdown[:, :, LAT:P], w_dkv.rearrange("(t p) n -> p t n", p=P))
                def x_in_load(b, m):
                    sp.wait_ge(ready["x_t"], b * 4 + m - 1)
                    sp.nop(nofuse=True)
                    sp.dma_start(x_in[:, m % 2], x_tiles[b * 4 + m]).then_inc(s_xin[m % 2], 16)

                def stack(b, g):
                    sp.wait_ge(s_lo, (b * GROUPS + g + 1) * 4)
                    sp.nop(nofuse=True)
                    if not (isinstance(b, int) and b * GROUPS + g < 2):
                        sp.wait_ge(s_qk, (b * GROUPS + g - 1) * PER_G)
                    for j in range(4):
                        for r in range(4):
                            q_part, k_part = r // 2, 2 + r % 2
                            sp.dma_start(stacks[QUAD * r:QUAD * (r + 1), g % 2, j].bitcast(F32),
                                         home[QUAD * j:QUAD * (j + 1), q_part:k_part + 1:k_part - q_part, :].bitcast(F32)
                                         ).then_inc(s_stack[j // 2], 16)

                def stack_latents(b, c):
                    sp.wait_ge(s_clo, b * 2 + c + 1)
                    sp.wait_ge(taken["c_t"], b * 2 + c + 1)
                    sp.nop(nofuse=True)
                    cs = slice(c * CHUNK, (c + 1) * CHUNK)
                    sp.dma_start(cq_t[LAT:P, cs].bitcast(F32), c_low[0:LAT, c].bitcast(F32)).then_inc(s_cst[c], 16)
                    sp.dma_start(ckv_t[0:LAT, cs].bitcast(F32), c_low[LAT:P, c].bitcast(F32)).then_inc(s_cst[c], 16)

                def body(b, late, nxt):
                    if late:
                        if not (isinstance(b, int) and b < 2):
                            sp.wait_ge(s_x1st, 16 * (b - 1))
                            sp.nop(nofuse=True)
                            sp.wait_ge(s_scat, 256 * (b - 1))
                        sp.nop(nofuse=True)
                        sp.dma_start(z[:, :, 0:D], x_batch[b - 1]).then_inc(s_z, 16)
                    stack(b, 1)
                    if nxt:
                        x_in_load(b + 1, 0)
                        x_in_load(b + 1, 1)
                    stack(b, 2)
                    if nxt:
                        x_in_load(b + 1, 2)
                        x_in_load(b + 1, 3)
                    stack(b, 3)
                    if late:
                        sp.wait_ge(s_x1, 8 * b)
                        sp.nop(nofuse=True)
                        sp.dma_start(x1_batch[b - 1], z[:, :, 0:D]).then_inc(s_x1st, 16)
                    if nxt:
                        stack_latents(b + 1, 0)
                        stack_latents(b + 1, 1)
                        stack(b + 1, 0)

                sp.wait_ge(s_zero, 2)
                for rows in (slice(0, LAT), slice(LAT, P)):
                    const(up_whole[rows, 0, :, :, 0:DH].rearrange("p g j d -> p (g j) d"),
                          w_uq.rearrange("k (h d) -> k h d", d=DH))
                    const(up_whole[rows, 0, :, :, DH:DH + DR].rearrange("p g j d -> p (g j) d"),
                          w_qr.rearrange("k (h d) -> k h d", d=DR))
                    const(up_whole[rows, 1, :, :, 0:DH].rearrange("p g j d -> p (g j) d"),
                          w_uk.rearrange("k (h d) -> k h d", d=DH))
                    const(uv_whole[rows], w_uv)
                x_in_load(0, 2)
                x_in_load(0, 3)
                const(wkr[:, :, DH:DH + DR], w_kr.rearrange("(t p) n -> p t n", p=P))
                const(rope_q[:], c_rope_q)
                const(sel[:], c_sel)
                const(rope[:], c_rope)
                stack_latents(0, 0)
                const(wo[:], w_o.rearrange("(t p) n -> p t n", p=P))
                const(wgate[:], wg.rearrange("(t p) n -> p t n", p=P))
                const(tri[:], c_tri.rearrange("a p n -> p a n"))
                const(iota[:], c_iota)
                assert n == FIRST_CONSTS + PROLOGUE_CONSTS + LATER_CONSTS
                stack_latents(0, 1)
                stack(0, 0)
                body(0, False, True)
                with sp.Fori(1, B - 1) as b:
                    body(b, True, True)
                body(B - 1, True, False)
                sp.wait_ge(s_x1st, 16 * (B - 1))
                sp.wait_ge(s_scat, 256 * (B - 1))
                sp.dma_start(z[:, :, 0:D], x_batch[B - 1]).then_inc(s_z, 16)
                sp.wait_ge(s_qk, (B - 1) * NU + 3 * PER_G)
                for e in range(E):
                    sp.dma_start(w1_sb[:, e], w1[e].rearrange("(t p) n -> p t n", p=P)).then_inc(s_w, 16)
                sp.wait_ge(ready["kr"], 3 * B)
                sp.dma_start(b2_sb[:], b2.partition_broadcast(P)).then_inc(s_w, 16)
                for i in range(2):
                    sp.wait_ge(s_stack[i], B * GROUPS * STACK_DMAS * 16)
                sp.dma_start(b1_sb[:], b1.partition_broadcast(P)).then_inc(s_w, 16)
                sp.wait_ge(s_qk, B * NU)
                for e in range(E):
                    sp.dma_start(w2_sb[:, e], w2[e].rearrange("(t p) n -> p t n", p=P)).then_inc(s_w, 16)
                sp.wait_ge(s_x1, 8 * B)
                sp.dma_start(x1_batch[B - 1], z[:, :, 0:D]).then_inc(s_x1st, 16)
                sp.wait_ge(s_zero_rows, 1)
                sp.dma_start(xs_d[SPARE:SPARE + P, :], zero_rows).then_inc(s_spare, 16)
                sp.wait_ge(tails_ready, 1)
                for e in range(E):
                    row = sp.value_load(tail_row[0:1, e:e + 1], min_val=0, max_val=SPARE - P)
                    sp.dma_start(xs_d[bass.ds(row, P), :], zero_rows).then_inc(tails_zero, 16)
                sp.wait_ge(tails_zero, 16 * E)
                sp.wait_ge(s_spare, 16)
                sp.wait_ge(s_w, 16 * WEIGHT_LOADS)
                sp.wait_ge(s_x1st, 16 * B)
                sp.wait_ge(s_scat, 256 * B)

            @block.tensor
            def _(pe):
                last = {}

                def job(kind, n, b, sequence=None):
                    misc = bank_for(kind, n, sequence)
                    key = -1 - sequence if isinstance(sequence, int) else sequence.index((kind, n)) % (2 * S_SLOTS)
                    if key in last:
                        pe.wait_ge(*last[key])
                    last[key] = taken[kind], b * JOBS[kind] + n + 1
                    if kind == "x_t":
                        pe.wait_ge(s_xin[n % 2], (b * 2 + n // 2 + 1) * 16)
                        for dt in range(DT):
                            for t in range(2):
                                mm = nc.tensor.transpose(misc[:, (dt * 2 + t) * P:(dt * 2 + t + 1) * P],
                                                         x_in[:, n % 2, t, dt * P:(dt + 1) * P], ident[:])
                    elif kind == "c_t":
                        pe.wait_ge(taken["x_t"], b * 4 + 2 * n + 2)
                        for dt in range(DT):
                            mm = nc.tensor.matmul(misc, wdown[:, dt, :], x_t[:, dt, n * CHUNK:(n + 1) * CHUNK],
                                                  start=dt == 0, stop=dt == DT - 1)
                    elif kind == "kr" and n == 0:
                        pe.wait_ge(taken["x_t"], b * 4 + 4)
                        for j in range(4):
                            for dt in range(DT):
                                mm = nc.tensor.matmul(misc[QUAD * j:QUAD * (j + 1), 0:QUARTER], wkr[:, dt, :],
                                                      x_t[:, dt, j * QUARTER:(j + 1) * QUARTER],
                                                      start=dt == 0, stop=dt == DT - 1)
                    elif kind == "kr":
                        pe.wait_ge(taken["kr"], b * 3 + 1)
                        for i in range(2):
                            mm = nc.tensor.matmul(misc[:, i * QUARTER:(i + 1) * QUARTER],
                                                  sel[:, 2 * (n - 1) + i, :], kr_part[:], start=True, stop=True)
                    elif kind == "v":
                        pe.wait_ge(s_cst[n // 2], (b + 1) * 32)
                        for t in range(2):
                            kt = 2 * n + t
                            for half in range(2):
                                mm = nc.tensor.matmul(misc[:, t * D:(t + 1) * D], ckv_t[:, kt * P:(kt + 1) * P],
                                                      wuv[:, half, :], start=half == 0, stop=half == 1)
                    elif kind == "proj":
                        g, c, is_k = n // 4, (n % 4) // 2, n % 2
                        pe.wait_ge(s_cst[c], (b + 1) * 32)
                        for half in range(2):
                            mm = nc.tensor.matmul(misc, wup[:, is_k, half, g].rearrange("p j d -> p (j d)"),
                                                  (ckv_t if is_k else cq_t)[:, c * CHUNK:(c + 1) * CHUNK],
                                                  start=half == 0, stop=half == 1)
                    elif kind == "ot":
                        pe.wait_ge(s_acc, b * 8 + n + 1)
                        for i in range(4):
                            mm = nc.tensor.transpose(misc[:, i * P:(i + 1) * P],
                                                     o_t[:, n % 2, i * P:(i + 1) * P], ident[:])
                    elif kind == "at":
                        pe.wait_ge(taken["ot"], b * 8 + (7 if n < 2 else 8))
                        for dt in range(DT):
                            for t in range(2):
                                mm = nc.tensor.transpose(misc[:, (dt * 2 + t) * P:(dt * 2 + t + 1) * P],
                                                         attn[:, 2 * n + t, dt * P:(dt + 1) * P], ident[:])
                    elif kind == "wo":
                        pe.wait_ge(taken["at"], b * 4 + n + 1)
                        for t in range(2):
                            for dt in range(DT):
                                mm = nc.tensor.matmul(misc[:, t * D:(t + 1) * D],
                                                      attn_t[:, n % 2, dt, t * P:(t + 1) * P], wo[:, dt, :],
                                                      start=dt == 0, stop=dt == DT - 1)
                    elif kind == "x1t":
                        pe.wait_ge(s_x1, b * 8 + 2 * n + 2)
                        for dt in range(DT):
                            for t in range(2):
                                mm = nc.tensor.transpose(misc[:, (dt * 2 + t) * P:(dt * 2 + t + 1) * P],
                                                         z[:, 2 * n + t, dt * P:(dt + 1) * P], ident[:])
                    elif kind == "lg":
                        pe.wait_ge(taken["x1t"], b * 4 + n + 1)
                        for t in range(2):
                            for dt in range(DT):
                                mm = nc.tensor.matmul(misc[:, t * E:(t + 1) * E],
                                                      attn_t[:, n % 2, dt, t * P:(t + 1) * P], wgate[:, dt, :],
                                                      start=dt == 0, stop=dt == DT - 1)
                    elif kind == "rk":
                        h = None if isinstance(sequence, int) else n
                        tn = len(tiles_of(h))
                        pe.wait_ge(s_hot, part(b, h))
                        for a in range(2):
                            mm = nc.tensor.matmul(misc[:, a * tn * E:(a + 1) * tn * E], tri[:, a, :],
                                                  hots[:, span(h), :].rearrange("p t e -> p (t e)"),
                                                  start=True, stop=True)
                    mm.then_inc(ready[kind], 1)

                def qk(b, u):
                    g, c, kt, hp = UNITS[u]
                    o = offset_in_chunk(c, kt)
                    if u % PER_G < 2:
                        pe.wait_ge(s_stack[hp], (b * GROUPS + g + 1) * STACK_DMAS * 16)
                    if not (isinstance(b, int) and b == 0 and u < S_SLOTS):
                        pe.wait_ge(s_exp, b * NU + u - S_SLOTS + 1)
                    for a in range(2):
                        j = 2 * hp + a
                        mm = nc.tensor.matmul(scores[:, u % S_SLOTS, a, o:CHUNK],
                                              stacks[:, g % 2, j, 1, kt * P:(kt + 1) * P],
                                              stacks[:, g % 2, j, 0, c * CHUNK + o:(c + 1) * CHUNK],
                                              start=True, stop=True)
                    mm.then_inc(s_qk, 1)

                def pv(b, u):
                    g, c, kt, hp = UNITS[u]
                    o = offset_in_chunk(c, kt)
                    if u == 0:
                        pe.wait_ge(taken["v"], (b + 1) * 4)
                    if u == (GROUPS - 1) * PER_G:
                        pe.wait_ge(s_vcopy, b + 1)
                    if kt == 0 and not (isinstance(b, int) and b == 0 and g == 0):
                        pe.wait_ge(s_acc, b * 8 + 2 * g + c - 1)
                    if is_diag(u):
                        pe.wait_ge(s_mask, b * N_MASK + MASKS_BEFORE[u] + 2)
                    else:
                        pe.wait_ge(s_clip, b * NU + u + 2)
                    for j in range(4):
                        mm = nc.tensor.matmul(acc[QUAD * j:QUAD * j + DH + 1, (2 * g + c) % 2, o:CHUNK],
                                              v_aug[:, kt, 4 * g + j, :],
                                              p_sb[:, (u + j // 2) % P_SLOTS, j % 2, o:CHUNK],
                                              start=kt == 0, stop=kt == 4 * c + 3)
                    mm.then_inc(s_pv, 1)

                def body(b, late, nxt):
                    jobs = EDGE_JOBS if isinstance(b, int) else LOOP_JOBS
                    turns = misc_turns(jobs)
                    for u in range(NU):
                        qk(b, u)
                        if u in jobs:
                            kind, n = jobs[u]
                            if kind == "proj":
                                if u < 3 * PER_G:
                                    job("proj", (u // PER_G + 1) * 4 + n, b, turns[u])
                                elif nxt:
                                    job("proj", n, b + 1, turns[u])
                            elif kind == "ot" and n == 7:
                                if late:
                                    job("ot", 7, b - 1, turns[u])
                            elif kind in LATE:
                                if late:
                                    job(kind, n, b - 1, turns[u])
                            elif kind in NEXT:
                                if nxt:
                                    job(kind, n, b + 1, turns[u])
                            else:
                                job("ot", n, b, turns[u])
                        if u % 2 == 0 and u >= LAG:
                            pv(b, u - LAG)
                        elif u % 2 == 0 and late:
                            pv(b - 1, NU - LAG + u)

                pe.wait_ge(s_first, 16 * FIRST_CONSTS)
                for kind, n in PROLOGUE:
                    if (kind, n) == ("kr", 0):
                        pe.wait_ge(s_const, 16 * PROLOGUE_CONSTS)
                        pe.wait_ge(s_setup, 5)
                    if (kind, n) == ("proj", 0):
                        pe.wait_ge(s_setup, 7)
                    job(kind, n, 0, PROLOGUE)
                pe.wait_ge(s_later, 16 * LATER_CONSTS)
                for kind in ("proj", "v"):
                    pe.wait_ge(taken[kind], 4)
                last.clear()

                def last_two(b):
                    assert [LOOP_JOBS[u] for u in sorted(LOOP_JOBS)[-2:]] == [("v", 3), ("ot", 6)]
                    last[-1] = taken["v"], (b + 1) * 4
                    last[-2] = taken["ot"], b * 8 - 1

                body(0, False, True)
                with pe.Fori(1, B - 1) as b:
                    last_two(b)
                    body(b, True, True)
                last_two(B - 1)
                body(B - 1, True, False)
                pe.wait_ge(s_exp, B * NU)
                last = {key: value for key, value in last.items() if key < 0}
                for kind, n in EPILOGUE:
                    if (kind, n) in (("at", 0), ("wo", 0), ("wo", 1)):
                        pv(B - 1, NU - LAG + 2 * (("at", 0), ("wo", 0), ("wo", 1)).index((kind, n)))
                    job(kind, n, B - 1, EPILOGUE)

            @block.scalar
            def _(act):
                def exp(b, u):
                    _, c, kt, _ = UNITS[u]
                    o = offset_in_chunk(c, kt)
                    act.wait_ge(s_qk, b * NU + u + 1)
                    if not (isinstance(b, int) and b == 0 and u < P_SLOTS):
                        act.wait_ge(s_pv, b * (NU // 2) + (u - P_SLOTS) // 2 + 1)
                    nc.scalar.activation(p_sb[:, u % P_SLOTS, :, o:CHUNK], scores[:, u % S_SLOTS, :, o:CHUNK],
                                         ACT.Exp, scale=SCALE).then_inc(s_exp, 1)

                def evac(kind, n, b, sequence=None):
                    act.wait_ge(ready[kind], b * JOBS[kind] + n + 1)
                    misc = bank_for(kind, n, sequence)
                    m2 = misc.rearrange("p (a n) -> p a n", a=2)
                    if kind == "x_t":
                        if not (isinstance(b, int) and b == 0):
                            act.wait_ge(ready["kr"], b * 3)
                        to = x_t[:, :, n * 2 * P:(n + 1) * 2 * P]
                    elif kind == "c_t":
                        if not (isinstance(b, int) and b == 0):
                            act.wait_ge(ready["proj"], b * 16)
                            act.wait_ge(ready["v"], b * 4)
                        for to, rows in ((cq_t, slice(0, LAT)), (ckv_t, slice(LAT, P))):
                            nc.scalar.copy(to[rows, n * CHUNK:(n + 1) * CHUNK], misc[rows]).then_inc(s_chi, 1)
                        return
                    elif kind == "v":
                        if not (isinstance(b, int) and b == 0):
                            act.wait_ge(s_vcopy, b)
                            act.wait_ge(s_pv, (b - 1) * (NU // 2) + (GROUPS - 1) * PER_G // 2)
                        last_g = (GROUPS - 1) * 4
                        vh = m2.rearrange("p t (h d) -> p t h d", d=DH)
                        nc.scalar.copy(v_aug[:, 2 * n:2 * n + 2, 0:last_g, 0:DH], vh[:, :, 0:last_g, :])
                        to, m2 = v_new[:, 2 * n:2 * n + 2, :], m2[:, :, last_g * DH:]
                    elif kind == "at":
                        if n >= 2:
                            act.wait_ge(ready["wo"], b * 4 + n - 1)
                        else:
                            act.wait_ge(ready["ot"], b * 8 + 7)
                        to = attn_t[:, n % 2, :, :]
                    elif kind == "x1t":
                        if n >= 2:
                            act.wait_ge(ready["lg"], b * 4 + n - 1)
                        to = attn_t[:, n % 2, :, :]
                    nc.scalar.copy(to, m2).then_inc(taken[kind], 1)

                def acc_out(b, n):
                    units = PER_G * (n // 2) + (C0 if n % 2 == 0 else PER_G)
                    act.wait_ge(s_pv, (b * NU + units) // 2 if isinstance(b, int) else b * (NU // 2) + units // 2)
                    if not (isinstance(b, int) and b == 0 and n < 2):
                        act.wait_ge(ready["ot"], b * 8 + n - 1)
                    nc.scalar.copy(o_t[:, n % 2, :], acc[:, n % 2, :]).then_inc(s_acc, 1)

                def router_exp(b, h=None):
                    act.wait_ge(s_dexp, part(b, h))
                    nc.scalar.activation(ex[:, span(h)].rearrange("p t e -> p (t e)"),
                                         dlt[:, span(h)].rearrange("p t e -> p (t e)"), ACT.Exp).then_inc(s_eexp, 1)

                def body(b, late, nxt):
                    jobs = EDGE_JOBS if isinstance(b, int) else LOOP_JOBS
                    turns = misc_turns(jobs)
                    for u in range(NU):
                        if u in jobs and jobs[u][0] in ACT_READS:
                            kind, n = jobs[u]
                            if kind in LATE and late:
                                evac(kind, n, b - 1, turns[u])
                            if kind in NEXT and nxt:
                                evac(kind, n, b + 1, turns[u])
                        if u == EXP_AT and late:
                            router_exp(b - 1)
                        if u % PER_G == C0 - 2 + LAG:
                            acc_out(b, 2 * (u // PER_G))
                        if u % PER_G == LAG - 2:
                            if u >= PER_G:
                                acc_out(b, 2 * (u // PER_G) - 1)
                            elif late:
                                acc_out(b - 1, 7)
                        exp(b, u)

                for kind, n in PROLOGUE:
                    if kind in ACT_READS:
                        evac(kind, n, 0, PROLOGUE)
                body(0, False, True)
                with act.Fori(1, B - 1) as b:
                    body(b, True, True)
                body(B - 1, True, False)
                for kind, n in EPILOGUE:
                    if kind in ACT_TAKES:
                        evac(kind, n, B - 1, EPILOGUE)
                    if (kind, n) == ("wo", 0):
                        acc_out(B - 1, 7)
                    if kind == "rk":
                        router_exp(B - 1, n)

            @block.vector
            def _(dve):
                main, late_t = Tally(), Tally()

                def evac(kind, n, b, sequence=None):
                    dve.wait_ge(ready[kind], b * JOBS[kind] + n + 1)
                    misc = bank_for(kind, n, sequence)
                    m2 = misc.rearrange("p (a n) -> p a n", a=2)
                    if kind == "c_t":
                        cs = slice(n * CHUNK, (n + 1) * CHUNK)
                        dve.wait_ge(s_chi, (b * 2 + n + 1) * 2)
                        if not (isinstance(b, int) and b == 0):
                            dve.wait_ge(s_cst[n], b * 32)
                        for of, rows, signal in ((cq_t, slice(0, LAT), s_clo), (ckv_t, slice(LAT, P), taken[kind])):
                            nc.vector.tensor_tensor(c_low[rows, n], misc[rows], of[rows, cs].bitcast(F32),
                                                    ALU.subtract).then_inc(signal, 1)
                    elif kind == "kr" and n == 0:
                        nc.vector.tensor_tensor(kr_part[:], misc[:, 0:QUARTER], rope_q[:], ALU.mult
                                                ).then_inc(taken[kind], 1)
                    elif kind == "kr":
                        nc.vector.tensor_copy(kr[:, (n - 1) * CHUNK:n * CHUNK], misc).then_inc(taken[kind], 1)
                    elif kind == "proj":
                        g, c, is_k = n // 4, (n % 4) // 2, n % 2
                        if not (isinstance(b, int) and b == 0 and n < 2):
                            dve.wait_ge(s_lo, b * 16 + n - 1)
                        cs = slice(c * CHUNK, (c + 1) * CHUNK)
                        if is_k:
                            dve.wait_ge(taken["kr"], b * 3 + c + 2)
                            nc.vector.tensor_tensor(full[:, 1, :], misc, kr[:, cs], ALU.add).then_inc(taken[kind], 1)
                        else:
                            nc.vector.tensor_tensor(full[:, 0, :], misc, rope[:, cs], ALU.mult).then_inc(taken[kind], 1)
                        if n % 4 == 0 and not (isinstance(b, int) and b * 4 + g == 0):
                            for i in range(2):
                                dve.wait_ge(s_stack[i], (b * GROUPS + g) * STACK_DMAS * 16)
                        dve.wait_ge(taken[kind], b * 16 + n + 1)
                        nc.vector.tensor_copy(home[:, 2 * is_k, cs], full[:, is_k, :]).then_inc(s_hi, 1)
                    elif kind == "ot":
                        g, c = n // 2, n % 2
                        m4 = misc.rearrange("p (i j r) -> p i j r", i=4, j=4)
                        if not (isinstance(b, int) and b == 0):
                            dve.wait_ge(ready["at"], (b - 1) * 4 + 2 * c + 2)
                        nc.vector.reciprocal(recip[:], m4[:, :, :, DH]).then_inc(c_main, 1)
                        dve.wait_ge(c_main, main.next())
                        nc.vector.tensor_tensor(
                            attn[:, 4 * c:4 * c + 4, g * 4 * DH:(g + 1) * 4 * DH].rearrange("p i (j d) -> p i j d", j=4),
                            m4[:, :, :, 0:DH], recip[:].unsqueeze(3).to_broadcast([P, 4, 4, DH]), ALU.mult
                        ).then_inc(taken[kind], 1)
                    elif kind == "wo":
                        dve.wait_ge(s_z, (b + 1) * 16)
                        zz = z[:, 2 * n:2 * n + 2, 0:D]
                        nc.vector.tensor_tensor(zz, m2, zz, ALU.add).then_inc(taken[kind], 1)
                        dve.wait_ge(taken[kind], b * 4 + n + 1)
                        for t in range(2 * n, 2 * n + 2):
                            nc.vector.bn_stats(stats[:, t, :], z[:, t, 0:D]).then_inc(c_late, 1)
                            v = late_t.next()
                        dve.wait_ge(c_late, v)
                        dve.nop(nofuse=True)
                        for t in range(2 * n, 2 * n + 2):
                            nc.vector.bn_aggr(mv[:, t, :], stats[:, t, :]).then_inc(s_stat, 1)
                    elif kind == "lg":
                        nc.vector.tensor_copy(lg[:, 2 * n:2 * n + 2, :],
                                              misc[:, 0:2 * E].rearrange("p (t e) -> p t e", t=2)
                                              ).then_inc(taken[kind], 1)
                    elif kind == "rk":
                        h = None if isinstance(sequence, int) else n
                        tn = len(tiles_of(h))
                        nc.vector.tensor_copy(rk[:, :, span(h)], misc[:, 0:2 * tn * E].rearrange(
                            "p (a t e) -> p a t e", a=2, t=tn)).then_inc(taken[kind], 1)

                def step(ins):
                    ins.then_inc(c_late, 1)
                    dve.wait_ge(c_late, late_t.next())

                def largest(b, h=None):
                    ts, tiles = span(h), tiles_of(h)
                    dve.wait_ge(taken["lg"], part(b, h, 4))
                    if not (isinstance(b, int) and b == 0):
                        dve.wait_ge(s_eexp, b)
                        dve.wait_ge(ready["rk"], b)
                    dve.nop(nofuse=True)
                    for t in tiles:
                        nc.vector.max(top[:, t, :], lg[:, t, :]).then_inc(c_late, 1)
                        v = late_t.next()
                    dve.wait_ge(c_late, v)
                    dve.nop(nofuse=True)
                    for t in tiles:
                        nc.vector.max_index(topi[:, t, :], top[:, t, :], lg[:, t, :]).then_inc(c_late, 1)
                        v = late_t.next()
                    return v

                def experts_of(b, h=None, before=0):
                    ts, tiles = span(h), tiles_of(h)
                    sh = [P, len(tiles), E]
                    nc.vector.tensor_tensor(dlt[:, ts], top[:, ts], top[:, ts, 0:1].to_broadcast(sh),
                                            ALU.subtract).then_inc(s_dexp, 1)
                    dve.wait_ge(c_late, before)
                    step(nc.vector.tensor_copy(topf[:, ts, 0:TOPK], topi[:, ts, 0:TOPK]))
                    for k in range(TOPK):
                        nc.vector.tensor_tensor(hot[:, k, ts], iota[:, 0:E].unsqueeze(1).to_broadcast(sh),
                                                topf[:, ts, k:k + 1].to_broadcast(sh),
                                                ALU.is_equal).then_inc(c_late, 1)
                        v = late_t.next()
                    dve.wait_ge(c_late, v)
                    nc.vector.tensor_tensor(hots[:, ts], hot[:, 0, ts], hot[:, 1, ts], ALU.add).then_inc(s_hot, 1)

                def gates_of(b, h=None):
                    ts = span(h)
                    dve.wait_ge(s_eexp, part(b, h))
                    step(nc.vector.tensor_reduce(den[:, ts].rearrange("p t o -> p (t o)"), ex[:, ts], AX.X, ALU.add))
                    step(nc.vector.reciprocal(den[:, ts], den[:, ts]))
                    step(nc.vector.tensor_tensor(gate_all[:, b, :, ts].rearrange("p k t -> p t k"), ex[:, ts, 0:TOPK],
                                                 den[:, ts].to_broadcast([P, len(tiles_of(h)), TOPK]), ALU.mult))

                def loads_before(b, tiles, h=None):
                    dve.wait_ge(taken["rk"], part(b, h))
                    for t in tiles:
                        step(nc.vector.tensor_tensor(load[:, t + 1, :], load[:, t, :], rk[:, 1, t, :], ALU.add))

                def positions(b, h=None):
                    ts, tiles = span(h), tiles_of(h)
                    step(nc.vector.tensor_tensor(where_[:, ts], rk[:, 0, ts], load[:, ts, :], ALU.add))
                    step(nc.vector.tensor_tensor(where_[:, ts], where_[:, ts],
                                                 region0[:].unsqueeze(1).to_broadcast([P, len(tiles), E]), ALU.add))
                    for k in range(TOPK):
                        step(nc.vector.tensor_tensor(tmp[:, k, ts], where_[:, ts], hot[:, k, ts], ALU.mult))
                        step(nc.vector.tensor_reduce(posf[:, k, ts], tmp[:, k, ts], AX.X, ALU.add))

                def send_off(b, h=None):
                    ts = span(h)
                    step(nc.vector.tensor_scalar(token[:, ts], token[:, ts], float(S), None, ALU.add))
                    if not (isinstance(b, int) and b == 0):
                        dve.wait_ge(s_scat, b * 256)
                    dve.nop(nofuse=True)
                    step(nc.vector.tensor_copy(z[:, ts, D:D + 1], token[:, ts]))
                    step(nc.vector.tensor_copy(z[:, ts, D + 1:D + 2], topf[:, ts, 0:1]))
                    nc.vector.tensor_copy(pos[:, :, ts], posf[:, :, ts]).then_inc(s_posr, 1)
                    if h != 0:
                        step(nc.vector.tensor_copy(load[:, 0, :], load[:, TILES, :]))

                def norm(b, t, h=None):
                    if t == tiles_of(h)[0]:
                        dve.wait_ge(s_rstd, part(b, h))
                    nc.vector.tensor_scalar(z[:, t, 0:D], z[:, t, 0:D], mv[:, t, 0:1], rstd[:, t, :],
                                            ALU.subtract, ALU.mult).then_inc(s_x1, 1)

                def clip(b, u):
                    _, c, kt, _ = UNITS[u]
                    o = offset_in_chunk(c, kt)
                    dve.wait_ge(s_exp, b * NU + u + 1)
                    pp = p_sb[:, u % P_SLOTS, :, o:CHUNK]
                    nc.vector.tensor_scalar(pp, pp, EXP_LO, EXP_HI, ALU.max, ALU.min).then_inc(s_clip, 1)

                def v_place(b):
                    if not (isinstance(b, int) and b == 0):
                        dve.wait_ge(s_pv, b * (NU // 2))
                    dve.wait_ge(taken["v"], (b + 1) * 4)
                    nc.vector.tensor_copy(v_aug[:, :, (GROUPS - 1) * 4:, 0:DH],
                                          v_new[:].rearrange("p t (h d) -> p t h d", d=DH)).then_inc(s_vcopy, 1)

                def body(b, late, nxt):
                    jobs = EDGE_JOBS if isinstance(b, int) else LOOP_JOBS
                    turns = misc_turns(jobs)
                    for u in range(NU):
                        if u in jobs:
                            kind, n = jobs[u]
                            if kind == "proj":
                                if u < 3 * PER_G:
                                    evac("proj", (u // PER_G + 1) * 4 + n, b, turns[u])
                                elif nxt:
                                    evac("proj", n, b + 1, turns[u])
                            elif kind == "ot" and n == 7:
                                if late:
                                    evac("ot", 7, b - 1, turns[u])
                            elif kind in ACT_TAKES:
                                pass
                            elif kind in LATE:
                                if late:
                                    evac(kind, n, b - 1, turns[u])
                            elif kind in NEXT:
                                if nxt:
                                    evac(kind, n, b + 1, turns[u])
                            else:
                                evac("ot", n, b, turns[u])
                        if late and NORM_AT <= u < NORM_AT + TILES:
                            norm(b - 1, u - NORM_AT)
                        if late and u == ROUTE_AT:
                            found = largest(b - 1)
                        if late and u == ROUTE_AT + 1:
                            experts_of(b - 1, None, found)
                        if late and u == GATES_AT:
                            gates_of(b - 1)
                        if late and u in (POS_AT, POS_AT + 1):
                            loads_before(b - 1, tiles_of(u - POS_AT))
                        if late and u == POS_AT + 2:
                            positions(b - 1)
                        if late and u == POS_AT + 3:
                            send_off(b - 1)
                        clip(b, u)
                        if u == LAG - 2:
                            v_place(b)

                def tables():
                    counts = load[:, 0, :]
                    steps = Tally()

                    def step(ins):
                        ins.then_inc(c_tab, 1)
                        dve.wait_ge(c_tab, steps.next())

                    nc.vector.memset(zero_rows, 0.0).then_inc(s_zero_rows, 1)
                    step(nc.vector.tensor_scalar(row_shift, iota[:, 0:E], float(REGION), None, ALU.mult))
                    nc.vector.tensor_tensor(tail_row[:], counts, row_shift, ALU.add).then_inc(tails_ready, 1)
                    step(nc.vector.tensor_scalar(thr, iota[:, 0:TOKENS // P], float(P), None, ALU.mult))
                    sh = [P, E, TOKENS // P]
                    step(nc.vector.tensor_tensor(over, counts.unsqueeze(2).to_broadcast(sh),
                                                 thr.unsqueeze(1).to_broadcast(sh), ALU.is_gt))
                    step(nc.vector.tensor_reduce(n_tiles, over, AX.X, ALU.add))
                    step(nc.vector.tensor_copy(ends, n_tiles))
                    for e in range(1, E):
                        step(nc.vector.tensor_tensor(ends[:, e:e + 1], ends[:, e:e + 1], ends[:, e - 1:e], ALU.add))
                    sh = [P, NT, E]
                    ends_b = ends.unsqueeze(1).to_broadcast(sh)
                    step(nc.vector.tensor_tensor(cmp, iota[:, 0:NT].unsqueeze(2).to_broadcast(sh), ends_b, ALU.is_ge))
                    step(nc.vector.tensor_reduce(tile_expert[:], cmp, AX.X, ALU.add))
                    step(nc.vector.tensor_tensor(ends, ends, n_tiles, ALU.subtract))
                    step(nc.vector.tensor_scalar(ends, ends, float(P), None, ALU.mult))
                    step(nc.vector.tensor_tensor(row_shift, row_shift, ends, ALU.subtract))
                    step(nc.vector.tensor_tensor(cmp, iota[:, 0:E].unsqueeze(1).to_broadcast(sh),
                                                 tile_expert[:].unsqueeze(2).to_broadcast(sh), ALU.is_equal))
                    step(nc.vector.tensor_tensor(cmp, cmp, row_shift.unsqueeze(1).to_broadcast(sh), ALU.mult))
                    step(nc.vector.tensor_reduce(tile_r, cmp, AX.X, ALU.add))
                    step(nc.vector.tensor_scalar(t128, iota[:, 0:NT], float(P), None, ALU.mult))
                    step(nc.vector.tensor_tensor(tile_r, tile_r, t128, ALU.add))
                    step(nc.vector.tensor_scalar(tile_u, tile_expert[:], float(E), None, ALU.is_ge))
                    step(nc.vector.tensor_scalar(tile_expert[:], tile_expert[:], float(E - 1), None, ALU.min))
                    step(nc.vector.tensor_copy(table[:, EXPERT, :], tile_expert[:]))
                    step(nc.vector.scalar_tensor_tensor(tile_r, tile_u, float(SPARE), tile_r, ALU.mult, ALU.add))
                    step(nc.vector.tensor_tensor(t128, t128, tile_u, ALU.mult))
                    nc.vector.tensor_tensor(table[:, READ, :], tile_r, t128, ALU.subtract).then_inc(tables_ready, 1)

                nc.vector.memset(acc[:], 0.0).then_inc(s_setup, 1)
                evac("c_t", 0, 0, PROLOGUE)
                dve.wait_ge(s_pool0, 3)
                dve.wait_ge(s_const, 16 * PROLOGUE_CONSTS)
                for to, of in ((0, 1), (1, 0)):
                    nc.vector.tensor_copy(up_whole[:, 0, :, :, DH + DR + to:QUAD:2],
                                          up_whole[:, 0, :, :, DH + of:DH + DR:2]).then_inc(s_setup, 1)
                    nc.vector.tensor_copy(wkr[:, :, DH + DR + to:QUAD:2],
                                          wkr[:, :, DH + of:DH + DR:2]).then_inc(s_setup, 1)
                dve.wait_ge(s_setup, 5)
                up = up_whole.rearrange("p a g j q -> p a (g j q)")
                nc.vector.tensor_copy(wup[:, :, 0].rearrange("p a g j q -> p a (g j q)"), up).then_inc(c_main, 1)
                main.next()
                nc.vector.tensor_copy(wuv[:, 0], uv_whole).then_inc(c_main, 1)
                dve.wait_ge(c_main, main.next())
                nc.vector.tensor_tensor(wup[:, :, 1].rearrange("p a g j q -> p a (g j q)"), up,
                                        wup[:, :, 0].rearrange("p a g j q -> p a (g j q)").bitcast(F32),
                                        ALU.subtract).then_inc(s_setup, 1)
                nc.vector.tensor_tensor(wuv[:, 1], uv_whole, wuv[:, 0].bitcast(F32), ALU.subtract
                                        ).then_inc(s_setup, 1)
                for kind, n in PROLOGUE:
                    if kind not in ACT_TAKES and (kind, n) != ("c_t", 0):
                        evac(kind, n, 0, PROLOGUE)
                dve.wait_ge(s_later, 16 * LATER_CONSTS)
                nc.vector.tensor_scalar(region0[:], iota[:, 0:E], float(REGION), None, ALU.mult).then_inc(c_main, 1)
                dve.wait_ge(c_main, main.next())
                nc.vector.tensor_scalar(token[:].rearrange("p t o -> p (t o)"), iota[:, 0:TILES], float(P),
                                        float(DUMMY + TOKENS - S), ALU.mult, ALU.add).then_inc(c_main, 1)
                dve.wait_ge(c_main, main.next())
                nc.vector.tensor_scalar(token[:].rearrange("p t o -> p (t o)"),
                                        token[:].rearrange("p t o -> p (t o)"), lane, None, ALU.add).then_inc(c_main, 1)
                dve.wait_ge(c_main, main.next())
                body(0, False, True)
                with dve.Fori(1, B - 1) as b:
                    main.enter(b, 1, DVE_MAIN_STEPS)
                    late_t.enter(b, 1, DVE_LATE_STEPS)
                    body(b, True, True)
                main.leave(B - 2)
                late_t.leave(B - 2)
                body(B - 1, True, False)
                for kind, n in (("wo", 0), ("wo", 1), ("ot", 7)):
                    evac(kind, n, B - 1, EPILOGUE)
                for t in tiles_of(0):
                    norm(B - 1, t, 0)
                for kind, n in (("wo", 2), ("wo", 3), ("lg", 0), ("lg", 1)):
                    evac(kind, n, B - 1, EPILOGUE)
                experts_of(B - 1, 0, largest(B - 1, 0))
                for t in tiles_of(1):
                    norm(B - 1, t, 1)
                gates_of(B - 1, 0)
                evac("rk", 0, B - 1, EPILOGUE)
                loads_before(B - 1, tiles_of(0), 0)
                positions(B - 1, 0)
                send_off(B - 1, 0)
                for n in (2, 3):
                    evac("lg", n, B - 1, EPILOGUE)
                experts_of(B - 1, 1, largest(B - 1, 1))
                gates_of(B - 1, 1)
                evac("rk", 1, B - 1, EPILOGUE)
                loads_before(B - 1, tiles_of(1), 1)
                positions(B - 1, 1)
                send_off(B - 1, 1)
                tables()

            @block.gpsimd
            def _(pool):
                chain = Tally()

                def low_part(b, n):
                    c, is_k = (n % 4) // 2, n % 2
                    cs = slice(c * CHUNK, (c + 1) * CHUNK)
                    pool.wait_ge(s_hi, b * 16 + n + 1)
                    nc.gpsimd.tensor_tensor(home[:, 2 * is_k + 1, cs], full[:, is_k, :],
                                            home[:, 2 * is_k, cs].bitcast(F32), ALU.subtract).then_inc(s_lo, 1)

                def mask(b, u):
                    _, c, kt, _ = UNITS[u]
                    o = offset_in_chunk(c, kt)
                    pool.wait_ge(s_clip, b * NU + u + 1)
                    pool.nop(nofuse=True)
                    pp = p_sb[:, u % P_SLOTS, :, o:o + P]
                    nc.gpsimd.affine_select(out=pp, in_=pp, compare_op=ALU.is_ge, fill=0.0, base=0,
                                            pattern=[[0, 2], [1, P]], channel_multiplier=-1).then_inc(s_mask, 1)

                def rstd_of(b, h=None):
                    ts = span(h)
                    pool.wait_ge(s_stat, part(b, h, TILES))
                    pool.nop(nofuse=True)
                    nc.gpsimd.tensor_scalar(rstd[:, ts], mv[:, ts, 1:2], EPS, None, ALU.add).then_inc(c_pool, 1)
                    pool.wait_ge(c_pool, chain.next())
                    nc.gpsimd.tensor_tensor(rstd[:, ts], rstd[:, ts], expo[:, ts], ALU.pow).then_inc(s_rstd, 1)

                def scatter(b, n, h=None):
                    k, t = n % 2, n // 2
                    if t == tiles_of(h)[0] and k == 0:
                        pool.wait_ge(s_posr, part(b, h))
                        pool.wait_ge(s_x1, part(b, h, TILES))
                        pool.nop(nofuse=True)
                    nc.gpsimd.indirect_dma_start(
                        out=xs_d, out_offset=bass.IndirectOffsetOnAxis(ap=pos[:, k, t:t + 1], axis=0),
                        in_=z[:, t, :], in_offset=None).then_inc(s_scat, 16)

                def body(b, late, nxt):
                    jobs = EDGE_JOBS if isinstance(b, int) else LOOP_JOBS
                    turns = misc_turns(jobs)
                    for u in range(NU):
                        if u in jobs and jobs[u][0] == "proj":
                            n = jobs[u][1]
                            if u < 3 * PER_G:
                                low_part(b, (u // PER_G + 1) * 4 + n)
                            elif nxt:
                                low_part(b + 1, n)
                        if late and u == RSTD_AT:
                            rstd_of(b - 1)
                        if late and u in SCATTER_AT:
                            scatter(b - 1, SCATTER_AT.index(u))
                        if is_diag(u):
                            mask(b, u)

                nc.gpsimd.memset(p_sb[:, 0], 0.0).then_inc(s_zero, 1)
                nc.gpsimd.memset(wkr[:], 0.0).then_inc(s_zero, 1)
                nc.gpsimd.memset(v_aug[:], 1.0).then_inc(s_pool0, 1)
                nc.gpsimd.memset(expo[:], -0.5).then_inc(s_pool0, 1)
                nc.gpsimd.memset(load[:], 0.0).then_inc(s_pool0, 1)
                for n in range(4):
                    low_part(0, n)
                body(0, False, True)
                with pool.Fori(1, B - 1) as b:
                    chain.enter(b, 1, 1)
                    body(b, True, True)
                chain.leave(B - 2)
                body(B - 1, True, False)
                for h in range(2):
                    rstd_of(B - 1, h)
                for h in range(2):
                    for n in range(h * TILES, (h + 1) * TILES):
                        scatter(B - 1, n, h)

        psum_scope.close()
        attn_scope.close()

        s_xs = [sem(f"rows_loaded{i}") for i in range(2)]
        s_xsT_ps, s_xsT = sem("rows_t_in_psum"), sem("rows_t_ready")
        s_h_ps, s_h = sem("hidden_in_psum"), sem("hidden_ready")
        s_hT_ps, s_hT = sem("hidden_t_in_psum"), sem("hidden_t_ready")
        s_y_ps, s_y = sem("expert_out_in_psum"), sem("expert_out_ready")
        s_yst = [sem(f"expert_out_stored{i}") for i in range(2)]
        s_dest = sem("destinations_ready")
        c_dest = sem("destination_chain")
        s_res = sem("residuals_loaded")
        rows = sb("rows", [P, 2, TOPK, TILES, D])
        res = sb("res", [P, B, TILES, D])
        moe_scope = ExitStack()
        M = moe_scope
        xs = sb("xs", [P, 2, ROW], where=M)
        mine = sb("mine", [P, 2, 1], where=M)
        destf = sb("destf", [P, MOE_TILES], where=M)
        dest = sb("dest", [P, 2, 1], U32, where=M)
        dummy = sb("padding_rows", [P, 2, 1], where=M)
        xs_t = sb("xs_t", [P, 2, DT, P], where=M)
        h = sb("h", [P, 2, HID], where=M)
        h_t = sb("h_t", [P, 2, FT, P], where=M)
        y = sb("y", [P, 2, D], where=M)
        ps_x = [psum(f"ps_x{i}", [P, CHUNK], M) for i in range(2)]
        ps_h = [psum(f"ps_h{i}", [P, CHUNK], M) for i in range(2)]
        ps_t = [psum(f"ps_t{i}", [P, CHUNK], M) for i in range(2)]
        ps_y = [psum(f"ps_y{i}", [P, CHUNK], M) for i in range(2)]
        LOOP_END = MOE_TILES - 2
        assert B * TILES < MOE_TILES // 2
        x1_tiles = x1_d.rearrange("(n p) d -> n p d", p=P)

        with nc.Block() as block:
            @block.sync
            def _(sp):
                def load_rows(n, slot, first=False):
                    row = sp.value_load(table[0:1, READ, bass.ds(n, 1)], min_val=0, max_val=SPARE)
                    if not first:
                        sp.wait_ge(s_xsT_ps, n - 1)
                        sp.wait_ge(c_dest, 2 * n - 2)
                    sp.nop(nofuse=True)
                    sp.dma_start(xs[:, slot, :], xs_d[bass.ds(row, P), :]).then_inc(s_xs[slot], 16)

                load_rows(0, 0, True)
                load_rows(1, 1, True)
                with sp.Fori(1, B * TILES + 1) as pair:
                    load_rows(2 * pair, 0)
                    load_rows(2 * pair + 1, 1)
                    sp.dma_start(res[:].rearrange("p b t d -> p (b t) d")[:, bass.ds(pair - 1, 1), :],
                                 x1_tiles[bass.ds(pair - 1, 1)].rearrange("n p d -> p n d")).then_inc(s_res, 16)
                with sp.Fori(B * TILES + 1, MOE_TILES // 2) as pair:
                    load_rows(2 * pair, 0)
                    load_rows(2 * pair + 1, 1)

            @block.tensor
            def _(pe):
                def rows_t(n, slot, first=False):
                    pe.wait_ge(s_xs[slot], 16 * (n // 2 + 1) if isinstance(n, int) else (n - slot) * 8 + 16)
                    if not first:
                        pe.wait_ge(s_xsT, n - 1)
                    for dt in range(DT):
                        mm = nc.tensor.transpose(ps_x[slot][:, dt * P:(dt + 1) * P],
                                                 xs[:, slot, dt * P:(dt + 1) * P], ident[:])
                    mm.then_inc(s_xsT_ps, 1)

                def up(n, slot, first=False):
                    e = pe.value_load(table[0:1, EXPERT, bass.ds(n, 1)], min_val=0, max_val=E - 1)
                    pe.wait_ge(s_xsT, n + 1)
                    if not first:
                        pe.wait_ge(s_h, n - 1)
                    for dt in range(DT):
                        mm = nc.tensor.matmul(ps_h[slot][:, :], xs_t[:, slot, dt, :], w1_sb[:, e, dt, :],
                                              start=dt == 0, stop=dt == DT - 1)
                    mm.then_inc(s_h_ps, 1)

                def hidden_t(n, slot, first=False):
                    pe.wait_ge(s_h, n + 1)
                    if not first:
                        pe.wait_ge(s_hT, n - 1)
                    for f in range(FT):
                        mm = nc.tensor.transpose(ps_t[slot][:, f * P:(f + 1) * P],
                                                 h[:, slot, f * P:(f + 1) * P], ident[:])
                    mm.then_inc(s_hT_ps, 1)

                def down(n, slot, first=False):
                    e = pe.value_load(table[0:1, EXPERT, bass.ds(n, 1)], min_val=0, max_val=E - 1)
                    pe.wait_ge(s_hT, n + 1)
                    if not first:
                        pe.wait_ge(s_y, n - 1)
                    for f in range(FT):
                        mm = nc.tensor.matmul(ps_y[slot][:, 0:D], h_t[:, slot, f, :], w2_sb[:, e, f, :],
                                              start=f == 0, stop=f == FT - 1)
                    mm.then_inc(s_y_ps, 1)

                rows_t(0, 0, True)

                def turn(n, slot):
                    static = isinstance(n, int)
                    if not static or n < MOE_TILES:
                        up(n, slot, static and n < 2)
                    if not static or 1 <= n <= MOE_TILES:
                        hidden_t(n - 1, 1 - slot, static and n < 3)
                    if not static or n + 1 < MOE_TILES:
                        rows_t(n + 1, 1 - slot, static and n < 1)
                    if not static or n >= 2:
                        down(n - 2, slot, static and n < 4)

                for n in range(4):
                    turn(n, n % 2)
                with pe.Fori(2, LOOP_END // 2) as pair:
                    for k in range(2):
                        turn(2 * pair + k, k)
                for n in range(LOOP_END, MOE_TILES + 2):
                    turn(n, n % 2)

            @block.scalar
            def _(act):
                def rows_out(n, slot, first=False):
                    act.wait_ge(s_xsT_ps, n + 1)
                    if not first:
                        act.wait_ge(s_h_ps, n - 1)
                    nc.scalar.copy(xs_t[:, slot].rearrange("p t n -> p (t n)"), ps_x[slot][:, 0:D]).then_inc(s_xsT, 1)

                def relu_out(n, slot, first=False):
                    act.wait_ge(s_hT_ps, n + 1)
                    if not first:
                        act.wait_ge(s_y_ps, n - 1)
                    nc.scalar.activation(h_t[:, slot].rearrange("p t n -> p (t n)"), ps_t[slot][:, :],
                                         ACT.Relu).then_inc(s_hT, 1)

                rows_out(0, 0, True)
                rows_out(1, 1, True)
                relu_out(0, 0, True)
                rows_out(2, 0)
                relu_out(1, 1, True)
                rows_out(3, 1)
                with act.Fori(1, LOOP_END // 2) as pair:
                    for k in range(2):
                        n = 2 * pair
                        relu_out(n + k, k)
                        rows_out(n + k + 2, k)
                for n in range(MOE_TILES - 2, MOE_TILES):
                    relu_out(n, n % 2)

            @block.vector
            def _(dve):
                def hidden(n, slot, first=False):
                    e = dve.value_load(table[0:1, EXPERT, bass.ds(n, 1)], min_val=0, max_val=E - 1)
                    dve.wait_ge(s_h_ps, n + 1)
                    if not first:
                        dve.wait_ge(s_hT_ps, n - 1)
                    static = isinstance(n, int)
                    dve.wait_ge(s_xs[slot], 16 * (n // 2 + 1) if static else (n - slot) * 8 + 16)
                    nc.vector.tensor_tensor(mine[:, slot], xs[:, slot, D + 1:D + 2],
                                            tile_expert[:, bass.ds(n, 1)], ALU.is_equal).then_inc(c_dest, 1)
                    dve.wait_ge(c_dest, 2 * n + 1)
                    nc.vector.scalar_tensor_tensor(destf[:, bass.ds(n, 1)], mine[:, slot], float(-TOKENS),
                                                   xs[:, slot, D:D + 1], ALU.mult, ALU.add).then_inc(c_dest, 1)
                    nc.vector.tensor_tensor(h[:, slot, :], ps_h[slot][:, :], b1_sb[:, e, :], ALU.add).then_inc(s_h, 1)

                def expert_out(n, slot, first=False):
                    e = dve.value_load(table[0:1, EXPERT, bass.ds(n, 1)], min_val=0, max_val=E - 1)
                    dve.wait_ge(s_y_ps, n + 1)
                    if not first:
                        dve.wait_ge(s_yst[slot], (n - slot) * 8)
                    dve.wait_ge(c_dest, 2 * n + 2)
                    nc.vector.tensor_tensor(dest[:, slot], destf[:, bass.ds(n, 1)], dummy[:, slot],
                                            ALU.max).then_inc(s_dest, 1)
                    nc.vector.tensor_tensor(y[:, slot, :], ps_y[slot][:, 0:D], b2_sb[:, e, :], ALU.add).then_inc(s_y, 1)

                for slot in range(2):
                    nc.vector.tensor_scalar(dummy[:, slot], lane, float(slot * P), None, ALU.add)
                hidden(0, 0, True)
                hidden(1, 1, True)
                hidden(2, 0)
                expert_out(0, 0, True)
                hidden(3, 1)
                expert_out(1, 1, True)
                with dve.Fori(2, MOE_TILES // 2) as pair:
                    for k in range(2):
                        n = 2 * pair
                        hidden(n + k, k)
                        expert_out(n + k - 2, k)
                for n in range(MOE_TILES - 2, MOE_TILES):
                    expert_out(n, n % 2)

            @block.gpsimd
            def _(pool):
                def store_rows(n, slot):
                    pool.wait_ge(s_y, n + 1)
                    pool.wait_ge(s_dest, n + 1)
                    pool.nop(nofuse=True)
                    nc.gpsimd.indirect_dma_start(
                        out=ys_d, out_offset=bass.IndirectOffsetOnAxis(ap=dest[:, slot], axis=0),
                        in_=y[:, slot, :], in_offset=None).then_inc(s_yst[slot], 16)

                with pool.Fori(0, MOE_TILES // 2) as pair:
                    store_rows(2 * pair, 0)
                    store_rows(2 * pair + 1, 1)
                for slot in range(2):
                    pool.wait_ge(s_yst[slot], 8 * MOE_TILES)

        moe_scope.close()

        s_rows = [[sem(f"rows_loaded{i}{hf}") for hf in range(2)] for i in range(2)]
        s_gate = sem("batch_gates_ready")
        s_sum = sem("sums_ready")
        s_st = sem("final_stats_ready")
        s_rs = sem("final_rstd_ready")
        s_o = sem("out_ready")
        s_ost = sem("out_stored")
        c_fin, c_fp = sem("final_chain"), sem("final_pool_chain")
        F = ExitStack()
        gate_cur = sb("gate_cur", [P, 2, TOPK, TILES], where=F)
        fst = sb("fst", [P, 2, TILES, 6], where=F)
        fmv = sb("fmv", [P, 2, TILES, 2], where=F)
        frs = sb("frs", [P, 2, TILES, 1], where=F)
        shift = sb("shift", [P, 2, TILES, 1], where=F)
        fexpo = sb("fexpo", [P, TILES, 1], where=F)
        HALF = TILES // 2
        out_pairs = out.rearrange("(n i) (t p) d -> i n p t d", i=2, p=P)
        ys_batch = ys_d[DUMMY:DUMMY + TOPK * TOKENS, :].rearrange("(k b t p) d -> k b p t d", k=TOPK, b=B, p=P)

        FREE = 2 * TILES

        def batch_rows(b):
            return res[:].rearrange("p b t d -> p (b t) d")[:, bass.ds(b * TILES, TILES), :]

        def half(hf):
            return slice(hf * HALF, (hf + 1) * HALF)

        with nc.Block() as block:
            @block.sync
            def _(sp):
                def load(b):
                    i = b % 2
                    for hf in range(2):
                        if b >= 2:
                            sp.wait_ge(s_sum, (b - 2) * TILES + (hf + 1) * HALF)
                        for k in range(TOPK):
                            sp.dma_start(rows[:, i, k, half(hf), :], ys_batch[k, b, :, half(hf), :]
                                         ).then_inc(s_rows[i][hf], 16)
                for b in range(B):
                    load(b)
                sp.wait_ge(s_ost, 2 * B * 16)

            @block.scalar
            def _(act):
                with act.Fori(0, B // 2) as pair:
                    for i in range(2):
                        b = 2 * pair + i
                        for hf in range(2):
                            act.wait_ge(s_rs, b * 2 + hf + 1)
                            for t in range(hf * HALF, (hf + 1) * HALF):
                                nc.scalar.activation(batch_rows(b)[:, t, :], batch_rows(b)[:, t, :], ACT.Identity,
                                                     bias=shift[:, i, t, :], scale=frs[:, i, t, :]).then_inc(s_o, 1)
                            act.wait_ge(s_o, FREE + b * TILES + (hf + 1) * HALF)
                            act.nop(nofuse=True)
                            act.dma_start(out_pairs[i, pair, :, half(hf), :], batch_rows(b)[:, half(hf), :]
                                          ).then_inc(s_ost, 16)

            @block.gpsimd
            def _(pool):
                nc.gpsimd.memset(fexpo[:], -0.5).then_inc(s_o, FREE)
                pool.wait_ge(s_o, FREE)
                chain = Tally()
                with pool.Fori(0, B // 2) as pair:
                    chain.enter(pair, 0, 12)
                    for i in range(2):
                        for hf in range(2):
                            ts = half(hf)
                            pool.wait_ge(s_st, (2 * pair + i) * TILES + (hf + 1) * HALF)
                            pool.nop(nofuse=True)
                            nc.gpsimd.tensor_scalar(frs[:, i, ts], fmv[:, i, ts, 1:2], EPS, None, ALU.add
                                                    ).then_inc(c_fp, 1)
                            nc.gpsimd.tensor_scalar(shift[:, i, ts], fmv[:, i, ts, 0:1], -1.0, None, ALU.mult
                                                    ).then_inc(c_fp, 1)
                            chain.next()
                            pool.wait_ge(c_fp, chain.next())
                            pool.nop(nofuse=True)
                            nc.gpsimd.tensor_tensor(frs[:, i, ts], frs[:, i, ts], fexpo[:, ts], ALU.pow
                                                    ).then_inc(c_fp, 1)
                            pool.wait_ge(c_fp, chain.next())
                            pool.nop(nofuse=True)
                            nc.gpsimd.tensor_tensor(shift[:, i, ts], shift[:, i, ts], frs[:, i, ts], ALU.mult
                                                    ).then_inc(s_rs, 1)
                chain.leave(B // 2)

            @block.vector
            def _(dve):
                steps = Tally()
                dve.wait_ge(s_res, 16 * B * TILES)

                def sum_half(b, i, hf):
                    tiles = range(hf * HALF, (hf + 1) * HALF)
                    dve.wait_ge(s_rows[i][hf], (b - i) * 16 + 32)
                    for k, signal in enumerate((c_fin, s_sum)):
                        for t in tiles:
                            nc.vector.scalar_tensor_tensor(
                                batch_rows(b)[:, t, :], rows[:, i, k, t, :], gate_cur[:, i, k, t:t + 1],
                                batch_rows(b)[:, t, :],
                                ALU.mult, ALU.add).then_inc(signal, 1)
                            if k == 0:
                                v = steps.next()
                        if k == 0:
                            dve.wait_ge(c_fin, v)
                    dve.wait_ge(s_sum, b * TILES + (hf + 1) * HALF)
                    dve.nop(nofuse=True)
                    for t in tiles:
                        nc.vector.bn_stats(fst[:, i, t, :], batch_rows(b)[:, t, :]).then_inc(c_fin, 1)
                        v = steps.next()
                    dve.wait_ge(c_fin, v)
                    dve.nop(nofuse=True)
                    for t in tiles:
                        nc.vector.bn_aggr(fmv[:, i, t, :], fst[:, i, t, :]).then_inc(s_st, 1)

                with dve.Fori(0, B // 2) as pair:
                    steps.enter(pair, 0, 4 * TILES)
                    for i in range(2):
                        b = 2 * pair + i
                        nc.vector.tensor_copy(gate_cur[:, i].rearrange("p k t -> p (k t)"),
                                              gate_all[:, b].rearrange("p k t -> p (k t)")).then_inc(s_gate, 1)
                        dve.wait_ge(s_gate, b + 1)
                        dve.wait_ge(s_o, FREE + (b - 1) * TILES)
                        sum_half(b, i, 0)
                        sum_half(b, i, 1)
                steps.leave(B // 2)

        F.close()


def constants():
    ident = np.eye(P, dtype=np.float32)
    sel = np.zeros((P, 4, P), np.float32)
    for d in range(DR):
        for j in range(4):
            for half in range(2):
                for q in range(4):
                    to = QUAD * j + DH + DR * half + d
                    sel[QUAD * q + DH + d, q, to] = sel[QUAD * q + DH + DR + d, q, to] = 1.0
    inv = np.float32(10000.0) ** (-np.arange(0, DR, 2, dtype=np.float32) / np.float32(DR))
    ang = np.arange(S, dtype=np.float32)[:, None] * inv.astype(np.float32)
    cos, sin = np.cos(ang).T, np.sin(ang).T
    rope = np.ones((P, S), np.float32)
    for j in range(4):
        for d in range(DR):
            rope[QUAD * j + DH + d] = cos[d // 2]
            rope[QUAD * j + DH + DR + d] = sin[d // 2] if d % 2 else -sin[d // 2]
    rope_q = np.concatenate([rope[0:QUAD, j * QUARTER:(j + 1) * QUARTER] for j in range(4)])
    tri = np.stack([np.triu(np.ones((P, P), np.float32), 1), np.ones((P, P), np.float32)])
    iota = np.zeros((P, MOE_TILES + 1), np.float32)
    iota[:, 0:MOE_TILES] = np.arange(MOE_TILES)
    iota[:, MOE_TILES] = np.arange(P)
    return {"ident": ident, "sel": sel, "rope": rope, "rope_q": rope_q, "tri": tri, "iota": iota}


_INS = ["L0_attn_x", "L0_attn_W_DQ", "L0_attn_W_UQ", "L0_attn_W_QR", "L0_attn_W_DKV", "L0_attn_W_UK",
        "L0_attn_W_UV", "L0_attn_W_KR", "L0_attn_W_O", "L0_ffn_Wg", "L0_ffn_W1", "L0_ffn_b1",
        "L0_ffn_W2", "L0_ffn_b2"]


def kernel(**inputs):
    import concourse.bacc as _bacc
    from concourse.bass_utils import run_bass_kernel_spmd as _run

    nc = _bacc.Bacc("TRN2", target_bir_lowering=False, num_devices=1)
    arrays, args = {}, []
    given = {name: np.ascontiguousarray(inputs[name]) for name in _INS} | constants()
    for name, a in given.items():
        arrays[f"in_{name}_dram"] = a
        args.append(nc.dram_tensor(f"in_{name}_dram", a.shape, mybir.dt.from_np(a.dtype), kind="ExternalInput").ap())
    out = nc.dram_tensor("out_0_dram", (B, S, D), F32, kind="ExternalOutput").ap()
    layer(nc, *args, out)
    r = _run(nc, [arrays], core_ids=[0])
    return r.results[0]["out_0_dram"]
```
